# Optimizing a Trainium2 kernel written in Bass

```python
import numpy as np
import jax
import jax.numpy as jnp

def _softmax(x, axis=-1):
    return jax.nn.softmax(x, axis=axis)

def _gelu(x):
    return jax.nn.gelu(x, approximate=True)

def _silu(x):
    return jax.nn.silu(x)

def _sigmoid(x):
    return jax.nn.sigmoid(x)

def _layernorm(x, axis=-1, eps=1e-05):
    m = jnp.mean(x, axis=axis, keepdims=True)
    v = jnp.var(x, axis=axis, keepdims=True)
    return (x - m) / jnp.sqrt(v + eps)

def _scatter_add(tgt, idx, src, axis=0):
    return tgt.at[idx].add(src)

def _segment_sum(src, seg, n):
    return jax.ops.segment_sum(src, seg, n)
kernel_name = 'mk_vit_tower_cls_d1_tok_img768_r4_0d3323'

def setup_inputs(seed: int=0):
    np.random.seed(seed)
    _w = jnp.asarray

    def _rec_inputs():
        import jax
        import jax.numpy as jnp
        _rk = jax.random.key(seed)
        x = -0.00016672 + 0.999947 * jax.random.normal(jax.random.fold_in(_rk, 1), (16, 128, 128, 3), jnp.float32)
        cls_tok = 0.02 * jax.random.normal(jax.random.fold_in(_rk, 5), (1, 1, 192), jnp.float32)
        return (x, cls_tok)
    x, cls_tok = _rec_inputs()

    def _L0_tok_setup():
        import jax, jax.numpy as jnp
        import numpy as np
        PATCH = 16
        D_MODEL = 192

        def _patchify(imgs, p):
            B, H, Wd, C = imgs.shape
            nh, nw = (H // p, Wd // p)
            x = imgs.reshape(B, nh, p, nw, p, C)
            x = x.transpose(0, 1, 3, 2, 4, 5)
            return x.reshape(B, nh * nw, p * p * C)
        key = jax.random.key(seed)
        k1, k2 = jax.random.split(key)
        B, H, W_, C = (64, 96, 96, 3)
        imgs = jax.random.normal(k1, (B, H, W_, C), dtype=jnp.float32)
        patch_dim = PATCH * PATCH * C
        W = jax.random.normal(k2, (patch_dim, D_MODEL), dtype=jnp.float32) * (1.0 / np.sqrt(patch_dim))
        b = jnp.zeros((D_MODEL,), dtype=jnp.float32)
        return {'imgs': imgs, 'W': W, 'b': b}
    _L0_tok_all = _L0_tok_setup()
    _L0_tok_in = {k: v for k, v in _L0_tok_all.items() if k in ('W', 'b')}
    del _L0_tok_all

    def _L0_attn_setup():
        import jax, jax.numpy as jnp
        import numpy as np
        B, N, D = (4, 2048, 192)
        H, DH = (12, 64)
        INNER = H * DH
        key = jax.random.key(seed)
        k0, k1, k2 = jax.random.split(key, 3)
        return {'x': jax.random.normal(k0, (B, N, D), dtype=jnp.float32), 'w_qkv': jax.random.normal(k1, (D, INNER), dtype=jnp.float32) * 0.02, 'temp': jnp.ones((H, 1), dtype=jnp.float32), 'w_out': jax.random.normal(k2, (INNER, D), dtype=jnp.float32) * 0.02, 'b_out': jnp.zeros((D,), dtype=jnp.float32)}
    _L0_attn_all = _L0_attn_setup()
    _L0_attn_in = {k: v for k, v in _L0_attn_all.items() if k in ('w_qkv', 'temp', 'w_out', 'b_out')}
    del _L0_attn_all

    def _L0_ffn_setup():
        import jax, jax.numpy as jnp
        import numpy as np

        def _layernorm(x, gamma, beta, eps=1e-05):
            mu = jnp.mean(x, axis=-1, keepdims=True)
            var = jnp.mean(jnp.square(x - mu), axis=-1, keepdims=True)
            return (x - mu) * jax.lax.rsqrt(var + eps) * gamma + beta

        def _sparse_ternary_linear(x, W, b, sparsity):
            absW = jnp.abs(W)
            scale = jnp.mean(absW)
            thresh = jnp.quantile(absW, sparsity)
            q = jnp.sign(W) * (absW > thresh).astype(W.dtype)
            return jnp.einsum('bnd,hd->bnh', x, q * scale) + b
        key = jax.random.key(seed)
        ks = jax.random.split(key, 8)
        B, N, D, H = (32, 256, 192, 768)
        return {'x': jax.random.normal(ks[0], (B, N, D), dtype=jnp.float32), 'ln1_g': jnp.ones((D,), jnp.float32), 'ln1_b': jnp.zeros((D,), jnp.float32), 'W1': jax.random.normal(ks[1], (H, D), dtype=jnp.float32) * 0.02, 'b1': jnp.zeros((H,), jnp.float32), 'ln2_g': jnp.ones((H,), jnp.float32), 'ln2_b': jnp.zeros((H,), jnp.float32), 'W2': jax.random.normal(ks[2], (D, H), dtype=jnp.float32) * 0.02, 'b2': jnp.zeros((D,), jnp.float32), 'sparsity': jnp.float32(0.5)}
    _L0_ffn_all = _L0_ffn_setup()
    _L0_ffn_in = {k: v for k, v in _L0_ffn_all.items() if k in ('ln1_g', 'ln1_b', 'W1', 'b1', 'ln2_g', 'ln2_b', 'W2', 'b2', 'sparsity')}
    del _L0_ffn_all
    return {'x': x, 'cls_tok': cls_tok, 'L0_tok_W': _L0_tok_in['W'], 'L0_tok_b': _L0_tok_in['b'], 'L0_attn_w_qkv': _L0_attn_in['w_qkv'], 'L0_attn_temp': _L0_attn_in['temp'], 'L0_attn_w_out': _L0_attn_in['w_out'], 'L0_attn_b_out': _L0_attn_in['b_out'], 'L0_ffn_ln1_g': _L0_ffn_in['ln1_g'], 'L0_ffn_ln1_b': _L0_ffn_in['ln1_b'], 'L0_ffn_W1': _L0_ffn_in['W1'], 'L0_ffn_b1': _L0_ffn_in['b1'], 'L0_ffn_ln2_g': _L0_ffn_in['ln2_g'], 'L0_ffn_ln2_b': _L0_ffn_in['ln2_b'], 'L0_ffn_W2': _L0_ffn_in['W2'], 'L0_ffn_b2': _L0_ffn_in['b2'], 'L0_ffn_sparsity': _L0_ffn_in['sparsity']}

def reference(x, cls_tok, L0_tok_W, L0_tok_b, L0_attn_w_qkv, L0_attn_temp, L0_attn_w_out, L0_attn_b_out, L0_ffn_ln1_g, L0_ffn_ln1_b, L0_ffn_W1, L0_ffn_b1, L0_ffn_ln2_g, L0_ffn_ln2_b, L0_ffn_W2, L0_ffn_b2, L0_ffn_sparsity):
    import jax
    import jax.numpy as jnp

    def _L0_tok_ref(imgs, W, b):
        import jax, jax.numpy as jnp
        import numpy as np
        PATCH = 16
        D_MODEL = 192

        def _patchify(imgs, p):
            B, H, Wd, C = imgs.shape
            nh, nw = (H // p, Wd // p)
            x = imgs.reshape(B, nh, p, nw, p, C)
            x = x.transpose(0, 1, 3, 2, 4, 5)
            return x.reshape(B, nh * nw, p * p * C)
        x = _patchify(imgs, PATCH)
        return jnp.einsum('bnd,de->bne', x, W) + b

    def _L0_attn_ref(x, w_qkv, temp, w_out, b_out):
        import jax, jax.numpy as jnp
        import numpy as np
        B, N, D = (4, 2048, 192)
        H, DH = (12, 64)
        INNER = H * DH
        b, n, _ = x.shape
        h = temp.shape[0]
        w = (x @ w_qkv).reshape(b, n, h, -1).transpose(0, 2, 1, 3)
        norm = jnp.sqrt(jnp.sum(w * w, axis=2, keepdims=True))
        w_normed = w / jnp.maximum(norm, 1e-12)
        logits = jnp.sum(w_normed * w_normed, axis=-1) * temp
        Pi = jax.nn.softmax(logits, axis=-1)
        Pi_norm = Pi / (jnp.sum(Pi, axis=-1, keepdims=True) + 1e-08)
        dots = jnp.einsum('bhn,bhnd->bhd', Pi_norm, w * w)[:, :, None, :]
        attn = 1.0 / (1.0 + dots)
        out = -(w * Pi[..., None]) * attn
        out = out.transpose(0, 2, 1, 3).reshape(b, n, -1)
        return out @ w_out + b_out

    def _L0_ffn_ref(x, ln1_g, ln1_b, W1, b1, ln2_g, ln2_b, W2, b2, sparsity):
        import jax, jax.numpy as jnp
        import numpy as np

        def _layernorm(x, gamma, beta, eps=1e-05):
            mu = jnp.mean(x, axis=-1, keepdims=True)
            var = jnp.mean(jnp.square(x - mu), axis=-1, keepdims=True)
            return (x - mu) * jax.lax.rsqrt(var + eps) * gamma + beta

        def _sparse_ternary_linear(x, W, b, sparsity):
            absW = jnp.abs(W)
            scale = jnp.mean(absW)
            thresh = jnp.quantile(absW, sparsity)
            q = jnp.sign(W) * (absW > thresh).astype(W.dtype)
            return jnp.einsum('bnd,hd->bnh', x, q * scale) + b
        h = _layernorm(x, ln1_g, ln1_b)
        h = _sparse_ternary_linear(h, W1, b1, sparsity)
        h = jax.nn.gelu(h)
        h = _layernorm(h, ln2_g, ln2_b)
        h = _sparse_ternary_linear(h, W2, b2, sparsity)
        return h
    h = _L0_tok_ref(x, L0_tok_W, L0_tok_b)
    h = jnp.concatenate([jnp.broadcast_to(cls_tok, (h.shape[0], 1, h.shape[2])), h], axis=1)
    h = h + _L0_attn_ref(_layernorm(h, axis=-1), L0_attn_w_qkv, L0_attn_temp, L0_attn_w_out, L0_attn_b_out)
    h = h + _L0_ffn_ref(_layernorm(h, axis=-1), L0_ffn_ln1_g, L0_ffn_ln1_b, L0_ffn_W1, L0_ffn_b1, L0_ffn_ln2_g, L0_ffn_ln2_b, L0_ffn_W2, L0_ffn_b2, L0_ffn_sparsity)
    return h

_drawn_inputs = setup_inputs


def setup_inputs(seed=0):
    import zlib

    import numpy as np

    out = dict(_drawn_inputs(seed))
    spreads = {'L0_tok_b': (0.0, 0.1),
     'L0_attn_temp': (1.0, 0.6),
     'L0_attn_b_out': (0.0, 0.1),
     'L0_ffn_ln1_g': (1.0, 0.2),
     'L0_ffn_ln1_b': (0.0, 0.296),
     'L0_ffn_b1': (0.0, 0.1),
     'L0_ffn_ln2_g': (1.0, 0.2),
     'L0_ffn_ln2_b': (0.0, 0.279),
     'L0_ffn_b2': (0.0, 0.1)}
    factors = {'cls_tok': 7.082, 'L0_attn_w_qkv': 8.0, 'L0_attn_w_out': 8.0}
    for name, (base, spread) in spreads.items():
        noise = np.random.default_rng([zlib.crc32(name.encode()), seed]).standard_normal(out[name].shape)
        drawn = base * np.exp(spread * noise) if base else spread * noise
        out[name] = jnp.asarray(drawn.astype(out[name].dtype))
    for name, factor in factors.items():
        out[name] = (out[name] * factor).astype(out[name].dtype)
    return out
```

```python
from contextlib import ExitStack

import numpy as np

import concourse.bass as bass
from concourse import mybir
from concourse.alu_op_type import AluOpType as ALU

ACT = mybir.ActivationFunctionType
AX = mybir.AxisListType
F32 = mybir.dt.float32
BF16 = mybir.dt.bfloat16
I32 = mybir.dt.int32
U16 = mybir.dt.uint16

P = 128
BATCH = 16
PATCHES = 64
SEQ = PATCHES + 1
D = 192
HALF = D // 2
HID = 768
C = HID // P
HEADS = 12
IPT = P // PATCHES
TILES = BATCH // IPT
EPS = 1e-5
N_W = HID * D
WCOLS = N_W // P
HI_ROUNDS = 15
LO_ROUNDS = 16
ROUNDS = HI_ROUNDS + LO_ROUNDS
BIG = 3.0e38
ROUND_MAGIC = 1.5 * 2.0 ** 23
MCH = WCOLS // P

HI_PLAN = [2] * 7 + [1]
LO_PLAN = [2] * 8


def vit_block(nc, x_t, cls_tok, tok_w, tok_b, w_qkv, temp, w_out, b_out, ln1_g, ln1_b, w1_flat, w1_t, b1,
              ln2_g, ln2_b, w2_t, b2, sparsity, head_cols, head_rows, ident_c, out):
    ctx = ExitStack()
    with ctx:
        def sb(name, shape, dt=F32):
            return ctx.enter_context(nc.sbuf_tensor(name, shape, dt))

        def pb(name, shape, dt=F32):
            return ctx.enter_context(nc.psum_tensor(name, shape, dt))

        def sem(name):
            return ctx.enter_context(nc.semaphore(name))

        x_sb = sb("x_sb", [P, TILES, C, P])
        tokw_sb = sb("tokw_sb", [P, C, D])
        tokb_sb = sb("tokb_sb", [P, D])
        wqkv_sb = sb("wqkv_sb", [HALF, 2, HID])
        wout_sb = sb("wout_sb", [P, C, D])
        bout_sb = sb("bout_sb", [P, D])
        b2_sb = sb("b2_sb", [P, D])
        temp_sb = sb("temp_sb", [HEADS, 1])
        ln1g_sb = sb("ln1g_sb", [HALF, 2])
        ln1b_sb = sb("ln1b_sb", [HALF, 2])
        ln2g_sb = sb("ln2g_sb", [P, C])
        ln2b_sb = sb("ln2b_sb", [P, C])
        hcols_sb = sb("hcols_sb", [P, C, HEADS])
        hrows_sb = sb("hrows_sb", [HEADS, C, P])
        ident = sb("ident", [P, P])
        ones = sb("ones", [P, P])
        ones_bf = sb("ones_bf", [P, 2], BF16)
        neg_half = sb("neg_half", [P, 1])

        h0 = sb("h0", [P, TILES, D])
        h0c = sb("h0c", [BATCH, D])
        hn = sb("hn", [P, 2, D])
        hT_all = sb("hT_all", [HALF, 2, TILES * P])
        hTc = sb("hTc", [HALF, 2, BATCH])
        st0 = sb("st0", [P, 2, 6])
        mv0 = sb("mv0", [P, 2, 2])
        rs0 = sb("rs0", [P, 2, 2])

        w_s = sb("w_s", [P, 2, 2, 6, SEQ])
        wsq = sb("wsq", [P, 2, 2, 6, SEQ])
        wcls = sb("wcls", [P, 2, 3])
        n2 = sb("n2", [P, 12])
        inv = sb("inv", [P, 2, 12])
        invm = sb("invm", [P, 12, HEADS])
        lg = sb("lg", [HEADS, 2, SEQ])
        nmx = sb("nmx", [HEADS, 2])
        ex = sb("ex", [HEADS, 2, SEQ])
        sm = sb("sm", [HEADS, 2])
        rsm = sb("rsm", [HEADS, 2])
        pi = sb("pi", [HEADS, 2, SEQ + 1])
        sp = sb("sp", [HEADS, 2, 2])
        wp = sb("wp", [P, 2, 2, 6, SEQ])
        wwp = sb("wwp", [P, 2, 6, SEQ])
        ds = sb("ds", [P, 12])
        att = sb("att", [P, 4, 12])
        oT = sb("oT", [P, 2, C, P])
        ocls = sb("ocls", [P, C, BATCH])

        h1 = sb("h1", [P, TILES, D])
        h1c = sb("h1c", [BATCH, D])
        yn = sb("yn", [P, 2, D])
        st1 = sb("st1", [P, 2, 6])
        mv1 = sb("mv1", [P, TILES + 1, 2])
        rs1 = sb("rs1", [P, TILES + 1, 2])
        yT = sb("yT", [HALF + 1, 2, 2, P])
        w1q = sb("w1q", [HALF + 1, 2, HID])
        w1t_sb = sb("w1t_sb", [HALF, 2, HID])
        w1neg = sb("w1neg", [HALF, 2, HID])
        w2q = sb("w2q", [P, C, D])
        w2neg = sb("w2neg", [P, C, D])
        w2g = sb("w2g", [P, C, D + 1])
        bet_b = sb("bet_b", [P, C, P])
        cg = sb("cg", [P, D])
        crow = sb("crow", [P, D])
        gl = sb("gl", [P, 2, C, P])
        glsq = sb("glsq", [P, 2, C, P])
        mom = sb("mom", [P, 2, 2])
        ms = sb("ms", [P, 2, 4])
        fin = sb("fin", [P, 2, D])

        w1f_sb = sb("w1f_sb", [P, WCOLS])
        w2f_sb = sb("w2f_sb", [P, C, D])
        w2f = w2f_sb[:, :, :].rearrange("p c n -> p (c n)")
        flat = [w1f_sb[:, :], w2f]
        absw = sb("absw", [P, 2, WCOLS])
        hi16 = sb("hi16", [P, 2, WCOLS], U16)
        lo16 = sb("lo16", [P, 2, WCOLS], U16)
        wide = sb("wide", [P, 2, WCOLS])
        cmask = sb("cmask", [P, 2, WCOLS], BF16)
        asum = sb("asum", [P, 2])
        part = sb("part", [P, 2])
        cand = sb("cand", [P, 2])
        turn = sb("turn", [P, 2])
        stepc = sb("stepc", [P, 1])
        q_sb = sb("q_sb", [P, 1])
        qs = sb("qs", [P, 12])
        hi_f = sb("hi_f", [P, 2])
        bits = sb("bits", [P, 4, 2], I32)
        sel = sb("sel", [P, 12, 2])
        w_scale = sb("w_scale", [P, 2])

        ps_w = pb("ps_w", [P, 2, 512])
        ps_b = pb("ps_b", [P, 2, 512])
        ps_l = pb("ps_l", [P, 512])
        ps_o = pb("ps_o", [P, 512])
        ps_t = pb("ps_t", [P, 512])
        ps_c = pb("ps_c", [P, 512])
        cnt_part = ps_c[:, 0:2]
        cnt_all = ps_c[:, 4:6]

        x_in = [sem(f"x_in{t}") for t in range(TILES)]
        tokw_in = sem("tokw_in")
        consts_in = sem("consts_in")
        row_in = sem("row_in")
        flat_in = [sem("w1_flat_in"), sem("w2_flat_in")]
        q_in = sem("q_in")
        attn_in = sem("attn_in")
        ffn_in = sem("ffn_in")
        memsets = sem("memsets")
        ones_set = sem("ones_set")
        tok_done = sem("tok_done")
        h0_ready = sem("h0_ready")
        st0_step = sem("st0_step")
        rs0_step = sem("rs0_step")
        hn_ready = sem("hn_ready")
        hn_turned = sem("hn_turned")
        hT_ready = sem("hT_ready")
        bias_in_h0 = sem("bias_in_h0")
        wcls_done = sem("wcls_done")
        wcls_copied = sem("wcls_copied")
        wcls_spread = sem("wcls_spread")
        w_done = sem("w_done")
        w_copied = sem("w_copied")
        wsq_ready = sem("wsq_ready")
        norm_step = sem("norm_step")
        invm_ready = sem("invm_ready")
        logits_done = sem("logits_done")
        soft_step = sem("soft_step")
        exp_done = sem("exp_done")
        pi_ready = sem("pi_ready")
        spread_done = sem("spread_done")
        wp_ready = sem("wp_ready")
        wwp_ready = sem("wwp_ready")
        att_step = sem("att_step")
        oT_ready = sem("oT_ready")
        ocls_ready = sem("ocls_ready")
        out_done = sem("out_done")
        h1_ready = sem("h1_ready")
        st1_step = sem("st1_step")
        rs1_step = sem("rs1_step")
        yn_ready = sem("yn_ready")
        yn_turned = sem("yn_turned")
        yT_ready = sem("yT_ready")
        crow_in_h1 = sem("crow_in_h1")
        hid_done = sem("hid_done")
        gl_ready = sem("gl_ready")
        glsq_ready = sem("glsq_ready")
        ffn_done = sem("ffn_done")
        mom_ready = sem("mom_ready")
        ms_step = sem("ms_step")
        fin_step = sem("fin_step")
        stored = [sem("stored_even"), sem("stored_odd")]
        abs_done = sem("abs_done")
        halves_ready = sem("halves_ready")
        q_step = sem("q_step")
        cand_ready = sem("cand_ready")
        mask_ready = sem("mask_ready")
        part_done = sem("part_done")
        part_copied = sem("part_copied")
        count_done = sem("count_done")
        turn_step = sem("turn_step")
        step_halved = sem("step_halved")
        low_step = sem("low_step")
        sel_step = sem("sel_step")
        sel_step2 = sem("sel_step2")
        next_ready = sem("next_ready")
        next_all = sem("next_all")
        asum_done = sem("asum_done")
        thresh_ready = sem("thresh_ready")
        tern_step = sem("tern_step")
        w2_sub = sem("w2_sub")
        w2g_ready = sem("w2g_ready")
        bet_ready = sem("bet_ready")
        rows_done = sem("rows_done")
        rows_ready = sem("rows_ready")

        N_CONSTS = 1
        N_ROW = 4
        N_ATTN = 4
        N_FFN = 7
        FFN_ORDER = [0, 1, TILES] + list(range(2, TILES))
        block = ctx.enter_context(nc.Block())

        hi_at, n = [], 0
        for k in HI_PLAN:
            hi_at.append(list(range(n, n + k)))
            n += k
        assert n == HI_ROUNDS
        lo_at = []
        for k in LO_PLAN:
            lo_at.append(list(range(n, n + k)))
            n += k
        assert n == ROUNDS

        def stores_before(i, j):
            return sum(1 if t == TILES else IPT for t in FFN_ORDER[i:j:2])

        @block.sync
        def _(sp):
            sp.dma_start(x_sb[:, 0], x_t[0]).then_inc(x_in[0], 16)
            sp.dma_start(tokw_sb[:], tok_w).then_inc(tokw_in, 16)
            for t in range(1, TILES):
                sp.dma_start(x_sb[:, t], x_t[t]).then_inc(x_in[t], 16)
            sp.dma_start(wout_sb[:], w_out).then_inc(attn_in, 16)
            sp.dma_start(w1t_sb[:], w1_t).then_inc(ffn_in, 16)
            sp.dma_start(w1q[HALF:HALF + 1, 1, :], b1).then_inc(ffn_in, 16)
            sp.dma_start(ln1g_sb[:], ln1_g).then_inc(ffn_in, 16)
            sp.dma_start(ln1b_sb[:], ln1_b).then_inc(ffn_in, 16)
            sp.dma_start(ln2g_sb[:], ln2_g).then_inc(ffn_in, 16)
            sp.dma_start(ln2b_sb[:], ln2_b).then_inc(ffn_in, 16)
            sp.dma_start(b2_sb[:], b2.partition_broadcast(P)).then_inc(ffn_in, 16)
            for j, t in enumerate(FFN_ORDER):
                sp.wait_ge(fin_step, 2 * (j + 1))
                if t == TILES:
                    sp.dma_start(out[:, 0, :], fin[0:BATCH, j % 2, :]).then_inc(stored[j % 2], 16)
                else:
                    for b in range(IPT):
                        sp.dma_start(out[IPT * t + b, 1:SEQ, :],
                                     fin[PATCHES * b:PATCHES * (b + 1), j % 2, :]).then_inc(stored[j % 2], 16)
            for i in range(2):
                sp.wait_ge(stored[i], 16 * stores_before(i, len(FFN_ORDER)))

        def turn_bank(t):
            return ps_t if t % 2 == 0 else ps_b[:, 0, :]

        @block.tensor
        def _(pe):
            def count(r):
                pe.wait_ge(mask_ready, 2 * (r + 1))
                for m in range(2):
                    for k in range(MCH):
                        last = nc.tensor.matmul(cnt_part[:, m:m + 1], cmask[:, m, k * P:(k + 1) * P],
                                                ones_bf[:, 0:1], start=(k == 0), stop=(k == MCH - 1))
                last.then_inc(part_done, 1)

            def total(r):
                pe.wait_ge(part_copied, r + 1)
                nc.tensor.matmul(cnt_all, ones[:], part[:], start=True, stop=True).then_inc(count_done, 1)

            def embed(t, ks):
                if ks[0] == 0:
                    if t == 0:
                        pe.wait_ge(tokw_in, 16)
                    if t >= 2:
                        pe.wait_ge(h0_ready, t - 1)
                    pe.wait_ge(x_in[t], 16)
                dst = (ps_l if t % 2 == 0 else ps_o)[:, 0:D]
                for k in ks:
                    last = nc.tensor.matmul(dst, x_sb[:, t, k, :], tokw_sb[:, k, :],
                                            start=(k == 0), stop=(k == C - 1))
                if ks[-1] == C - 1:
                    last.then_inc(tok_done, 1)

            def turn_hn(t):
                pe.wait_ge(hn_ready, t + 1)
                if t >= 2:
                    pe.wait_ge(hT_ready, t - 1)
                for k in range(2):
                    last = nc.tensor.transpose(turn_bank(t)[0:HALF, k * P:(k + 1) * P],
                                               hn[:, t % 2, k * HALF:(k + 1) * HALF], ident[:])
                last.then_inc(hn_turned, 1)

            pe.wait_ge(ones_set, 2)
            pe.wait_ge(consts_in, 16 * N_CONSTS)
            embed(0, range(C))
            for t in range(TILES):
                parts = [range(0, 3), range(3, C)] if t + 1 < TILES else [None, None]
                rr = hi_at[t]
                for i in range(max(2, len(rr))):
                    if i < len(rr):
                        count(rr[i])
                    if i < 2 and parts[i] is not None:
                        embed(t + 1, parts[i])
                    if i < len(rr):
                        total(rr[i])
                turn_hn(t)
            pe.wait_ge(hn_ready, TILES + 1)
            pe.wait_ge(hT_ready, TILES - 1)
            for k in range(2):
                last = nc.tensor.transpose(ps_t[0:HALF, k * P:k * P + BATCH],
                                           hn[0:BATCH, 0, k * HALF:(k + 1) * HALF], ident[0:BATCH, 0:BATCH])
            last.then_inc(hn_turned, 1)

            def project(t):
                pe.wait_ge(hT_ready, t + 1)
                if t >= 1:
                    pe.wait_ge(w_copied, t)
                    pe.wait_ge(wsq_ready, t)
                for c in range(C):
                    for k in range(2):
                        last = nc.tensor.matmul(ps_w[:, c // 3, (c % 3) * P:(c % 3 + 1) * P],
                                                wqkv_sb[:, k, c * P:(c + 1) * P], hT_all[:, k, t * P:(t + 1) * P],
                                                start=(k == 0), stop=(k == 1))
                last.then_inc(w_done, 1)

            def logits(t):
                pe.wait_ge(invm_ready, t + 1)
                if t >= 1:
                    pe.wait_ge(soft_step, 6 * (t - 1) + 1)
                pe.wait_ge(wsq_ready, t + 1)
                for b in range(IPT):
                    for c in range(C):
                        j = 2 * (c % 3) + b
                        last = nc.tensor.matmul(ps_l[0:HEADS, b * SEQ:(b + 1) * SEQ],
                                                invm[:, (c // 3) * 6 + j, :], wsq[:, t % 2, c // 3, j, :],
                                                start=(c == 0), stop=(c == C - 1))
                last.then_inc(logits_done, 1)

            def spread(t):
                pe.wait_ge(pi_ready, t + 1)
                if t >= 1:
                    pe.wait_ge(att_step, 4 * (t - 1) + 2)
                for c in range(C):
                    last = nc.tensor.matmul(ps_b[:, c // 3, (c % 3) * 2 * (SEQ + 1):(c % 3 + 1) * 2 * (SEQ + 1)],
                                            hrows_sb[:, c, :], pi[:, :, :].rearrange("h b n -> h (b n)"),
                                            start=True, stop=True)
                last.then_inc(spread_done, 1)

            def combine(t):
                pe.wait_ge(oT_ready, t + 1)
                if t >= 1:
                    pe.wait_ge(h1_ready, t)
                for c in range(C):
                    last = nc.tensor.matmul(ps_o[:, 0:D], oT[:, t % 2, c, :], wout_sb[:, c, :],
                                            start=(c == 0), stop=(c == C - 1))
                last.then_inc(out_done, 1)

            pe.wait_ge(attn_in, 16 * N_ATTN)
            pe.wait_ge(hT_ready, TILES + 1)
            for c in range(C):
                for k in range(2):
                    last = nc.tensor.matmul(ps_t[:, 256 + c:257 + c], wqkv_sb[:, k, c * P:(c + 1) * P],
                                            hTc[:, k, 0:1], start=(k == 0), stop=(k == 1))
            last.then_inc(wcls_done, 1)
            for s in range(-1, TILES + 1):
                rr = lo_at[s + 1] if s + 1 < len(lo_at) else []
                if s + 1 < TILES:
                    project(s + 1)
                for i, r in enumerate(rr):
                    if i == 0:
                        count(r)
                        if 0 <= s < TILES:
                            spread(s)
                        total(r)
                    elif i == 1:
                        count(r)
                        if 1 <= s:
                            combine(s - 1)
                        total(r)
                    else:
                        count(r)
                        total(r)
                if len(rr) < 1 and 0 <= s < TILES:
                    spread(s)
                if len(rr) < 2 and 1 <= s:
                    combine(s - 1)
                if s + 1 < TILES:
                    logits(s + 1)
            pe.wait_ge(ocls_ready, TILES)
            pe.wait_ge(h1_ready, TILES)
            for c in range(C):
                last = nc.tensor.matmul(ps_o[0:BATCH, 0:D], ocls[:, c, :], wout_sb[:, c, :],
                                        start=(c == 0), stop=(c == C - 1))
            last.then_inc(out_done, 1)

            count(ROUNDS)
            total(ROUNDS)
            pe.wait_ge(abs_done, 2)
            pe.wait_ge(sel_step, 1)
            nc.tensor.matmul(cnt_all, ones[:], asum[:], start=True, stop=True).then_inc(asum_done, 1)

            def rows():
                pe.wait_ge(w2_sub, 1)
                pe.wait_ge(bet_ready, 1)
                for c in range(C):
                    nc.tensor.matmul(ps_t[:, 0:D], bet_b[:, c, :], w2q[:, c, :], start=(c == 0), stop=(c == C - 1))
                pe.wait_ge(w2g_ready, C)
                for c in range(C):
                    last = nc.tensor.matmul(ps_t[:, D:2 * D], ones[:], w2g[:, c, 0:D],
                                            start=(c == 0), stop=(c == C - 1))
                last.then_inc(rows_done, 1)

            def turn_yn(j):
                n = BATCH if FFN_ORDER[j] == TILES else P
                pe.wait_ge(yn_ready, j + 1)
                if j >= 2:
                    pe.wait_ge(yT_ready, 2 * (j - 1))
                dst = ps_c if j % 2 == 0 else ps_l
                for k in range(2):
                    last = nc.tensor.transpose(dst[0:HALF, 128 + k * P:128 + k * P + n],
                                               yn[0:n, j % 2, k * HALF:(k + 1) * HALF], ident[0:n, 0:n])
                last.then_inc(yn_turned, 1)

            def hidden(j):
                n = BATCH if FFN_ORDER[j] == TILES else P
                pe.wait_ge(yT_ready, 2 * (j + 1))
                if j >= 2:
                    pe.wait_ge(gl_ready, j - 1)
                dst = ps_w if j % 2 == 0 else ps_b
                for c in range(C):
                    for k in range(2):
                        rows_k = HALF + k
                        last = nc.tensor.matmul(dst[:, c // 3, (c % 3) * P:(c % 3) * P + n],
                                                w1q[0:rows_k, k, c * P:(c + 1) * P], yT[0:rows_k, j % 2, k, 0:n],
                                                start=(k == 0), stop=(k == 1))
                last.then_inc(hid_done, 1)

            def contract(j):
                n = BATCH if FFN_ORDER[j] == TILES else P
                pe.wait_ge(glsq_ready, j + 1)
                if j >= 2:
                    pe.wait_ge(fin_step, 2 * (j - 1))
                if j == 0:
                    pe.wait_ge(rows_ready, 2)
                dst = ps_o if j % 2 == 0 else ps_t
                for c in range(C):
                    nc.tensor.matmul(dst[0:n, D + 1:D + 2], glsq[:, j % 2, c, 0:n], ones[:, 0:1],
                                     start=(c == 0), stop=(c == C - 1))
                for c in range(C):
                    last = nc.tensor.matmul(dst[0:n, 0:D + 1], gl[:, j % 2, c, 0:n], w2g[:, c, :],
                                            start=(c == 0), stop=(c == C - 1))
                last.then_inc(ffn_done, 1)

            NB = len(FFN_ORDER)
            turn_yn(0)
            pe.wait_ge(tern_step, 3)
            hidden(0)
            rows()
            for j in range(NB):
                if j + 1 < NB:
                    turn_yn(j + 1)
                    hidden(j + 1)
                contract(j)

        @block.scalar
        def _(act):
            act.dma_start(flat[0], w1_flat).then_inc(flat_in[0], 16)
            act.dma_start(w2f_sb[:], w2_t).then_inc(flat_in[1], 16)
            act.dma_start(q_sb[:], sparsity.partition_broadcast(P)).then_inc(q_in, 16)
            act.dma_start(tokb_sb[:], tok_b.partition_broadcast(P)).then_inc(row_in, 16)
            act.dma_start(ident[:], ident_c).then_inc(consts_in, 16)
            act.dma_start(bout_sb[:], b_out.partition_broadcast(P)).then_inc(row_in, 16)
            act.dma_start(h0c[:], cls_tok.partition_broadcast(BATCH)).then_inc(row_in, 16)
            act.dma_start(temp_sb[:], temp).then_inc(row_in, 16)
            act.dma_start(wqkv_sb[:], w_qkv).then_inc(attn_in, 16)
            act.dma_start(hcols_sb[:], head_cols).then_inc(attn_in, 16)
            act.dma_start(hrows_sb[:], head_rows).then_inc(attn_in, 16)

            def copy_part(r):
                act.wait_ge(part_done, r + 1)
                nc.scalar.copy(part[:], cnt_part).then_inc(part_copied, 1)

            def copy_hT(t):
                act.wait_ge(hn_turned, t + 1)
                nc.scalar.copy(hT_all[:, :, t * P:(t + 1) * P],
                               turn_bank(t)[0:HALF, 0:2 * P]
                               .rearrange("p (k n) -> p k n", k=2)).then_inc(hT_ready, 1)

            for m in range(2):
                act.wait_ge(flat_in[m], 16)
                nc.scalar.activation(absw[:, m, :], flat[m], ACT.Abs, accum_out=asum[:, m:m + 1]).then_inc(abs_done, 1)
            for t in range(TILES):
                for r in hi_at[t]:
                    copy_part(r)
                copy_hT(t)
            act.wait_ge(hn_turned, TILES + 1)
            nc.scalar.copy(hTc[:, :, :], ps_t[0:HALF, 0:2 * P].rearrange("p (k n) -> p k n", k=2)[:, :, 0:BATCH])\
                .then_inc(hT_ready, 1)

            act.wait_ge(wcls_done, 1)
            nc.scalar.copy(wcls[:, :, :].rearrange("p k c -> p (k c)"), ps_t[:, 256:256 + C]).then_inc(wcls_copied, 1)

            def copy_w(t):
                act.wait_ge(w_done, t + 1)
                if t >= 2:
                    act.wait_ge(wwp_ready, t - 1)
                src = ps_w[:, :, 0:3 * P].rearrange("p k (j n) -> p k j n", n=PATCHES)
                nc.scalar.copy(w_s[:, t % 2, :, :, 0:PATCHES], src).then_inc(w_copied, 1)
                if t >= 2:
                    act.wait_ge(logits_done, t - 1)
                nc.scalar.activation(wsq[:, t % 2, :, :, 0:PATCHES], src, ACT.Square).then_inc(wsq_ready, 1)

            def exps(t):
                act.wait_ge(soft_step, 6 * t + 2)
                for b in range(IPT):
                    nc.scalar.activation(ex[:, b, :], lg[:, b, :], ACT.Exp, bias=nmx[:, b:b + 1],
                                         accum_out=sm[:, b:b + 1]).then_inc(exp_done, 1)

            for s in range(-1, TILES + 1):
                rr = lo_at[s + 1] if s + 1 < len(lo_at) else []
                if s == 0:
                    act.wait_ge(soft_step, 2)
                if 0 <= s < TILES:
                    exps(s)
                if s + 1 < TILES:
                    copy_w(s + 1)
                for r in rr:
                    copy_part(r)
            copy_part(ROUNDS)

            for j, t in enumerate(FFN_ORDER):
                n = BATCH if t == TILES else P
                act.wait_ge(hid_done, j + 1)
                if j >= 2:
                    act.wait_ge(ffn_done, j - 1)
                src = (ps_w if j % 2 == 0 else ps_b)[:, :, 0:3 * P].rearrange("p k (c n) -> p k c n", n=P)[:, :, :, 0:n]
                dst = gl[:, j % 2, :, 0:n].rearrange("p (k c) n -> p k c n", k=2)
                nc.scalar.activation(dst, src, ACT.Gelu_apprx_tanh).then_inc(gl_ready, 1)
                act.wait_ge(gl_ready, j + 1)
                nc.scalar.activation(glsq[:, j % 2, :, 0:n], gl[:, j % 2, :, 0:n], ACT.Square).then_inc(glsq_ready, 1)

        @block.gpsimd
        def _(pool):
            def rstd_front(t, n=P):
                i = t % 2
                pool.wait_ge(st0_step, 2 * t + 2)
                if t >= 2:
                    pool.wait_ge(hn_ready, t - 1)
                nc.gpsimd.tensor_scalar(rs0[0:n, i, 0:1], mv0[0:n, i, 1:2], EPS, None, ALU.add).then_inc(rs0_step, 1)
                pool.wait_ge(rs0_step, 2 * t + 1)
                nc.gpsimd.tensor_tensor(rs0[0:n, i, 1:2], rs0[0:n, i, 0:1], neg_half[0:n, :], ALU.pow)\
                    .then_inc(rs0_step, 1)

            nc.gpsimd.memset(neg_half[:], -0.5).then_inc(memsets, 1)
            nc.gpsimd.memset(w2g[:, :, D:D + 1], 1.0).then_inc(memsets, 1)
            pool.wait_ge(memsets, 3)
            pool.wait_ge(row_in, 16 * N_ROW)
            for t in range(TILES):
                rstd_front(t)
                pool.wait_ge(hn_ready, t + 1)
                nc.gpsimd.tensor_tensor(h0[:, t, :], h0[:, t, :], bout_sb[:], ALU.add).then_inc(bias_in_h0, 1)
            rstd_front(TILES, BATCH)
            pool.wait_ge(hn_ready, TILES + 1)
            nc.gpsimd.tensor_tensor(h0c[:], h0c[:], bout_sb[0:BATCH, :], ALU.add).then_inc(bias_in_h0, 1)

            pool.wait_ge(wcls_copied, 1)
            src = wcls[:, :, :].unsqueeze(3).to_broadcast([P, 2, 3, IPT])
            for i in range(2):
                for b in range(IPT):
                    nc.gpsimd.tensor_copy(
                        w_s[:, i, :, :, PATCHES].rearrange("p k (c b) -> p k c b", b=IPT)[:, :, :, b], wcls[:])\
                        .then_inc(wcls_spread, 1)
                    nc.gpsimd.tensor_tensor(
                        wsq[:, i, :, :, PATCHES].rearrange("p k (c b) -> p k c b", b=IPT)[:, :, :, b], wcls[:], wcls[:],
                        ALU.mult).then_inc(wcls_spread, 1)

            def squares(t):
                pool.wait_ge(wp_ready, t + 1)
                if t >= 1:
                    pool.wait_ge(att_step, 4 * (t - 1) + 1)
                nc.gpsimd.tensor_tensor(wwp[:], w_s[:, t % 2], wp[:, t % 2], ALU.mult).then_inc(wwp_ready, 1)

            for t in range(TILES):
                squares(t)

            def rstd_mid(t, n=P):
                pool.wait_ge(st1_step, 2 * t + 2)
                nc.gpsimd.tensor_scalar(rs1[0:n, t, 0:1], mv1[0:n, t, 1:2], 1.0 + EPS, EPS * EPS, ALU.mult, ALU.add)\
                    .then_inc(rs1_step, 1)
                pool.wait_ge(rs1_step, 2 * t + 1)
                nc.gpsimd.tensor_tensor(rs1[0:n, t, 1:2], rs1[0:n, t, 0:1], neg_half[0:n, :], ALU.pow)\
                    .then_inc(rs1_step, 1)

            for t in range(TILES):
                rstd_mid(t)
            rstd_mid(TILES, BATCH)
            pool.wait_ge(next_ready, 1)
            nc.gpsimd.partition_all_reduce(sel[:, 2, :], sel[:, 1, :], P, bass.bass_isa.ReduceOp.max)\
                .then_inc(next_all, 1)

            pool.wait_ge(tern_step, 5)
            nc.gpsimd.tensor_tensor(w2q[:], w2q[:], w2neg[:], ALU.subtract).then_inc(w2_sub, 1)

            pool.wait_ge(rows_ready, 2)
            for j, t in enumerate(FFN_ORDER):
                n = BATCH if t == TILES else P
                h = h1c[:] if t == TILES else h1[:, t, :]
                pool.wait_ge(yn_ready, j + 1)
                nc.gpsimd.tensor_tensor(h, h, crow[0:n, :], ALU.add).then_inc(crow_in_h1, 1)
                pool.wait_ge(mom_ready, j + 1)
                i = j % 2
                nc.gpsimd.tensor_tensor(ms[0:n, i, 0:1], mom[0:n, i, 0:1], mom[0:n, i, 0:1], ALU.mult)\
                    .then_inc(ms_step, 1)
                pool.wait_ge(ms_step, 5 * j + 1)
                nc.gpsimd.tensor_tensor(ms[0:n, i, 1:2], mom[0:n, i, 1:2], ms[0:n, i, 0:1], ALU.subtract)\
                    .then_inc(ms_step, 1)
                pool.wait_ge(ms_step, 5 * j + 2)
                nc.gpsimd.tensor_scalar(ms[0:n, i, 0:1], ms[0:n, i, 1:2], 0.0, EPS, ALU.max, ALU.add)\
                    .then_inc(ms_step, 1)
                pool.wait_ge(ms_step, 5 * j + 3)
                if j >= 2:
                    pool.wait_ge(fin_step, 2 * (j - 1))
                nc.gpsimd.tensor_tensor(ms[0:n, i, 2:3], ms[0:n, i, 0:1], neg_half[0:n, :], ALU.pow)\
                    .then_inc(ms_step, 1)
                pool.wait_ge(ms_step, 5 * j + 4)
                nc.gpsimd.tensor_tensor(ms[0:n, i, 3:4], mom[0:n, i, 0:1], ms[0:n, i, 2:3], ALU.mult)\
                    .then_inc(ms_step, 1)

        @block.vector
        def _(dve):
            nc.vector.memset(ones[:], 1.0).then_inc(ones_set, 1)
            nc.vector.memset(ones_bf[:], 1.0).then_inc(ones_set, 1)
            nc.vector.memset(yT[HALF:HALF + 1, :, 1, :], 1.0).then_inc(memsets, 1)
            nc.vector.memset(stepc[:], 2.0 ** (HI_ROUNDS - 1)).then_inc(step_halved, 1)
            nc.vector.memset(cand[:], 2.0 ** (HI_ROUNDS - 1)).then_inc(cand_ready, 1)

            dve.wait_ge(q_in, 16)
            steps = [0]

            def q_op(ins):
                steps[0] += 1
                ins.then_inc(q_step, 1)
                dve.wait_ge(q_step, steps[0])

            def col(i):
                return qs[:, i:i + 1]

            q_op(nc.vector.tensor_scalar(col(0), q_sb[:], float(N_W - 1), None, ALU.mult))
            q_op(nc.vector.tensor_scalar(col(1), col(0), ROUND_MAGIC, None, ALU.add))
            q_op(nc.vector.tensor_scalar(col(1), col(1), ROUND_MAGIC, None, ALU.subtract))
            q_op(nc.vector.tensor_tensor(col(2), col(1), col(0), ALU.is_gt))
            q_op(nc.vector.tensor_tensor(col(2), col(1), col(2), ALU.subtract))
            q_op(nc.vector.tensor_tensor(col(3), col(0), col(2), ALU.subtract))
            q_op(nc.vector.tensor_scalar(col(6), col(3), -1.0, 1.0, ALU.mult, ALU.add))
            q_op(nc.vector.tensor_scalar(col(7), col(3), 0.0, None, ALU.is_gt))
            q_op(nc.vector.tensor_tensor(col(7), col(2), col(7), ALU.add))
            q_op(nc.vector.tensor_scalar(col(4), col(2), 0.0, float(N_W - 1), ALU.max, ALU.min))
            q_op(nc.vector.tensor_scalar(col(5), col(7), 0.0, float(N_W - 1), ALU.max, ALU.min))

            for m in range(2):
                dve.wait_ge(flat_in[m], 16)
                v = flat[m].bitcast(U16).rearrange("p (n e) -> p n e", e=2)
                nc.vector.tensor_scalar(hi16[:, m, :], v[:, :, 1], 0x7FFF, None, ALU.bitwise_and)\
                    .then_inc(halves_ready, 1)

            def cands(r):
                return r + 1 if r < HI_ROUNDS else r + 2

            def masks(r):
                dve.wait_ge(cand_ready, cands(r))
                keys = hi16 if r < HI_ROUNDS else lo16
                if r == 0:
                    dve.wait_ge(halves_ready, 2)
                for m in range(2):
                    nc.vector.tensor_scalar(cmask[:, m, :], keys[:, m, :], cand[:, m:m + 1], None, ALU.is_lt)\
                        .then_inc(mask_ready, 1)

            def update(r):
                dve.wait_ge(count_done, r + 1)
                nc.vector.tensor_scalar(turn[:], cnt_all, col(4), 0.5, ALU.is_le, ALU.subtract)\
                    .then_inc(turn_step, 1)
                dve.wait_ge(turn_step, r + 1)
                dve.wait_ge(step_halved, r + 1)
                dve.wait_ge(mask_ready, 2 * (r + 1))
                nc.vector.scalar_tensor_tensor(cand[:], turn[:], stepc[:], cand[:], ALU.mult, ALU.add)\
                    .then_inc(cand_ready, 1)
                if r != HI_ROUNDS - 1:
                    dve.wait_ge(cand_ready, cands(r) + 1)
                    nc.vector.tensor_scalar(stepc[:], stepc[:], 0.5, None, ALU.mult).then_inc(step_halved, 1)
                else:
                    low_keys()

            def low_keys():
                dve.wait_ge(cand_ready, HI_ROUNDS + 1)
                nc.vector.tensor_scalar(hi_f[:], cand[:], 0.5, None, ALU.subtract).then_inc(low_step, 1)
                dve.wait_ge(low_step, 1)
                for m in range(2):
                    nc.vector.tensor_scalar(wide[:, m, :], hi16[:, m, :], hi_f[:, m:m + 1], 65536.0,
                                            ALU.subtract, ALU.mult).then_inc(low_step, 1)
                for m in range(2):
                    v = flat[m].bitcast(U16).rearrange("p (n e) -> p n e", e=2)
                    dve.wait_ge(low_step, 2 + m)
                    nc.vector.tensor_tensor(wide[:, m, :], wide[:, m, :], v[:, :, 0], ALU.add).then_inc(low_step, 1)
                for m in range(2):
                    dve.wait_ge(low_step, 4 + m)
                    nc.vector.tensor_scalar(lo16[:, m, :], wide[:, m, :], 0.0, 65535.0, ALU.max, ALU.min)\
                        .then_inc(low_step, 1)
                nc.vector.memset(stepc[:], 2.0 ** (LO_ROUNDS - 1)).then_inc(step_halved, 1)
                nc.vector.memset(cand[:], 2.0 ** (LO_ROUNDS - 1)).then_inc(cand_ready, 1)
                dve.wait_ge(low_step, 7)


            def stats_front(t, n=P):
                i = t % 2
                src = h0[:, t, :] if t < TILES else h0c[:]
                dst = st0[0:n, i, :]
                nc.vector.bn_stats(dst, src).then_inc(st0_step, 1)
                dve.wait_ge(st0_step, 2 * t + 1)
                nc.vector.bn_aggr(mv0[0:n, i, :], dst).then_inc(st0_step, 1)

            def take_tok(t):
                dve.wait_ge(tok_done, t + 1)
                src = (ps_l if t % 2 == 0 else ps_o)[:, 0:D]
                nc.vector.tensor_tensor(h0[:, t, :], src, tokb_sb[:], ALU.add).then_inc(h0_ready, 1)
                dve.wait_ge(h0_ready, t + 1)

            def norm_front(t, n=P):
                i = t % 2
                src = h0[:, t, :] if t < TILES else h0c[:]
                dve.wait_ge(rs0_step, 2 * t + 2)
                if t >= 2:
                    dve.wait_ge(hn_turned, t - 1)
                nc.vector.tensor_scalar(hn[0:n, i, :], src, mv0[0:n, i, 0:1], rs0[0:n, i, 1:2],
                                        ALU.subtract, ALU.mult).then_inc(hn_ready, 1)

            dve.wait_ge(row_in, 16 * N_ROW)
            for t in range(TILES):
                rr = hi_at[t]
                masks(rr[0])
                take_tok(t)
                stats_front(t)
                update(rr[0])
                for r in rr[1:]:
                    masks(r)
                norm_front(t)
                for r in rr[1:]:
                    update(r)
            stats_front(TILES, BATCH)
            norm_front(TILES, BATCH)

            def norms(t):
                dve.wait_ge(wsq_ready, t + 1)
                if t == 0:
                    dve.wait_ge(wcls_spread, 4 * IPT)
                nc.vector.tensor_reduce(n2[:], wsq[:, t % 2].rearrange("p k j n -> p (k j) n"), AX.X, ALU.add)\
                    .then_inc(norm_step, 1)
                dve.wait_ge(norm_step, 3 * t + 1)
                nc.vector.tensor_scalar(inv[:, 0, :], n2[:], 1e-24, None, ALU.max).then_inc(norm_step, 1)
                dve.wait_ge(norm_step, 3 * t + 2)
                nc.vector.reciprocal(inv[:, 1, :], inv[:, 0, :]).then_inc(norm_step, 1)
                dve.wait_ge(norm_step, 3 * t + 3)
                if t >= 1:
                    dve.wait_ge(logits_done, t)
                nc.vector.tensor_tensor(invm[:, :, :].rearrange("p (c b) h -> p c b h", b=IPT),
                                        hcols_sb[:, :, :].unsqueeze(2).to_broadcast([P, C, IPT, HEADS]),
                                        inv[:, 1, :].rearrange("p (c b) -> p c b", b=IPT).unsqueeze(3)
                                        .to_broadcast([P, C, IPT, HEADS]), ALU.mult).then_inc(invm_ready, 1)

            def soft_a(t):
                dve.wait_ge(logits_done, t + 1)
                if t >= 1:
                    dve.wait_ge(exp_done, 2 * t)
                nc.vector.tensor_scalar(lg[:, :, :].rearrange("h b n -> h (b n)"), ps_l[0:HEADS, 0:2 * SEQ],
                                        temp_sb[:], None, ALU.mult).then_inc(soft_step, 1)
                dve.wait_ge(soft_step, 6 * t + 1)
                nc.vector.tensor_reduce(nmx[:], lg[:], AX.X, ALU.max, negate=True).then_inc(soft_step, 1)

            def soft_b(t):
                dve.wait_ge(exp_done, 2 * (t + 1))
                nc.vector.reciprocal(rsm[:], sm[:]).then_inc(soft_step, 1)
                dve.wait_ge(soft_step, 6 * t + 3)
                if t >= 1:
                    dve.wait_ge(spread_done, t)
                nc.vector.tensor_tensor(pi[:, :, 0:SEQ], ex[:], rsm[:].unsqueeze(2).to_broadcast([HEADS, 2, SEQ]),
                                        ALU.mult).then_inc(soft_step, 1)
                dve.wait_ge(soft_step, 6 * t + 4)
                nc.vector.tensor_reduce(sp[:, 0, :], pi[:, :, 0:SEQ], AX.X, ALU.add).then_inc(soft_step, 1)
                dve.wait_ge(soft_step, 6 * t + 5)
                nc.vector.tensor_scalar(sp[:, 1, :], sp[:, 0, :], 1e-8, None, ALU.add).then_inc(soft_step, 1)
                dve.wait_ge(soft_step, 6 * t + 6)
                nc.vector.reciprocal(pi[:, :, SEQ], sp[:, 1, :]).then_inc(pi_ready, 1)

            def spread_view():
                return ps_b[:, :, 0:6 * (SEQ + 1)].rearrange("p k (j n) -> p k j n", n=SEQ + 1)

            def weigh(t):
                dve.wait_ge(spread_done, t + 1)
                dve.wait_ge(w_copied, t + 1)
                if t >= 2:
                    dve.wait_ge(ocls_ready, t - 1)
                    dve.wait_ge(wwp_ready, t - 1)
                nc.vector.tensor_tensor(wp[:, t % 2], w_s[:, t % 2], spread_view()[:, :, :, 0:SEQ], ALU.mult)\
                    .then_inc(wp_ready, 1)

            def attend(t):
                dve.wait_ge(wwp_ready, t + 1)
                nc.vector.tensor_reduce(ds[:], wwp[:, :, :, :].rearrange("p k j n -> p (k j) n"), AX.X, ALU.add)\
                    .then_inc(att_step, 1)
                dve.wait_ge(att_step, 4 * t + 1)
                nc.vector.tensor_tensor(att[:, 0, :].rearrange("p (k j) -> p k j", k=2),
                                        ds[:].rearrange("p (k j) -> p k j", k=2),
                                        spread_view()[:, :, :, SEQ], ALU.mult).then_inc(att_step, 1)
                dve.wait_ge(att_step, 4 * t + 2)
                nc.vector.tensor_scalar(att[:, 1, :], att[:, 0, :], -1.0, -1.0, ALU.mult, ALU.add).then_inc(att_step, 1)
                dve.wait_ge(att_step, 4 * t + 3)
                nc.vector.reciprocal(att[:, 2, :], att[:, 1, :]).then_inc(att_step, 1)
                dve.wait_ge(att_step, 4 * t + 4)
                dve.wait_ge(wp_ready, t + 1)
                if t >= 2:
                    dve.wait_ge(out_done, t - 1)
                src = wp[:, t % 2].rearrange("p k j n -> p (k j) n")
                dst = oT[:, t % 2, :, :].rearrange("p c (b n) -> p (c b) n", b=IPT)
                nc.vector.tensor_tensor(dst, src[:, :, 0:PATCHES],
                                        att[:, 2, :].unsqueeze(2).to_broadcast([P, 12, PATCHES]), ALU.mult)\
                    .then_inc(oT_ready, 1)
                nc.vector.tensor_tensor(ocls[:, :, IPT * t:IPT * (t + 1)],
                                        src[:, :, PATCHES].rearrange("p (c b) -> p c b", b=IPT),
                                        att[:, 2, :].rearrange("p (c b) -> p c b", b=IPT), ALU.mult)\
                    .then_inc(ocls_ready, 1)

            def take_out(t):
                n = P if t < TILES else BATCH
                dst = h1[:, t, :] if t < TILES else h1c[:]
                src = h0[:, t, :] if t < TILES else h0c[:]
                dve.wait_ge(out_done, t + 1)
                dve.wait_ge(bias_in_h0, t + 1)
                nc.vector.tensor_tensor(dst, ps_o[0:n, 0:D], src, ALU.add).then_inc(h1_ready, 1)
                dve.wait_ge(h1_ready, t + 1)
                nc.vector.bn_stats(st1[0:n, t % 2, :], dst).then_inc(st1_step, 1)
                dve.wait_ge(st1_step, 2 * t + 1)
                nc.vector.bn_aggr(mv1[0:n, t, :], st1[0:n, t % 2, :]).then_inc(st1_step, 1)

            for s in range(-1, TILES + 1):
                rr = lo_at[s + 1] if s + 1 < len(lo_at) else []
                if 0 <= s < TILES:
                    soft_b(s)
                if rr:
                    masks(rr[0])
                if 0 <= s < TILES:
                    weigh(s)
                if rr:
                    update(rr[0])
                if s + 1 < TILES:
                    norms(s + 1)
                for i, r in enumerate(rr[1:]):
                    masks(r)
                    if i < len(rr) - 2:
                        update(r)
                if 1 <= s:
                    take_out(s - 1)
                if 0 <= s < TILES:
                    attend(s)
                if len(rr) > 1:
                    update(rr[-1])
                if s + 1 < TILES:
                    soft_a(s + 1)
            take_out(TILES)

            done = [0]

            def sel_op(ins):
                done[0] += 1
                ins.then_inc(sel_step2, 1)
                dve.wait_ge(sel_step2, done[0])

            dve.wait_ge(cand_ready, ROUNDS + 2)
            sel_op(nc.vector.tensor_scalar(bits[:, 0, :], cand[:], 0.5, None, ALU.subtract))
            sel_op(nc.vector.tensor_copy(bits[:, 1, :], hi_f[:]))
            sel_op(nc.vector.tensor_scalar(bits[:, 2, :], bits[:, 1, :], 16, None, ALU.logical_shift_left))
            sel_op(nc.vector.tensor_tensor(bits[:, 3, :], bits[:, 2, :], bits[:, 0, :], ALU.bitwise_or))
            s_lo = bits[:, 3, :].bitcast(F32)
            dve.wait_ge(abs_done, 2)
            for m in range(2):
                nc.vector.tensor_scalar(cmask[:, m, :], absw[:, m, :], s_lo[:, m:m + 1], None, ALU.is_le)\
                    .then_inc(mask_ready, 1)
            for m in range(2):
                sel_op(nc.vector.tensor_scalar(wide[:, m, :], absw[:, m, :], s_lo[:, m:m + 1], BIG,
                                               ALU.is_le, ALU.mult))
                sel_op(nc.vector.tensor_tensor(wide[:, m, :], wide[:, m, :], absw[:, m, :], ALU.add))
                sel_op(nc.vector.tensor_reduce(sel[:, 0, m:m + 1], wide[:, m, :], AX.X, ALU.min))
            nc.vector.tensor_scalar(sel[:, 1, :], sel[:, 0, :], -1.0, None, ALU.mult).then_inc(next_ready, 1)
            dve.wait_ge(count_done, ROUNDS + 1)
            nc.vector.tensor_scalar(sel[:, 3, :], cnt_all, col(5), None, ALU.is_gt).then_inc(sel_step, 1)
            dve.wait_ge(sel_step, 1)
            sel_op(nc.vector.tensor_tensor(sel[:, 4, :], sel[:, 3, :], s_lo, ALU.mult))
            sel_op(nc.vector.tensor_scalar(sel[:, 5, :], sel[:, 3, :], 1.0, None, ALU.subtract))
            dve.wait_ge(next_all, 1)
            sel_op(nc.vector.tensor_tensor(sel[:, 6, :], sel[:, 5, :], sel[:, 2, :], ALU.mult))
            sel_op(nc.vector.tensor_tensor(sel[:, 7, :], sel[:, 4, :], sel[:, 6, :], ALU.add))
            sel_op(nc.vector.tensor_scalar(sel[:, 8, :], s_lo, col(6), None, ALU.mult))
            sel_op(nc.vector.tensor_scalar(sel[:, 9, :], sel[:, 7, :], col(3), None, ALU.mult))
            sel_op(nc.vector.tensor_tensor(sel[:, 10, :], sel[:, 8, :], sel[:, 9, :], ALU.add))
            sel_op(nc.vector.tensor_scalar(sel[:, 11, :], sel[:, 10, :], -1.0, None, ALU.mult))
            dve.wait_ge(asum_done, 1)
            sel_op(nc.vector.tensor_scalar(w_scale[:], cnt_all, 1.0 / N_W, None, ALU.mult))

            def th(m, n=P):
                return sel[0:n, 10, m:m + 1]

            def nth(m, n=P):
                return sel[0:n, 11, m:m + 1]

            dve.wait_ge(ffn_in, 16 * N_FFN)
            nc.vector.tensor_scalar(w1q[0:HALF], w1t_sb[:], th(0, HALF), w_scale[0:HALF, 0:1], ALU.is_gt, ALU.mult)\
                .then_inc(tern_step, 1)
            nc.vector.tensor_scalar(w1neg[:], w1t_sb[:], nth(0, HALF), w_scale[0:HALF, 0:1], ALU.is_lt, ALU.mult)\
                .then_inc(tern_step, 1)
            dve.wait_ge(tern_step, 2)
            nc.vector.tensor_tensor(w1q[0:HALF], w1q[0:HALF], w1neg[:], ALU.subtract).then_inc(tern_step, 1)
            nc.vector.tensor_scalar(w2q[:], w2f_sb[:], th(1), w_scale[:, 1:2], ALU.is_gt, ALU.mult)\
                .then_inc(tern_step, 1)
            nc.vector.tensor_scalar(w2neg[:], w2f_sb[:], nth(1), w_scale[:, 1:2], ALU.is_lt, ALU.mult)\
                .then_inc(tern_step, 1)

            def norm_mid(j):
                t = FFN_ORDER[j]
                n = BATCH if t == TILES else P
                src = h1c[:] if t == TILES else h1[:, t, :]
                dve.wait_ge(rs1_step, 2 * t + 2)
                if j >= 2:
                    dve.wait_ge(yn_turned, j - 1)
                nc.vector.tensor_scalar(yn[0:n, j % 2, :], src, mv1[0:n, t, 0:1], rs1[0:n, t, 1:2],
                                        ALU.subtract, ALU.mult).then_inc(yn_ready, 1)

            def take_yT(j):
                n = BATCH if FFN_ORDER[j] == TILES else P
                dve.wait_ge(yn_turned, j + 1)
                if j >= 2:
                    dve.wait_ge(hid_done, j - 1)
                src = ps_c if j % 2 == 0 else ps_l
                for k in range(2):
                    nc.vector.tensor_scalar(yT[0:HALF, j % 2, k, 0:n], src[0:HALF, 128 + k * P:128 + k * P + n],
                                            ln1g_sb[:, k:k + 1], ln1b_sb[:, k:k + 1], ALU.mult, ALU.add)\
                        .then_inc(yT_ready, 1)

            def finish(j):
                t = FFN_ORDER[j]
                n = BATCH if t == TILES else P
                i = j % 2
                src = ps_o if j % 2 == 0 else ps_t
                h = h1c[:] if t == TILES else h1[:, t, :]
                dve.wait_ge(ffn_done, j + 1)
                if j >= 2:
                    dve.wait_ge(ms_step, 5 * (j - 1))
                nc.vector.tensor_scalar(mom[0:n, i, :], src[0:n, D:D + 2], 1.0 / HID, None, ALU.mult)\
                    .then_inc(mom_ready, 1)
                if j + 1 < len(FFN_ORDER):
                    pass
                dve.wait_ge(ms_step, 5 * (j + 1))
                dve.wait_ge(crow_in_h1, j + 1)
                if j >= 2:
                    dve.wait_ge(stored[i], 16 * stores_before(i, j - 1))
                nc.vector.scalar_tensor_tensor(fin[0:n, i, :], cg[0:n, :], ms[0:n, i, 3:4], h, ALU.mult, ALU.add)\
                    .then_inc(fin_step, 1)
                dve.wait_ge(fin_step, 2 * j + 1)
                nc.vector.scalar_tensor_tensor(fin[0:n, i, :], src[0:n, 0:D], ms[0:n, i, 2:3], fin[0:n, i, :],
                                               ALU.mult, ALU.add).then_inc(fin_step, 1)

            norm_mid(0)
            dve.wait_ge(memsets, 3)
            take_yT(0)
            nc.vector.tensor_copy(bet_b[:], ln2b_sb[:].unsqueeze(2).to_broadcast([P, C, P])).then_inc(bet_ready, 1)
            dve.wait_ge(w2_sub, 1)
            for c in range(C):
                nc.vector.tensor_scalar(w2g[:, c, 0:D], w2q[:, c, :], ln2g_sb[:, c:c + 1], None, ALU.mult)\
                    .then_inc(w2g_ready, 1)
            norm_mid(1)
            take_yT(1)
            dve.wait_ge(rows_done, 1)
            nc.vector.tensor_tensor(crow[:], ps_t[:, 0:D], b2_sb[:], ALU.add).then_inc(rows_ready, 1)
            nc.vector.tensor_scalar(cg[:], ps_t[:, D:2 * D], -1.0, None, ALU.mult).then_inc(rows_ready, 1)
            for j in range(len(FFN_ORDER)):
                if j + 2 < len(FFN_ORDER):
                    norm_mid(j + 2)
                    take_yT(j + 2)
                finish(j)


def kernel(x, cls_tok, L0_tok_W, L0_tok_b, L0_attn_w_qkv, L0_attn_temp, L0_attn_w_out, L0_attn_b_out, L0_ffn_ln1_g,
           L0_ffn_ln1_b, L0_ffn_W1, L0_ffn_b1, L0_ffn_ln2_g, L0_ffn_ln2_b, L0_ffn_W2, L0_ffn_b2, L0_ffn_sparsity):
    import concourse.bacc as _bacc
    from concourse.bass_utils import run_bass_kernel_spmd as _run

    def chunks(a, rows):
        a = np.asarray(a)
        return a.reshape(a.shape[0] // rows, rows, -1).transpose(1, 0, 2)

    img = np.asarray(x).reshape(BATCH, 8, 16, 8, 16, 3).transpose(2, 4, 5, 0, 1, 3).reshape(C, P, TILES, P)
    heads = np.repeat(np.eye(HEADS, dtype=np.float32), PATCHES, axis=0)
    ins = {
        "x_t": img.transpose(2, 1, 0, 3),
        "cls_tok": np.asarray(cls_tok).reshape(D),
        "tok_w": chunks(L0_tok_W, P),
        "tok_b": L0_tok_b,
        "w_qkv": chunks(L0_attn_w_qkv, HALF),
        "temp": L0_attn_temp,
        "w_out": chunks(L0_attn_w_out, P),
        "b_out": L0_attn_b_out,
        "ln1_g": np.asarray(L0_ffn_ln1_g).reshape(2, HALF).T,
        "ln1_b": np.asarray(L0_ffn_ln1_b).reshape(2, HALF).T,
        "w1_flat": np.asarray(L0_ffn_W1).reshape(P, WCOLS),
        "w1_t": chunks(np.asarray(L0_ffn_W1).T, HALF),
        "b1": np.asarray(L0_ffn_b1).reshape(1, HID),
        "ln2_g": np.asarray(L0_ffn_ln2_g).reshape(C, P).T,
        "ln2_b": np.asarray(L0_ffn_ln2_b).reshape(C, P).T,
        "w2_t": chunks(np.asarray(L0_ffn_W2).T, P),
        "b2": L0_ffn_b2,
        "sparsity": np.asarray(L0_ffn_sparsity).reshape(1),
        "head_cols": chunks(heads, P),
        "head_rows": np.ascontiguousarray(heads.T).reshape(HEADS, C, P),
        "ident_c": np.eye(P, dtype=np.float32),
    }
    nc = _bacc.Bacc("TRN2", target_bir_lowering=False, num_devices=1)
    arrays, args = {}, {}
    for name, a in ins.items():
        a = np.ascontiguousarray(a)
        arrays[f"in_{name}"] = a
        args[name] = nc.dram_tensor(f"in_{name}", a.shape, mybir.dt.from_np(a.dtype), kind="ExternalInput").ap()
    out = nc.dram_tensor("out_0", (BATCH, SEQ, D), F32, kind="ExternalOutput").ap()
    vit_block(nc, out=out, **args)
    r = _run(nc, [arrays], core_ids=[0])
    return r.results[0]["out_0"]
```

```python
from contextlib import ExitStack

import numpy as np

import concourse.bass as bass
from concourse import mybir
from concourse.alu_op_type import AluOpType as ALU

ACT = mybir.ActivationFunctionType
AX = mybir.AxisListType
F32 = mybir.dt.float32
BF16 = mybir.dt.bfloat16
I32 = mybir.dt.int32
F16 = mybir.dt.float16
U16 = mybir.dt.uint16

P = 128
BATCH = 16
PATCHES = 64
SEQ = PATCHES + 1
D = 192
HALF = D // 2
HID = 768
C = HID // P
HEADS = 12
IPT = P // PATCHES
TILES = BATCH // IPT
EPS = 1e-5
N_W = HID * D
WCOLS = N_W // P
HI_ROUNDS = 15
LO_ROUNDS = 16
ROUNDS = HI_ROUNDS + LO_ROUNDS
BIG = 3.0e38
ROUND_MAGIC = 1.5 * 2.0 ** 23
MCH = WCOLS // P

EARLY = 2
ATTN_PLAN = [3] * 7
assert EARLY + TILES + sum(ATTN_PLAN) == ROUNDS


def head_row(h):
    c = h // 2
    return 32 * (c % 4) + 2 * (c // 4) + h % 2


def vit_block(nc, x_t, cls_tok, tok_w, rows3, w_qkv, temp, w_out, ln1_gb, w1_flat, w1_t, b1,
              ln2_gb, w2_t, sparsity, head_cols, rows_ident, out):
    ctx = ExitStack()
    with ctx:
        def sb(name, shape, dt=F32):
            return ctx.enter_context(nc.sbuf_tensor(name, shape, dt))

        def pb(name, shape, dt=F32):
            return ctx.enter_context(nc.psum_tensor(name, shape, dt))

        def sem(name):
            return ctx.enter_context(nc.semaphore(name))

        x_sb = sb("x_sb", [P, TILES, C, P])
        tokw_sb = sb("tokw_sb", [P, C, D])
        rows3_sb = sb("rows3_sb", [P, 3, D])
        tokb_sb, bout_sb, b2_sb = (rows3_sb[:, i, :] for i in range(3))
        wqkv_sb = sb("wqkv_sb", [HALF, 2, HID])
        wout_sb = sb("wout_sb", [P, C, D])
        temp_sb = sb("temp_sb", [P, 1])
        ln1gb_sb = sb("ln1gb_sb", [HALF, 2, 2])
        ln2gb_sb = sb("ln2gb_sb", [P, 2, C])
        hcols_sb = sb("hcols_sb", [P, C, 32])
        ri_sb = sb("ri_sb", [P, C + 1, P])
        hrows_sb = ri_sb[:, 0:C, :]
        ident = ri_sb[:, C, :]
        ones = sb("ones", [P, P])
        ones_bf = sb("ones_bf", [P, P], BF16)
        twos_bf = sb("twos_bf", [P, 2], BF16)
        half_n = sb("half_n", [P, 2], BF16)
        neg_half = sb("neg_half", [P, 1])

        h0 = sb("h0", [P, TILES, D])
        h0c = sb("h0c", [BATCH, D])
        hn = sb("hn", [P, 2, D])
        hT_all = sb("hT_all", [HALF, 2, TILES * P + 1])
        st0 = sb("st0", [P, 2, 6])
        mv0 = sb("mv0", [P, 2, 2])
        rs0 = sb("rs0", [P, 2, 2])

        w_s = sb("w_s", [P, 2, 2, 6, SEQ])
        wsq = sb("wsq", [P, 2, 2, 6, SEQ])
        wcls = sb("wcls", [P, 2, 3])
        n2 = sb("n2", [P, 12])
        inv = sb("inv", [P, 2, 12])
        invm = sb("invm", [P, 12, 32])
        lg = sb("lg", [P, 2, SEQ])
        nmx = sb("nmx", [P, 2])
        ex = sb("ex", [P, 2, SEQ])
        sm = sb("sm", [P, 2])
        rsm = sb("rsm", [P, 2])
        pi = sb("pi", [P, 2, SEQ + 1])
        sp = sb("sp", [P, 2, 2])
        wp = sb("wp", [P, 2, 2, 6, SEQ])
        wwp = sb("wwp", [P, 2, 6, SEQ])
        ds = sb("ds", [P, 12])
        att = sb("att", [P, 4, 12])
        oT = sb("oT", [P, 2, C, P])
        ocls = sb("ocls", [P, C, BATCH])

        h1 = sb("h1", [P, TILES, D])
        h1c = sb("h1c", [BATCH, D])
        yn = sb("yn", [P, 2, D])
        ync = sb("ync", [BATCH, D])
        st1 = sb("st1", [P, 2, 6])
        mv1 = sb("mv1", [P, TILES + 1, 2])
        rs1 = sb("rs1", [P, TILES + 1, 2])
        yT = sb("yT", [HALF + 1, 2, 2, P + BATCH])
        w1q = sb("w1q", [HALF + 1, 2, HID])
        w1t_sb = sb("w1t_sb", [HALF, 2, HID])
        w1neg = sb("w1neg", [HALF, 2, HID])
        w2q = sb("w2q", [P, C, D])
        w2neg = sb("w2neg", [P, C, D])
        w2g = sb("w2g", [P, C, D + 1])
        bet_b = sb("bet_b", [P, C, P])
        cg = sb("cg", [P, D])
        crow = sb("crow", [P, D])
        gl = sb("gl", [P, 2, C, P + BATCH])
        glsq = sb("glsq", [P, 2, C, P + BATCH])
        gsum = sb("gsum", [P, 2, P + BATCH])
        mom = sb("mom", [P, 2, 2])
        ms = sb("ms", [P, 2, 4])
        fin = sb("fin", [P, 2, D])

        w1f_sb = sb("w1f_sb", [P, WCOLS])
        w2f_sb = sb("w2f_sb", [P, C, D])
        w2f = w2f_sb[:, :, :].rearrange("p c n -> p (c n)")
        flat = [w1f_sb[:, :], w2f]
        absw = sb("absw", [P, 2, WCOLS])
        hi16 = sb("hi16", [P, 2, WCOLS], U16)
        lo16 = sb("lo16", [P, 2, WCOLS], U16)
        wide = sb("wide", [P, 2, WCOLS])
        cmask = sb("cmask", [P, 2, WCOLS], BF16)
        asum = sb("asum", [P, 2])
        part = sb("part", [P, 2], F16)
        signs = sb("signs", [P, WCOLS], BF16)
        cand_off = sb("cand_off", [P, 2])
        cand = sb("cand", [P, 2])
        turn = sb("turn", [P, 2])
        stepc = sb("stepc", [P, 1])
        q_sb = sb("q_sb", [P, 1])
        qs = sb("qs", [P, 12])
        hi_f = sb("hi_f", [P, 2])
        bits = sb("bits", [P, 4, 2], I32)
        sel = sb("sel", [P, 12, 2])
        w_scale = sb("w_scale", [P, 2])

        ps_w = pb("ps_w", [P, 2, 512])
        ps_b = pb("ps_b", [P, 2, 512])
        ps_l = pb("ps_l", [P, 512])
        ps_o = pb("ps_o", [P, 512])
        ps_t = pb("ps_t", [P, 512])
        ps_c = pb("ps_c", [P, 512])
        cnt_part = ps_c[:, 0:2]
        cnt_all = ps_c[:, 4:6]

        x_in = [sem(f"x_in{t}") for t in range(TILES)]
        tokw_in = sem("tokw_in")
        consts_in = sem("consts_in")
        row_in = sem("row_in")
        flat_in = [sem("w1_flat_in"), sem("w2_flat_in")]
        q_in = sem("q_in")
        attn_in = sem("attn_in")
        ffn_in = sem("ffn_in")
        memsets = sem("memsets")
        ones_set = sem("ones_set")
        tok_done = sem("tok_done")
        h0_ready = sem("h0_ready")
        st0_step = sem("st0_step")
        rs0_step = sem("rs0_step")
        hn_ready = sem("hn_ready")
        hn_turned = sem("hn_turned")
        hT_ready = sem("hT_ready")
        bias_in_h0 = sem("bias_in_h0")
        wcls_done = sem("wcls_done")
        wcls_copied = sem("wcls_copied")
        wcls_spread = sem("wcls_spread")
        w_done = sem("w_done")
        w_copied = sem("w_copied")
        wsq_ready = sem("wsq_ready")
        norm_step = sem("norm_step")
        invm_ready = sem("invm_ready")
        logits_done = sem("logits_done")
        lg_ready = sem("lg_ready")
        nmx_ready = sem("nmx_ready")
        rsm_ready = sem("rsm_ready")
        pi_scaled = sem("pi_scaled")
        sp_ready = sem("sp_ready")
        exp_done = sem("exp_done")
        pi_ready = sem("pi_ready")
        spread_done = sem("spread_done")
        wp_ready = sem("wp_ready")
        wwp_ready = sem("wwp_ready")
        att_step = sem("att_step")
        oT_ready = sem("oT_ready")
        ocls_ready = sem("ocls_ready")
        out_done = sem("out_done")
        h1_ready = sem("h1_ready")
        st1_step = sem("st1_step")
        rs1_step = sem("rs1_step")
        yn_ready = sem("yn_ready")
        ync_ready = sem("ync_ready")
        gsum_ready = sem("gsum_ready")
        yn_turned = sem("yn_turned")
        yT_ready = sem("yT_ready")
        crow_in_h1 = sem("crow_in_h1")
        hid_done = sem("hid_done")
        gl_ready = sem("gl_ready")
        glsq_ready = sem("glsq_ready")
        ffn_done = sem("ffn_done")
        mom_ready = sem("mom_ready")
        ms_step = sem("ms_step")
        fin_step = sem("fin_step")
        stored = [sem("stored_even"), sem("stored_odd")]
        abs_done = sem("abs_done")
        halves_ready = sem("halves_ready")
        q_step = sem("q_step")
        cand_ready = sem("cand_ready")
        mask_ready = sem("mask_ready")
        part_done = sem("part_done")
        part_copied = sem("part_copied")
        count_done = sem("count_done")
        turn_step = sem("turn_step")
        step_halved = sem("step_halved")
        low_step = sem("low_step")
        sel_step = sem("sel_step")
        sel_step2 = sem("sel_step2")
        next_ready = sem("next_ready")
        next_all = sem("next_all")
        asum_done = sem("asum_done")
        thresh_ready = sem("thresh_ready")
        tern_step = sem("tern_step")
        w2_sub = sem("w2_sub")
        w2g_ready = sem("w2g_ready")
        bet_ready = sem("bet_ready")
        rows_done = sem("rows_done")
        rows_ready = sem("rows_ready")

        N_ATTN = 4
        N_FFN = 4
        CLS = TILES
        CLS_WITH = 2
        JOBS = [(t, 0, P) for t in range(TILES)]
        JOBS.insert(CLS_WITH + 1, (CLS, P, BATCH))
        NJ = len(JOBS)
        rounds_of = {s - 1: [EARLY + TILES + sum(ATTN_PLAN[:s]) + i for i in range(k)]
                     for s, k in enumerate(ATTN_PLAN)}
        block = ctx.enter_context(nc.Block())

        def job(i):
            t, col, n = JOBS[i]
            return t, CLS_WITH if t == CLS else t, col, n, h1c[:] if t == CLS else h1[:, t, :]

        def last_job(t):
            return t + 2 if t >= CLS_WITH else t + 1

        def width(t):
            return P + BATCH if t == CLS_WITH else P

        def stores_before(i, j):
            return sum(1 if t == CLS else IPT for t, _, _ in JOBS[i:j:2])

        @block.sync
        def _(sp):
            sp.dma_start(x_sb[:, 0], x_t[0]).then_inc(x_in[0], 16)
            sp.dma_start(flat[0], w1_flat).then_inc(flat_in[0], 16)
            sp.dma_start(h0c[:], cls_tok.partition_broadcast(BATCH)).then_inc(row_in, 16)
            sp.dma_start(rows3_sb[:], rows3.partition_broadcast(P)).then_inc(row_in, 16)
            for t in range(1, TILES):
                sp.dma_start(x_sb[:, t], x_t[t]).then_inc(x_in[t], 16)
                if t == 3:
                    sp.dma_start(wqkv_sb[:], w_qkv).then_inc(attn_in, 16)
            sp.dma_start(wout_sb[:], w_out).then_inc(attn_in, 16)
            sp.dma_start(w1t_sb[:], w1_t).then_inc(ffn_in, 16)
            sp.dma_start(w1q[HALF:HALF + 1, 1, :], b1).then_inc(ffn_in, 16)
            sp.dma_start(ln1gb_sb[:], ln1_gb).then_inc(ffn_in, 16)
            sp.dma_start(ln2gb_sb[:], ln2_gb).then_inc(ffn_in, 16)
            for i, (t, _, n) in enumerate(JOBS):
                sp.wait_ge(fin_step, 2 * (i + 1))
                if t == CLS:
                    sp.dma_start(out[:, 0, :], fin[0:n, i % 2, :]).then_inc(stored[i % 2], 16)
                else:
                    for b in range(IPT):
                        sp.dma_start(out[IPT * t + b, 1:SEQ, :],
                                     fin[PATCHES * b:PATCHES * (b + 1), i % 2, :]).then_inc(stored[i % 2], 16)
            for i in range(2):
                sp.wait_ge(stored[i], 16 * stores_before(i, NJ))

        def turn_bank(f):
            return ps_t if f % 2 == 0 else ps_b[:, 0, :]

        def ffn_turn_bank(j):
            return ps_c if j % 2 == 0 else ps_l

        def hidden_bank(j):
            return ps_w if j % 2 == 0 else ps_b

        def contract_bank(j):
            return ps_t if j % 2 == 0 else ps_o

        def cands(r):
            return r + 1 if r < HI_ROUNDS else r + 2

        @block.tensor
        def _(pe):
            def count(r, both=False):
                pe.wait_ge(mask_ready, r + 1 if not both else ROUNDS + 2)
                for m in range(2 if both else 1):
                    for k in range(MCH):
                        last = nc.tensor.matmul(cnt_part[:, m:m + 1], cmask[:, m, k * P:(k + 1) * P],
                                                twos_bf[:, 0:1], start=(k == 0), stop=(k == MCH - 1))
                last.then_inc(part_done, 1)

            def total(r, both=False):
                pe.wait_ge(part_copied, r + 1)
                if not both:
                    nc.tensor.matmul(cnt_all, ones_bf[:], half_n[:], start=True, stop=False)
                nc.tensor.matmul(cnt_all, ones_bf[:], part[:], start=both, stop=True).then_inc(count_done, 1)

            def embed(t, ks):
                if ks[0] == 0:
                    if t == 0:
                        pe.wait_ge(tokw_in, 16)
                    if t >= 2:
                        pe.wait_ge(h0_ready, t - 1)
                    pe.wait_ge(x_in[t], 16)
                dst = (ps_l if t % 2 == 0 else ps_o)[:, 0:D]
                for k in ks:
                    last = nc.tensor.matmul(dst, x_sb[:, t, k, :], tokw_sb[:, k, :],
                                            start=(k == 0), stop=(k == C - 1))
                if ks[-1] == C - 1:
                    last.then_inc(tok_done, 1)

            def turn_hn(f):
                n = BATCH if f == 0 else P
                pe.wait_ge(hn_ready, f + 1)
                if f >= 2:
                    pe.wait_ge(hT_ready, f - 1)
                for k in range(2):
                    last = nc.tensor.transpose(turn_bank(f)[0:HALF, k * P:k * P + n],
                                               hn[0:n, f % 2, k * HALF:(k + 1) * HALF], ident[0:n, 0:n])
                last.then_inc(hn_turned, 1)

            def project(t, half):
                if half == 0:
                    pe.wait_ge(hT_ready, t + 2)
                    if t == 0:
                        pe.wait_ge(attn_in, 16 * N_ATTN)
                    else:
                        pe.wait_ge(w_copied, t)
                n = P + 1 if t == 0 else P
                at = t * P + (t > 0)
                for c in range(3 * half, 3 * half + 3):
                    for k in range(2):
                        last = nc.tensor.matmul(ps_w[:, half, (c % 3) * n:(c % 3 + 1) * n],
                                                wqkv_sb[:, k, c * P:(c + 1) * P], hT_all[:, k, at:at + n],
                                                start=(k == 0), stop=(k == 1))
                if half == 1:
                    last.then_inc(w_done, 1)

            def logits(t):
                pe.wait_ge(invm_ready, t + 1)
                if t >= 1:
                    pe.wait_ge(lg_ready, t)
                for b in range(IPT):
                    for c in range(C):
                        j = 2 * (c % 3) + b
                        g = 32 * (c % 4)
                        last = nc.tensor.matmul(ps_l[g:g + 32, b * SEQ:(b + 1) * SEQ],
                                                invm[:, (c // 3) * 6 + j, :], wsq[:, t % 2, c // 3, j, :],
                                                start=(c < 4), stop=(c + 4 >= C), tile_position=(0, g))
                last.then_inc(logits_done, 1)

            def spread(t):
                pe.wait_ge(pi_ready, t + 1)
                if t >= 1:
                    pe.wait_ge(att_step, 4 * (t - 1) + 2)
                for c in range(C):
                    last = nc.tensor.matmul(ps_b[:, c // 3, (c % 3) * 2 * (SEQ + 1):(c % 3 + 1) * 2 * (SEQ + 1)],
                                            hrows_sb[:, c, :], pi[:, :, :].rearrange("h b n -> h (b n)"),
                                            start=True, stop=True)
                last.then_inc(spread_done, 1)

            def combine(t, cs):
                if cs[0] == 0:
                    pe.wait_ge(oT_ready, t + 1)
                    if t >= 1:
                        pe.wait_ge(h1_ready, t)
                for c in cs:
                    last = nc.tensor.matmul(ps_o[:, 0:D], oT[:, t % 2, c, :], wout_sb[:, c, :],
                                            start=(c == 0), stop=(c == C - 1))
                if cs[-1] == C - 1:
                    last.then_inc(out_done, 1)

            def combine_cls():
                pe.wait_ge(ocls_ready, TILES)
                pe.wait_ge(h1_ready, TILES)
                for c in range(C):
                    last = nc.tensor.matmul(ps_o[0:BATCH, 0:D], ocls[:, c, :], wout_sb[:, c, :],
                                            start=(c == 0), stop=(c == C - 1))
                last.then_inc(out_done, 1)

            def beta_row():
                pe.wait_ge(w2_sub, 1)
                pe.wait_ge(bet_ready, 1)
                for c in range(C):
                    nc.tensor.matmul(ps_t[:, 0:D], bet_b[:, c, :], w2q[:, c, :], start=(c == 0), stop=(c == C - 1))

            def column_sums():
                pe.wait_ge(w2g_ready, C)
                for c in range(C):
                    last = nc.tensor.matmul(ps_t[:, D:2 * D], ones[:], w2g[:, c, 0:D],
                                            start=(c == 0), stop=(c == C - 1))
                last.then_inc(rows_done, 1)

            def turn_yn(t):
                pe.wait_ge(yn_ready, t + 1)
                if t >= 2:
                    pe.wait_ge(yT_ready, 2 * (t - 1))
                if t == CLS_WITH:
                    pe.wait_ge(ync_ready, 1)
                bank = ffn_turn_bank(t)
                for k in range(2):
                    at = 128 + k * width(t)
                    last = nc.tensor.transpose(bank[0:HALF, at:at + P], yn[:, t % 2, k * HALF:(k + 1) * HALF], ident)
                    if t == CLS_WITH:
                        last = nc.tensor.transpose(bank[0:HALF, at + P:at + P + BATCH],
                                                   ync[:, k * HALF:(k + 1) * HALF], ident[0:BATCH, 0:BATCH])
                last.then_inc(yn_turned, 1)

            def hidden(t):
                n = width(t)
                pe.wait_ge(yT_ready, 2 * (t + 1))
                if t == 0:
                    pe.wait_ge(tern_step, 3)
                if t == 1:
                    pe.wait_ge(att_step, 4 * TILES)
                if t >= 2:
                    pe.wait_ge(gl_ready, t - 1)
                for c in range(C):
                    for k in range(2):
                        last = nc.tensor.matmul(hidden_bank(t)[:, c // 3, (c % 3) * n:(c % 3 + 1) * n],
                                                w1q[0:HALF + k, k, c * P:(c + 1) * P], yT[0:HALF + k, t % 2, k, 0:n],
                                                start=(k == 0), stop=(k == 1))
                last.then_inc(hid_done, 1)

            def contract(i):
                _, ht, at, n, _ = job(i)
                dst = contract_bank(i)
                pe.wait_ge(gl_ready, ht + 1)
                if i >= 2:
                    pe.wait_ge(fin_step, 2 * (i - 1))
                if i == 0:
                    pe.wait_ge(rows_ready, 2)
                if i == 1:
                    pe.wait_ge(h1_ready, TILES + 1)
                for c in range(C):
                    nc.tensor.matmul(dst[0:n, 0:D + 1], gl[:, ht % 2, c, at:at + n], w2g[:, c, :],
                                     start=(c == 0), stop=(c == C - 1))
                pe.wait_ge(gsum_ready, ht + 1)
                nc.tensor.matmul(dst[0:n, D + 1:D + 2], gsum[:, ht % 2, at:at + n], ones[:, 0:1],
                                 start=True, stop=True).then_inc(ffn_done, 1)

            pe.wait_ge(ones_set, 4)
            embed(0, range(C))
            for r in range(EARLY):
                count(r)
                total(r)
            pe.wait_ge(consts_in, 16)
            for t in range(TILES):
                r = EARLY + t
                if t + 1 < TILES:
                    embed(t + 1, range(0, 3))
                else:
                    project(0, 0)
                turn_hn(t)
                count(r)
                if t + 1 < TILES:
                    embed(t + 1, range(3, C))
                else:
                    project(0, 1)
                total(r)
            turn_hn(TILES)

            for s in range(-1, TILES):
                rr = rounds_of.get(s, [])
                before = rounds_of.get(s - 1, [])
                if 0 <= s < TILES - 1:
                    project(s + 1, 0)
                if before:
                    total(before[-1])
                if 0 <= s < TILES - 1:
                    project(s + 1, 1)
                if rr:
                    count(rr[0])
                if s >= 0:
                    spread(s)
                if rr:
                    total(rr[0])
                if s >= 1:
                    combine(s - 1, range(0, 3))
                if rr:
                    count(rr[1])
                if s >= 1:
                    combine(s - 1, range(3, C))
                if rr:
                    total(rr[1])
                if s < TILES - 1:
                    logits(s + 1)
                if rr:
                    count(rr[2])
                if s == len(ATTN_PLAN) - 1:
                    count(ROUNDS, both=True)
                    total(ROUNDS, both=True)
                    pe.wait_ge(abs_done, 2)
                    pe.wait_ge(sel_step, 1)
                    nc.tensor.matmul(cnt_all, ones[:], asum[:], start=True, stop=True).then_inc(asum_done, 1)

            turn_yn(0)
            hidden(0)
            combine(TILES - 1, range(C))
            turn_yn(1)
            beta_row()
            combine_cls()
            hidden(1)
            column_sums()
            turn_yn(2)
            contract(0)
            hidden(2)
            for t in range(1, TILES):
                if t + 2 < TILES:
                    turn_yn(t + 2)
                contract(last_job(t - 1))
                if t == CLS_WITH:
                    contract(last_job(t) - 1)
                if t + 2 < TILES:
                    hidden(t + 2)

        @block.scalar
        def _(act):
            act.dma_start(tokw_sb[:], tok_w).then_inc(tokw_in, 16)
            act.dma_start(q_sb[:], sparsity.partition_broadcast(P)).then_inc(q_in, 16)
            act.dma_start(w2f_sb[:], w2_t).then_inc(flat_in[1], 16)
            act.dma_start(ri_sb[:], rows_ident).then_inc(consts_in, 16)
            act.dma_start(temp_sb[:], temp).then_inc(attn_in, 16)
            act.dma_start(hcols_sb[:], head_cols).then_inc(attn_in, 16)

            def signs_of(r):
                act.wait_ge(cand_ready, cands(r))
                if r == 0:
                    act.wait_ge(halves_ready, 2)
                keys = hi16 if r < HI_ROUNDS else lo16
                with nc.allow_low_precision(reason="whole numbers up to WCOLS are exact in float16"):
                    nc.scalar.activation(signs[:], keys[:, 1, :], ACT.Sign, bias=cand[:, 1:2], scale=-1.0,
                                         accum_out=part[:, 1:2])

            def copy_part(r, cols=1):
                act.wait_ge(part_done, r + 1)
                nc.scalar.copy(part[:, 0:cols], cnt_part[:, 0:cols]).then_inc(part_copied, 1)

            def copy_hT(f):
                act.wait_ge(hn_turned, f + 1)
                src = turn_bank(f)[0:HALF, 0:2 * P].rearrange("p (k n) -> p k n", k=2)
                if f == 0:
                    nc.scalar.copy(hT_all[:, :, P:P + 1], src[:, :, 0:1]).then_inc(hT_ready, 1)
                else:
                    at = (f - 1) * P + (f > 1)
                    nc.scalar.copy(hT_all[:, :, at:at + P], src).then_inc(hT_ready, 1)

            def w_parts(t):
                if t == 0:
                    for b in range(IPT):
                        src = ps_w[:, :, 0:3 * (P + 1)].rearrange("p k (c n) -> p k c n", n=P + 1)
                        yield (src[:, :, :, b * PATCHES:(b + 1) * PATCHES],
                               lambda buf, b=b: buf[:, 0].rearrange("p k (c b) n -> p k c b n", b=IPT)
                               [:, :, :, b, 0:PATCHES])
                else:
                    yield (ps_w[:, :, 0:3 * P].rearrange("p k (j n) -> p k j n", n=PATCHES),
                           lambda buf: buf[:, t % 2, :, :, 0:PATCHES])

            def square_w(t):
                act.wait_ge(w_done, t + 1)
                if t >= 2:
                    act.wait_ge(logits_done, t - 1)
                for src, at in w_parts(t):
                    last = nc.scalar.activation(at(wsq), src, ACT.Square)
                last.then_inc(wsq_ready, 1)

            def copy_w(t):
                if t >= 2:
                    act.wait_ge(wwp_ready, t - 1)
                for src, at in w_parts(t):
                    last = nc.scalar.copy(at(w_s), src)
                last.then_inc(w_copied, 1)

            def scale_logits(t):
                act.wait_ge(logits_done, t + 1)
                nc.scalar.activation(lg[:, :, :].rearrange("h b n -> h (b n)"), ps_l[:, 0:2 * SEQ],
                                     ACT.Copy, scale=temp_sb[:]).then_inc(lg_ready, 1)

            def exps(t):
                act.wait_ge(nmx_ready, t + 1)
                for b in range(IPT):
                    nc.scalar.activation(ex[:, b, :], lg[:, b, :], ACT.Exp, bias=nmx[:, b:b + 1],
                                         accum_out=sm[:, b:b + 1]).then_inc(exp_done, 1)

            def scale_pi(t):
                act.wait_ge(rsm_ready, t + 1)
                if t >= 1:
                    act.wait_ge(spread_done, t)
                for b in range(IPT):
                    nc.scalar.activation(pi[:, b, 0:SEQ], ex[:, b, :], ACT.Copy, scale=rsm[:, b:b + 1],
                                         accum_out=sp[:, 0, b:b + 1]).then_inc(pi_scaled, 1)

            def gelu(t):
                n = width(t)
                act.wait_ge(hid_done, t + 1)
                if t >= 2:
                    act.wait_ge(ffn_done, last_job(t - 2))
                src = hidden_bank(t)[:, :, 0:3 * n].rearrange("p k (c n) -> p k c n", n=n)
                dst = gl[:, t % 2, :, 0:n].rearrange("p (k c) n -> p k c n", k=2)
                nc.scalar.activation(dst, src, ACT.Gelu_apprx_tanh).then_inc(gl_ready, 1)
                act.wait_ge(gl_ready, t + 1)
                if t >= 2:
                    act.wait_ge(gsum_ready, t - 1)
                nc.scalar.activation(glsq[:, t % 2, :, 0:n], gl[:, t % 2, :, 0:n], ACT.Square).then_inc(glsq_ready, 1)

            for r in range(EARLY):
                signs_of(r)
                copy_part(r)
            for t in range(TILES):
                r = EARLY + t
                copy_hT(t)
                signs_of(r)
                copy_part(r)
            copy_hT(TILES)
            act.wait_ge(w_done, 1)
            nc.scalar.copy(wcls[:], ps_w[:, :, 0:3 * (P + 1)].rearrange("p k (c n) -> p k c n", n=P + 1)[:, :, :, P])\
                .then_inc(wcls_copied, 1)

            for s in range(-1, TILES):
                rr = rounds_of.get(s, [])
                if s >= 0:
                    exps(s)
                    scale_pi(s)
                if rr:
                    signs_of(rr[0])
                if s < TILES - 1:
                    square_w(s + 1)
                    copy_w(s + 1)
                if rr:
                    copy_part(rr[0])
                    signs_of(rr[1])
                    copy_part(rr[1])
                if s == 0:
                    for m in range(2):
                        nc.scalar.activation(absw[:, m, :], flat[m], ACT.Abs, accum_out=asum[:, m:m + 1])\
                            .then_inc(abs_done, 1)
                if s < TILES - 1:
                    scale_logits(s + 1)
                if rr:
                    signs_of(rr[2])
                    copy_part(rr[2])
                if s == len(ATTN_PLAN) - 1:
                    copy_part(ROUNDS, 2)
            for t in range(TILES):
                gelu(t)

        @block.gpsimd
        def _(pool):
            def rstd_front(f):
                i = f % 2
                n = BATCH if f == 0 else P
                pool.wait_ge(st0_step, 2 * f + 2)
                if f >= 2:
                    pool.wait_ge(hn_ready, f - 1)
                nc.gpsimd.tensor_scalar(rs0[0:n, i, 0:1], mv0[0:n, i, 1:2], EPS, None, ALU.add).then_inc(rs0_step, 1)
                pool.wait_ge(rs0_step, 2 * f + 1)
                nc.gpsimd.tensor_tensor(rs0[0:n, i, 1:2], rs0[0:n, i, 0:1], neg_half[0:n, :], ALU.pow)\
                    .then_inc(rs0_step, 1)

            def add_bias(f):
                pool.wait_ge(hn_ready, f + 1)
                if f == 0:
                    nc.gpsimd.tensor_tensor(h0c[:], h0c[:], bout_sb[0:BATCH, :], ALU.add).then_inc(bias_in_h0, 1)
                else:
                    nc.gpsimd.tensor_tensor(h0[:, f - 1, :], h0[:, f - 1, :], bout_sb, ALU.add)\
                        .then_inc(bias_in_h0, 1)

            def spread_cls():
                pool.wait_ge(wcls_copied, 1)
                for i in range(2):
                    for b in range(IPT):
                        nc.gpsimd.tensor_copy(
                            w_s[:, i, :, :, PATCHES].rearrange("p k (c b) -> p k c b", b=IPT)[:, :, :, b], wcls[:])\
                            .then_inc(wcls_spread, 1)
                        nc.gpsimd.tensor_tensor(
                            wsq[:, i, :, :, PATCHES].rearrange("p k (c b) -> p k c b", b=IPT)[:, :, :, b],
                            wcls[:], wcls[:], ALU.mult).then_inc(wcls_spread, 1)

            def squares(t):
                pool.wait_ge(wp_ready, t + 1)
                if t >= 1:
                    pool.wait_ge(att_step, 4 * (t - 1) + 1)
                nc.gpsimd.tensor_tensor(wwp[:], w_s[:, t % 2], wp[:, t % 2], ALU.mult).then_inc(wwp_ready, 1)

            def rstd_mid(t):
                n = BATCH if t == CLS else P
                pool.wait_ge(st1_step, 2 * t + 2)
                nc.gpsimd.tensor_scalar(rs1[0:n, t, 0:1], mv1[0:n, t, 1:2], 1.0 + EPS, EPS * EPS, ALU.mult, ALU.add)\
                    .then_inc(rs1_step, 1)
                pool.wait_ge(rs1_step, 2 * t + 1)
                nc.gpsimd.tensor_tensor(rs1[0:n, t, 1:2], rs1[0:n, t, 0:1], neg_half[0:n, :], ALU.pow)\
                    .then_inc(rs1_step, 1)

            def moments(i):
                n = job(i)[3]
                b = i % 2
                pool.wait_ge(mom_ready, i + 1)
                if i >= 2:
                    pool.wait_ge(fin_step, 2 * (i - 1))
                nc.gpsimd.tensor_tensor(ms[0:n, b, 0:1], mom[0:n, b, 0:1], mom[0:n, b, 0:1], ALU.mult)\
                    .then_inc(ms_step, 1)
                pool.wait_ge(ms_step, 5 * i + 1)
                nc.gpsimd.tensor_tensor(ms[0:n, b, 1:2], mom[0:n, b, 1:2], ms[0:n, b, 0:1], ALU.subtract)\
                    .then_inc(ms_step, 1)
                pool.wait_ge(ms_step, 5 * i + 2)
                nc.gpsimd.tensor_scalar(ms[0:n, b, 0:1], ms[0:n, b, 1:2], 0.0, EPS, ALU.max, ALU.add)\
                    .then_inc(ms_step, 1)
                pool.wait_ge(ms_step, 5 * i + 3)
                nc.gpsimd.tensor_tensor(ms[0:n, b, 2:3], ms[0:n, b, 0:1], neg_half[0:n, :], ALU.pow)\
                    .then_inc(ms_step, 1)
                pool.wait_ge(ms_step, 5 * i + 4)
                nc.gpsimd.tensor_tensor(ms[0:n, b, 3:4], mom[0:n, b, 0:1], ms[0:n, b, 2:3], ALU.mult)\
                    .then_inc(ms_step, 1)

            def add_crow(i):
                _, _, _, n, h = job(i)
                pool.wait_ge(rows_ready, 2)
                if i == CLS_WITH + 1:
                    pool.wait_ge(ync_ready, 1)
                else:
                    pool.wait_ge(yn_ready, i + 1 if i <= CLS_WITH else i)
                nc.gpsimd.tensor_tensor(h, h, crow[0:n, :], ALU.add).then_inc(crow_in_h1, 1)

            nc.gpsimd.memset(neg_half[:], -0.5).then_inc(memsets, 1)
            nc.gpsimd.memset(w2g[:, :, D:D + 1], 1.0).then_inc(memsets, 1)
            pool.wait_ge(memsets, 3)
            pool.wait_ge(row_in, 32)
            rstd_front(0)
            add_bias(0)
            for t in range(TILES):
                rstd_front(t + 1)
                add_bias(t + 1)
            spread_cls()
            for t in range(TILES):
                squares(t)
                if t >= 1:
                    rstd_mid(t - 1)
                if t == len(ATTN_PLAN) - 1:
                    pool.wait_ge(next_ready, 1)
                    nc.gpsimd.partition_all_reduce(sel[:, 2, :], sel[:, 1, :], P, bass.bass_isa.ReduceOp.max)\
                        .then_inc(next_all, 1)
            pool.wait_ge(tern_step, 5)
            nc.gpsimd.tensor_tensor(w2q[:], w2q[:], w2neg[:], ALU.subtract).then_inc(w2_sub, 1)
            rstd_mid(TILES - 1)
            rstd_mid(CLS)
            for i in range(NJ):
                add_crow(i)
                moments(i)

        @block.vector
        def _(dve):
            nc.vector.memset(ones[:], 1.0).then_inc(ones_set, 1)
            nc.vector.memset(ones_bf[:], 1.0).then_inc(ones_set, 1)
            nc.vector.memset(twos_bf[:], 2.0).then_inc(ones_set, 1)
            nc.vector.memset(half_n[:, 0:1], 0.0)
            nc.vector.memset(half_n[:, 1:2], float(WCOLS)).then_inc(ones_set, 1)
            nc.vector.memset(yT[HALF:HALF + 1, :, 1, :], 1.0).then_inc(memsets, 1)
            nc.vector.memset(stepc[:], 2.0 ** (HI_ROUNDS - 1)).then_inc(step_halved, 1)
            nc.vector.memset(cand_off[:, 0:1], 0.5)
            nc.vector.memset(cand_off[:, 1:2], 0.0)

            def first_cands(rounds):
                nc.vector.memset(cand[:, 0:1], 2.0 ** (rounds - 1))
                nc.vector.memset(cand[:, 1:2], 2.0 ** (rounds - 1) - 0.5).then_inc(cand_ready, 1)

            first_cands(HI_ROUNDS)

            for m in range(2):
                dve.wait_ge(flat_in[m], 16)
                v = flat[m].bitcast(U16).rearrange("p (n e) -> p n e", e=2)
                nc.vector.tensor_scalar(hi16[:, m, :], v[:, :, 1], 0x7FFF, None, ALU.bitwise_and)\
                    .then_inc(halves_ready, 1)

            def masks(r):
                dve.wait_ge(cand_ready, cands(r))
                keys = hi16 if r < HI_ROUNDS else lo16
                if r == 0:
                    dve.wait_ge(halves_ready, 2)
                nc.vector.tensor_scalar(cmask[:, 0, :], keys[:, 0, :], cand[:, 0:1], None, ALU.is_lt)\
                    .then_inc(mask_ready, 1)

            def update(r):
                dve.wait_ge(count_done, r + 1)
                nc.vector.tensor_scalar(turn[:], cnt_all, col(8), 0.5, ALU.is_le, ALU.subtract)\
                    .then_inc(turn_step, 1)
                dve.wait_ge(turn_step, r + 1)
                dve.wait_ge(step_halved, r + 1)
                nc.vector.scalar_tensor_tensor(cand[:], turn[:], stepc[:], cand[:], ALU.mult, ALU.add)\
                    .then_inc(cand_ready, 1)
                dve.wait_ge(cand_ready, cands(r) + 1)

            def halve(r):
                if r != HI_ROUNDS - 1:
                    nc.vector.tensor_scalar(stepc[:], stepc[:], 0.5, None, ALU.mult).then_inc(step_halved, 1)

            def low_keys():
                nc.vector.tensor_tensor(hi_f[:], cand[:], cand_off[:], ALU.subtract).then_inc(low_step, 1)
                dve.wait_ge(low_step, 1)
                for m in range(2):
                    nc.vector.tensor_scalar(wide[:, m, :], hi16[:, m, :], hi_f[:, m:m + 1], 65536.0,
                                            ALU.subtract, ALU.mult).then_inc(low_step, 1)
                for m in range(2):
                    v = flat[m].bitcast(U16).rearrange("p (n e) -> p n e", e=2)
                    dve.wait_ge(low_step, 2 + m)
                    nc.vector.tensor_tensor(wide[:, m, :], wide[:, m, :], v[:, :, 0], ALU.add).then_inc(low_step, 1)
                for m in range(2):
                    dve.wait_ge(low_step, 4 + m)
                    nc.vector.tensor_scalar(lo16[:, m, :], wide[:, m, :], 0.0, 65535.0, ALU.max, ALU.min)\
                        .then_inc(low_step, 1)
                nc.vector.memset(stepc[:], 2.0 ** (LO_ROUNDS - 1)).then_inc(step_halved, 1)
                dve.wait_ge(low_step, 7)
                first_cands(LO_ROUNDS)

            def next_round(r):
                update(r)
                if r == HI_ROUNDS - 1:
                    low_keys()
                if r + 1 < ROUNDS:
                    masks(r + 1)
                halve(r)

            masks(0)
            dve.wait_ge(q_in, 16)
            steps = [0]

            def q_op(ins):
                steps[0] += 1
                ins.then_inc(q_step, 1)
                dve.wait_ge(q_step, steps[0])

            def col(i):
                return qs[:, i:i + 1]

            q_op(nc.vector.tensor_scalar(col(0), q_sb[:], float(N_W - 1), None, ALU.mult))
            q_op(nc.vector.tensor_scalar(col(1), col(0), ROUND_MAGIC, None, ALU.add))
            q_op(nc.vector.tensor_scalar(col(1), col(1), ROUND_MAGIC, None, ALU.subtract))
            q_op(nc.vector.tensor_tensor(col(2), col(1), col(0), ALU.is_gt))
            q_op(nc.vector.tensor_tensor(col(2), col(1), col(2), ALU.subtract))
            q_op(nc.vector.tensor_scalar(col(4), col(2), 0.0, float(N_W - 1), ALU.max, ALU.min))
            q_op(nc.vector.tensor_scalar(col(8), col(4), 2.0, None, ALU.mult))
            q_op(nc.vector.tensor_tensor(col(3), col(0), col(2), ALU.subtract))
            q_op(nc.vector.tensor_scalar(col(6), col(3), -1.0, 1.0, ALU.mult, ALU.add))
            q_op(nc.vector.tensor_scalar(col(7), col(3), 0.0, None, ALU.is_gt))
            q_op(nc.vector.tensor_tensor(col(7), col(2), col(7), ALU.add))
            q_op(nc.vector.tensor_scalar(col(5), col(7), 0.0, float(N_W - 1), ALU.max, ALU.min))

            def stats_front(f):
                n = BATCH if f == 0 else P
                i = f % 2
                src = h0c[:] if f == 0 else h0[:, f - 1, :]
                dst = st0[0:n, i, :]
                if f >= 1:
                    dve.wait_ge(h0_ready, f)
                nc.vector.bn_stats(dst, src).then_inc(st0_step, 1)
                dve.wait_ge(st0_step, 2 * f + 1)
                nc.vector.bn_aggr(mv0[0:n, i, :], dst).then_inc(st0_step, 1)

            def take_tok(t):
                dve.wait_ge(tok_done, t + 1)
                src = (ps_l if t % 2 == 0 else ps_o)[:, 0:D]
                nc.vector.tensor_tensor(h0[:, t, :], src, tokb_sb, ALU.add).then_inc(h0_ready, 1)

            def norm_front(f):
                n = BATCH if f == 0 else P
                i = f % 2
                src = h0c[:] if f == 0 else h0[:, f - 1, :]
                dve.wait_ge(rs0_step, 2 * f + 2)
                if f >= 2:
                    dve.wait_ge(hn_turned, f - 1)
                nc.vector.tensor_scalar(hn[0:n, i, :], src, mv0[0:n, i, 0:1], rs0[0:n, i, 1:2],
                                        ALU.subtract, ALU.mult).then_inc(hn_ready, 1)

            def norms(t):
                dve.wait_ge(wsq_ready, t + 1)
                if t == 0:
                    dve.wait_ge(wcls_spread, 4 * IPT)
                nc.vector.tensor_reduce(n2[:], wsq[:, t % 2].rearrange("p k j n -> p (k j) n"), AX.X, ALU.add)\
                    .then_inc(norm_step, 1)
                dve.wait_ge(norm_step, 3 * t + 1)
                nc.vector.tensor_scalar(inv[:, 0, :], n2[:], 1e-24, None, ALU.max).then_inc(norm_step, 1)
                dve.wait_ge(norm_step, 3 * t + 2)
                nc.vector.reciprocal(inv[:, 1, :], inv[:, 0, :]).then_inc(norm_step, 1)
                dve.wait_ge(norm_step, 3 * t + 3)
                if t >= 1:
                    dve.wait_ge(logits_done, t)
                nc.vector.tensor_tensor(invm[:, :, :].rearrange("p (c b) h -> p c b h", b=IPT),
                                        hcols_sb[:, :, :].unsqueeze(2).to_broadcast([P, C, IPT, 32]),
                                        inv[:, 1, :].rearrange("p (c b) -> p c b", b=IPT).unsqueeze(3)
                                        .to_broadcast([P, C, IPT, 32]), ALU.mult).then_inc(invm_ready, 1)

            def row_max(t):
                dve.wait_ge(lg_ready, t + 1)
                nc.vector.tensor_reduce(nmx[:], lg[:], AX.X, ALU.max, negate=True).then_inc(nmx_ready, 1)

            def soft_scale(t):
                dve.wait_ge(exp_done, 2 * (t + 1))
                nc.vector.reciprocal(rsm[:], sm[:]).then_inc(rsm_ready, 1)

            def soft_norm(t):
                dve.wait_ge(pi_scaled, 2 * (t + 1))
                nc.vector.tensor_scalar(sp[:, 1, :], sp[:, 0, :], 1e-8, None, ALU.add).then_inc(sp_ready, 1)
                dve.wait_ge(sp_ready, t + 1)
                nc.vector.reciprocal(pi[:, :, SEQ], sp[:, 1, :]).then_inc(pi_ready, 1)

            def spread_view():
                return ps_b[:, :, 0:6 * (SEQ + 1)].rearrange("p k (j n) -> p k j n", n=SEQ + 1)

            def weigh(t):
                dve.wait_ge(spread_done, t + 1)
                dve.wait_ge(w_copied, t + 1)
                if t >= 2:
                    dve.wait_ge(ocls_ready, t - 1)
                    dve.wait_ge(wwp_ready, t - 1)
                nc.vector.tensor_tensor(wp[:, t % 2], w_s[:, t % 2], spread_view()[:, :, :, 0:SEQ], ALU.mult)\
                    .then_inc(wp_ready, 1)

            def attend(t):
                dve.wait_ge(wwp_ready, t + 1)
                nc.vector.tensor_reduce(ds[:], wwp[:, :, :, :].rearrange("p k j n -> p (k j) n"), AX.X, ALU.add)\
                    .then_inc(att_step, 1)
                dve.wait_ge(att_step, 4 * t + 1)
                nc.vector.tensor_tensor(att[:, 0, :].rearrange("p (k j) -> p k j", k=2),
                                        ds[:].rearrange("p (k j) -> p k j", k=2),
                                        spread_view()[:, :, :, SEQ], ALU.mult).then_inc(att_step, 1)
                dve.wait_ge(att_step, 4 * t + 2)
                nc.vector.tensor_scalar(att[:, 1, :], att[:, 0, :], -1.0, -1.0, ALU.mult, ALU.add).then_inc(att_step, 1)
                dve.wait_ge(att_step, 4 * t + 3)
                nc.vector.reciprocal(att[:, 2, :], att[:, 1, :]).then_inc(att_step, 1)
                dve.wait_ge(att_step, 4 * t + 4)
                dve.wait_ge(wp_ready, t + 1)
                if t >= 2:
                    dve.wait_ge(out_done, t - 1)
                src = wp[:, t % 2].rearrange("p k j n -> p (k j) n")
                dst = oT[:, t % 2, :, :].rearrange("p c (b n) -> p (c b) n", b=IPT)
                nc.vector.tensor_tensor(dst, src[:, :, 0:PATCHES],
                                        att[:, 2, :].unsqueeze(2).to_broadcast([P, 12, PATCHES]), ALU.mult)\
                    .then_inc(oT_ready, 1)
                nc.vector.tensor_tensor(ocls[:, :, IPT * t:IPT * (t + 1)],
                                        src[:, :, PATCHES].rearrange("p (c b) -> p c b", b=IPT),
                                        att[:, 2, :].rearrange("p (c b) -> p c b", b=IPT), ALU.mult)\
                    .then_inc(ocls_ready, 1)

            def take_out(t):
                n = P if t < TILES else BATCH
                dst = h1[:, t, :] if t < TILES else h1c[:]
                src = h0[:, t, :] if t < TILES else h0c[:]
                dve.wait_ge(out_done, t + 1)
                dve.wait_ge(bias_in_h0, min(t + 2, TILES + 1))
                nc.vector.tensor_tensor(dst, ps_o[0:n, 0:D], src, ALU.add).then_inc(h1_ready, 1)
                dve.wait_ge(h1_ready, t + 1)
                nc.vector.bn_stats(st1[0:n, t % 2, :], dst).then_inc(st1_step, 1)
                dve.wait_ge(st1_step, 2 * t + 1)
                nc.vector.bn_aggr(mv1[0:n, t, :], st1[0:n, t % 2, :]).then_inc(st1_step, 1)

            done = [0]
            s_lo = bits[:, 3, :].bitcast(F32)

            def sel_op(ins):
                done[0] += 1
                ins.then_inc(sel_step2, 1)
                dve.wait_ge(sel_step2, done[0])

            def lower_statistic():
                dve.wait_ge(cand_ready, ROUNDS + 2)
                sel_op(nc.vector.tensor_tensor(bits[:, 0, :], cand[:], cand_off[:], ALU.subtract))
                sel_op(nc.vector.tensor_copy(bits[:, 1, :], hi_f[:]))
                sel_op(nc.vector.tensor_scalar(bits[:, 2, :], bits[:, 1, :], 16, None, ALU.logical_shift_left))
                sel_op(nc.vector.tensor_tensor(bits[:, 3, :], bits[:, 2, :], bits[:, 0, :], ALU.bitwise_or))
                dve.wait_ge(abs_done, 2)
                for m in range(2):
                    nc.vector.tensor_scalar(cmask[:, m, :], absw[:, m, :], s_lo[:, m:m + 1], None, ALU.is_le)\
                        .then_inc(mask_ready, 1)

            def next_statistic():
                for m in range(2):
                    sel_op(nc.vector.tensor_scalar(wide[:, m, :], absw[:, m, :], s_lo[:, m:m + 1], BIG,
                                                   ALU.is_le, ALU.mult))
                for m in range(2):
                    nc.vector.tensor_tensor_reduce(out=wide[:, m, :], in0=wide[:, m, :], in1=absw[:, m, :],
                                                   scale=1.0, scalar=BIG, op0=ALU.add, op1=ALU.min,
                                                   accum_out=sel[:, 0, m:m + 1]).then_inc(sel_step2, 1)
                    done[0] += 1
                dve.wait_ge(sel_step2, done[0])
                nc.vector.tensor_scalar(sel[:, 1, :], sel[:, 0, :], -1.0, None, ALU.mult).then_inc(next_ready, 1)

            def thresholds():
                dve.wait_ge(count_done, ROUNDS + 1)
                sel_op(nc.vector.tensor_scalar(sel[:, 5, :], cnt_all, 0.5, None, ALU.mult))
                nc.vector.tensor_scalar(sel[:, 3, :], sel[:, 5, :], col(5), None, ALU.is_gt).then_inc(sel_step, 1)
                dve.wait_ge(sel_step, 1)
                sel_op(nc.vector.tensor_tensor(sel[:, 4, :], sel[:, 3, :], s_lo, ALU.mult))
                sel_op(nc.vector.tensor_scalar(sel[:, 5, :], sel[:, 3, :], 1.0, None, ALU.subtract))
                dve.wait_ge(next_all, 1)
                sel_op(nc.vector.tensor_tensor(sel[:, 6, :], sel[:, 5, :], sel[:, 2, :], ALU.mult))
                sel_op(nc.vector.tensor_tensor(sel[:, 7, :], sel[:, 4, :], sel[:, 6, :], ALU.add))
                sel_op(nc.vector.tensor_scalar(sel[:, 8, :], s_lo, col(6), None, ALU.mult))
                sel_op(nc.vector.tensor_scalar(sel[:, 9, :], sel[:, 7, :], col(3), None, ALU.mult))
                sel_op(nc.vector.tensor_tensor(sel[:, 10, :], sel[:, 8, :], sel[:, 9, :], ALU.add))
                sel_op(nc.vector.tensor_scalar(sel[:, 11, :], sel[:, 10, :], -1.0, None, ALU.mult))
                dve.wait_ge(asum_done, 1)
                sel_op(nc.vector.tensor_scalar(w_scale[:], cnt_all, 1.0 / N_W, None, ALU.mult))

            def above(m, n=P):
                return sel[0:n, 10, m:m + 1]

            def below(m, n=P):
                return sel[0:n, 11, m:m + 1]

            def ternary_1():
                dve.wait_ge(ffn_in, 16 * N_FFN)
                nc.vector.tensor_scalar(w1q[0:HALF], w1t_sb[:], above(0, HALF), w_scale[0:HALF, 0:1],
                                        ALU.is_gt, ALU.mult).then_inc(tern_step, 1)
                nc.vector.tensor_scalar(w1neg[:], w1t_sb[:], below(0, HALF), w_scale[0:HALF, 0:1],
                                        ALU.is_lt, ALU.mult).then_inc(tern_step, 1)
                dve.wait_ge(tern_step, 2)
                nc.vector.tensor_tensor(w1q[0:HALF], w1q[0:HALF], w1neg[:], ALU.subtract).then_inc(tern_step, 1)

            def ternary_2():
                nc.vector.tensor_scalar(w2q[:], w2f_sb[:], above(1), w_scale[:, 1:2], ALU.is_gt, ALU.mult)\
                    .then_inc(tern_step, 1)
                nc.vector.tensor_scalar(w2neg[:], w2f_sb[:], below(1), w_scale[:, 1:2], ALU.is_lt, ALU.mult)\
                    .then_inc(tern_step, 1)

            def spread_beta():
                nc.vector.tensor_copy(bet_b[:], ln2gb_sb[:, 1, :].unsqueeze(2).to_broadcast([P, C, P])).then_inc(bet_ready, 1)

            def gamma_w2():
                dve.wait_ge(w2_sub, 1)
                for c in range(C):
                    nc.vector.tensor_scalar(w2g[:, c, 0:D], w2q[:, c, :], ln2gb_sb[:, 0, c:c + 1], None, ALU.mult)\
                        .then_inc(w2g_ready, 1)

            def common_rows():
                dve.wait_ge(rows_done, 1)
                nc.vector.tensor_tensor(crow[:], ps_t[:, 0:D], b2_sb, ALU.add).then_inc(rows_ready, 1)
                nc.vector.tensor_scalar(cg[:], ps_t[:, D:2 * D], -1.0, None, ALU.mult).then_inc(rows_ready, 1)

            def norm_mid(t):
                src, dst, n = (h1c[:], ync[:], BATCH) if t == CLS else (h1[:, t, :], yn[:, t % 2, :], P)
                dve.wait_ge(rs1_step, 2 * t + 2)
                if 2 <= t < TILES:
                    dve.wait_ge(yn_turned, t - 1)
                nc.vector.tensor_scalar(dst, src, mv1[0:n, t, 0:1], rs1[0:n, t, 1:2], ALU.subtract, ALU.mult)\
                    .then_inc(ync_ready if t == CLS else yn_ready, 1)

            def take_yT(t):
                n = width(t)
                dve.wait_ge(yn_turned, t + 1)
                if t >= 2:
                    dve.wait_ge(hid_done, t - 1)
                for k in range(2):
                    nc.vector.tensor_scalar(yT[0:HALF, t % 2, k, 0:n],
                                            ffn_turn_bank(t)[0:HALF, 128 + k * n:128 + (k + 1) * n],
                                            ln1gb_sb[:, 0, k:k + 1], ln1gb_sb[:, 1, k:k + 1], ALU.mult, ALU.add)\
                        .then_inc(yT_ready, 1)

            def sum_squares(t):
                n = width(t)
                dve.wait_ge(glsq_ready, t + 1)
                if t >= 2:
                    dve.wait_ge(ffn_done, last_job(t - 2))
                nc.vector.tensor_reduce(gsum[:, t % 2, 0:n], glsq[:, t % 2, :, 0:n].rearrange("p c n -> p n c"),
                                        AX.X, ALU.add).then_inc(gsum_ready, 1)

            def take_moments(i):
                n = job(i)[3]
                dve.wait_ge(ffn_done, i + 1)
                if i >= 2:
                    dve.wait_ge(ms_step, 5 * (i - 1))
                nc.vector.tensor_scalar(mom[0:n, i % 2, :], contract_bank(i)[0:n, D:D + 2], 1.0 / HID, None, ALU.mult)\
                    .then_inc(mom_ready, 1)

            def finish(i):
                _, _, _, n, h = job(i)
                b = i % 2
                dve.wait_ge(ms_step, 5 * (i + 1))
                dve.wait_ge(crow_in_h1, i + 1)
                if i >= 2:
                    dve.wait_ge(stored[b], 16 * stores_before(b, i - 1))
                nc.vector.scalar_tensor_tensor(fin[0:n, b, :], cg[0:n, :], ms[0:n, b, 3:4], h, ALU.mult, ALU.add)\
                    .then_inc(fin_step, 1)
                dve.wait_ge(fin_step, 2 * i + 1)
                nc.vector.scalar_tensor_tensor(fin[0:n, b, :], contract_bank(i)[0:n, 0:D], ms[0:n, b, 2:3],
                                               fin[0:n, b, :], ALU.mult, ALU.add).then_inc(fin_step, 1)

            dve.wait_ge(row_in, 32)
            stats_front(0)
            for r in range(EARLY):
                next_round(r)
            norm_front(0)
            for t in range(TILES):
                take_tok(t)
                stats_front(t + 1)
                next_round(EARLY + t)
                norm_front(t + 1)

            for s in range(-1, TILES):
                rr = rounds_of.get(s, [])
                before = rounds_of.get(s - 1, [])
                if before:
                    next_round(before[-1])
                if s >= 0:
                    soft_scale(s)
                if s >= 1:
                    attend(s - 1)
                if s >= 0:
                    soft_norm(s)
                if s < TILES - 1:
                    norms(s + 1)
                if rr:
                    next_round(rr[0])
                if s >= 0:
                    weigh(s)
                if s == len(ATTN_PLAN) - 1:
                    lower_statistic()
                    next_statistic()
                if rr:
                    next_round(rr[1])
                if s >= 1:
                    take_out(s - 1)
                if s == len(ATTN_PLAN) - 1:
                    thresholds()
                    ternary_1()
                if s < TILES - 1:
                    row_max(s + 1)
            norm_mid(0)
            dve.wait_ge(memsets, 3)
            take_yT(0)
            ternary_2()
            attend(TILES - 1)
            norm_mid(1)
            take_yT(1)
            spread_beta()
            take_out(TILES - 1)
            gamma_w2()
            norm_mid(2)
            take_out(CLS)
            norm_mid(CLS)
            common_rows()
            take_yT(2)
            sum_squares(0)
            i = 0
            for t in range(TILES):
                take_moments(last_job(t) - 1 - (t == CLS_WITH))
                if t + 3 < TILES:
                    norm_mid(t + 3)
                finish(last_job(t) - 1 - (t == CLS_WITH))
                if t + 1 < TILES:
                    sum_squares(t + 1)
                if t + 3 < TILES:
                    take_yT(t + 3)
                if t == CLS_WITH:
                    take_moments(last_job(t) - 1)
                    finish(last_job(t) - 1)


def kernel(x, cls_tok, L0_tok_W, L0_tok_b, L0_attn_w_qkv, L0_attn_temp, L0_attn_w_out, L0_attn_b_out, L0_ffn_ln1_g,
           L0_ffn_ln1_b, L0_ffn_W1, L0_ffn_b1, L0_ffn_ln2_g, L0_ffn_ln2_b, L0_ffn_W2, L0_ffn_b2, L0_ffn_sparsity):
    import concourse.bacc as _bacc
    from concourse.bass_utils import run_bass_kernel_spmd as _run

    def chunks(a, rows):
        a = np.asarray(a)
        return a.reshape(a.shape[0] // rows, rows, -1).transpose(1, 0, 2)

    img = np.asarray(x).reshape(BATCH, 8, 16, 8, 16, 3).transpose(2, 4, 5, 0, 1, 3).reshape(C, P, TILES, P)
    head_cols = np.zeros((P, C, 32), np.float32)
    head_rows = np.zeros((P, C, P), np.float32)
    temp = np.zeros((P, 1), np.float32)
    for h in range(HEADS):
        at = slice(h % 2 * PATCHES, (h % 2 + 1) * PATCHES)
        head_cols[at, h // 2, head_row(h) % 32] = 1
        head_rows[head_row(h), h // 2, at] = 1
        temp[head_row(h)] = np.asarray(L0_attn_temp)[h]
    ins = {
        "x_t": img.transpose(2, 1, 0, 3),
        "cls_tok": np.asarray(cls_tok).reshape(D),
        "tok_w": chunks(L0_tok_W, P),
        "rows3": np.stack([np.asarray(a) for a in (L0_tok_b, L0_attn_b_out, L0_ffn_b2)]),
        "w_qkv": chunks(L0_attn_w_qkv, HALF),
        "temp": temp,
        "w_out": chunks(L0_attn_w_out, P),
        "ln1_gb": np.stack([np.asarray(a).reshape(2, HALF).T for a in (L0_ffn_ln1_g, L0_ffn_ln1_b)], axis=1),
        "w1_flat": np.asarray(L0_ffn_W1).reshape(P, WCOLS),
        "w1_t": chunks(np.asarray(L0_ffn_W1).T, HALF),
        "b1": np.asarray(L0_ffn_b1).reshape(1, HID),
        "ln2_gb": np.stack([np.asarray(a).reshape(C, P).T for a in (L0_ffn_ln2_g, L0_ffn_ln2_b)], axis=1),
        "w2_t": chunks(np.asarray(L0_ffn_W2).T, P),
        "sparsity": np.asarray(L0_ffn_sparsity).reshape(1),
        "head_cols": head_cols,
        "rows_ident": np.concatenate([head_rows, np.eye(P, dtype=np.float32)[:, None, :]], axis=1),
    }
    nc = _bacc.Bacc("TRN2", target_bir_lowering=False, num_devices=1)
    arrays, args = {}, {}
    for name, a in ins.items():
        a = np.ascontiguousarray(a)
        arrays[f"in_{name}"] = a
        args[name] = nc.dram_tensor(f"in_{name}", a.shape, mybir.dt.from_np(a.dtype), kind="ExternalInput").ap()
    out = nc.dram_tensor("out_0", (BATCH, SEQ, D), F32, kind="ExternalOutput").ap()
    vit_block(nc, out=out, **args)
    r = _run(nc, [arrays], core_ids=[0])
    return r.results[0]["out_0"]
```

```python
from contextlib import ExitStack

import numpy as np

import concourse.bass as bass
from concourse import mybir
from concourse.alu_op_type import AluOpType as ALU

ACT = mybir.ActivationFunctionType
AX = mybir.AxisListType
F32 = mybir.dt.float32
BF16 = mybir.dt.bfloat16
I32 = mybir.dt.int32
F16 = mybir.dt.float16
U16 = mybir.dt.uint16

P = 128
BATCH = 16
PATCHES = 64
SEQ = PATCHES + 1
D = 192
HALF = D // 2
HID = 768
C = HID // P
HEADS = 12
IPT = P // PATCHES
TILES = BATCH // IPT
EPS = 1e-5
N_W = HID * D
WCOLS = N_W // P
HI_ROUNDS = 15
LO_ROUNDS = 16
ROUNDS = HI_ROUNDS + LO_ROUNDS
FOLD = SEQ // 2
BIG = 3.0e38
LIFT = 2.0 ** 127
ROUND_MAGIC = 1.5 * 2.0 ** 23
MCH = WCOLS // P

ONES_CH = 2
ONES_COLS = ONES_CH * P
EARLY = 2
ATTN_PLAN = [(0, 1, 2, 3), (0, 2, 3), (0, 1, 2, 3), (0, 1, 2, 3), (0, 1, 2, 3), (0, 1)]
assert EARLY + TILES + sum(map(len, ATTN_PLAN)) == ROUNDS and len(ATTN_PLAN) == TILES - 2
LAST_ROUNDS = len(ATTN_PLAN) - 1
PROJECT_0 = 2
CLS_WITH = 4


def head_row(h):
    c = h // 2
    return 32 * (c % 4) + 2 * (c // 4) + h % 2


def vit_block(nc, x_t, cls_tok, tok_w, rows3, w_qkv, temp_cols, w_out, ln1_gb, w1_flat, w1_t, b1,
              ln2_gb, w2_t, sparsity, head_cols, rows_ident, out):
    ctx = ExitStack()
    with ctx:
        def sb(name, shape, dt=F32):
            return ctx.enter_context(nc.sbuf_tensor(name, shape, dt))

        def pb(name, shape, dt=F32):
            return ctx.enter_context(nc.psum_tensor(name, shape, dt))

        def sem(name):
            return ctx.enter_context(nc.semaphore(name))

        x_sb = sb("x_sb", [P, TILES, C, P])
        tokw_sb = sb("tokw_sb", [P, C, D])
        rows3_sb = sb("rows3_sb", [P, 3, D])
        tokb_sb, bout_sb, b2_sb = (rows3_sb[:, i, :] for i in range(3))
        wqkv_sb = sb("wqkv_sb", [HALF, 2, HID])
        wout_sb = sb("wout_sb", [P, C, D])
        temp_rows_sb = sb("temp_rows_sb", [P, C, 32])
        ln1gb_sb = sb("ln1gb_sb", [HALF, 2, 2])
        ln2gb_sb = sb("ln2gb_sb", [P, 2, C])
        hcols_sb = sb("hcols_sb", [P, C, 32])
        tcols = sb("tcols", [P, C, 32])
        ri_sb = sb("ri_sb", [P, C + 1, P])
        hrows_sb = ri_sb[:, 0:C, :]
        ident = ri_sb[:, C, :]
        ones = sb("ones", [P, P])
        ones_bf = sb("ones_bf", [P, P], BF16)
        twos_bf = sb("twos_bf", [P, 2], BF16)
        half_n = sb("half_n", [P, 2], BF16)
        neg_half = sb("neg_half", [P, 1])

        h0 = sb("h0", [P, TILES, D])
        h0c = sb("h0c", [BATCH, D])
        hn = sb("hn", [P, 2, D])
        hT_all = sb("hT_all", [HALF, 2, TILES * P + 1])
        st0 = sb("st0", [P, 2, 6])
        mv0 = sb("mv0", [P, 2, 2])
        rs0 = sb("rs0", [P, 2, 2])

        w_s = sb("w_s", [P, 2, 2, 6, SEQ])
        wsq = sb("wsq", [P, 2, 2, 6, SEQ])
        wcls = sb("wcls", [P, 2, 3])
        n2 = sb("n2", [P, 12])
        inv = sb("inv", [P, 2, 12])
        invm = sb("invm", [P, 12, 32])
        nmx = sb("nmx", [P, 2])
        ex = sb("ex", [P, 2, SEQ])
        sm = sb("sm", [P, 2])
        rsm = sb("rsm", [P, 2])
        pi = sb("pi", [P, 2, SEQ + 1])
        sp = sb("sp", [P, 2, 2])
        wp = sb("wp", [P, 2, 2, 6, SEQ])
        wwp = sb("wwp", [P, 2, 6, SEQ])
        ds = sb("ds", [P, 12])
        inv_sum = sb("inv_sum", [P, 12])
        att = sb("att", [P, 3, 12])
        oT = sb("oT", [P, 2, C, P])
        ocls = sb("ocls", [P, C, BATCH])

        h1 = sb("h1", [P, TILES, D])
        h1c = sb("h1c", [BATCH, D])
        yn = sb("yn", [P, 2, D])
        ync = sb("ync", [BATCH, D])
        st1 = sb("st1", [P, 2, 6])
        mv1 = sb("mv1", [P, TILES + 1, 2])
        rs1 = sb("rs1", [P, TILES + 1, 2])
        yT = sb("yT", [HALF, 2, 2, P + BATCH])
        y_parts = sb("y_parts", [HALF + 3, 2, 3, 2, P + BATCH], BF16)
        y_rest = sb("y_rest", [HALF, 2, P + BATCH])
        y0_rest = sb("y0_rest", [HALF, 2, P])
        w1q = sb("w1q", [HALF + 3, 2, HID], BF16)
        w1t_sb = sb("w1t_sb", [HALF, 2, HID])
        w1neg = sb("w1neg", [HALF, 2, HID], BF16)
        gb1_s = sb("gb1_s", [HALF, 2, 2])
        gb2_s = sb("gb2_s", [P, 2, C])
        w2_work = sb("w2_work", [P, 2, WCOLS])
        hi_value = w2_work[:, :, :]
        w2q, w2neg = (w2_work[:, i, :].rearrange("p (c n) -> p c n", n=D) for i in range(2))
        w2g = sb("w2g", [P, C, D + 1])
        bet_b = sb("bet_b", [P, C, P])
        cg = sb("cg", [P, D])
        crow = sb("crow", [P, D])
        gl = sb("gl", [P, 2, C, P + BATCH])
        glsq = sb("glsq", [P, 2, C, P + BATCH])
        b1_rest = glsq[0:1, :, :, :].rearrange("p i c n -> p (i c n)")[:, 0:HID]
        b1_parts = gl[0:1, :, :, :].rearrange("p i c n -> p (i c n)").bitcast(BF16)[:, 0:3 * HID]\
            .rearrange("p (j n) -> p j n", n=HID)
        gsum = sb("gsum", [P, 2, P + BATCH])
        mom = sb("mom", [P, 2, 2])
        ms = sb("ms", [P, 2, 4])
        fin = sb("fin", [P, 2, D])

        w1f_sb = sb("w1f_sb", [P, WCOLS])
        w2f_sb = sb("w2f_sb", [P, C, D])
        w2f = w2f_sb[:, :, :].rearrange("p c n -> p (c n)")
        flat = [w1f_sb[:, :], w2f]
        absw = sb("absw", [P, 2, WCOLS])
        hi16 = sb("hi16", [P, 2, WCOLS], U16)
        lo16 = sb("lo16", [P, 2, WCOLS], U16)
        wide = sb("wide", [P, 2, WCOLS])
        cmask = sb("cmask", [P, 2, WCOLS], BF16)
        asum = sb("asum", [P, 2])
        part = sb("part", [P, 4], F16)
        signs = sb("signs", [P, WCOLS - ONES_COLS], BF16)
        cand_off = sb("cand_off", [P, 2])
        cand = sb("cand", [P, 2])
        base = sb("base", [P, 2, 2])
        rise = sb("rise", [P, 2])
        q_sb = sb("q_sb", [P, 1])
        qs = sb("qs", [P, 12])
        hi_f = sb("hi_f", [P, 2])
        hi_top = sb("hi_top", [P, 2])
        bits = sb("bits", [P, 4, 2], I32)
        sel = sb("sel", [P, 12, 2])
        w_scale = sb("w_scale", [P, 2])

        ps_w = pb("ps_w", [P, 2, 512])
        ps_b = pb("ps_b", [P, 2, 512])
        ps_l = pb("ps_l", [P, 512])
        ps_o = pb("ps_o", [P, 512])
        ps_t = pb("ps_t", [P, 512])
        ps_c = pb("ps_c", [P, 512])
        cnt_part = ps_c[:, 0:2]
        cnt_all = ps_c[:, 4:6]
        asum_all = ps_c[:, 8:10]

        x_in = [sem(f"x_in{t}") for t in range(TILES)]
        tokw_in = sem("tokw_in")
        consts_in = sem("consts_in")
        row_in = sem("row_in")
        flat_in = [sem("w1_flat_in"), sem("w2_flat_in")]
        q_in = sem("q_in")
        wqkv_in = sem("wqkv_in")
        attn_in = sem("attn_in")
        b1_in = sem("b1_in")
        ffn_in = sem("ffn_in")
        memsets = sem("memsets")
        ones_set = sem("ones_set")
        tok_done = sem("tok_done")
        h0_ready = sem("h0_ready")
        st0_step = sem("st0_step")
        rs0_step = sem("rs0_step")
        hn_ready = sem("hn_ready")
        hn_turned = sem("hn_turned")
        hT_ready = sem("hT_ready")
        bias_in_h0 = sem("bias_in_h0")
        wcls_copied = sem("wcls_copied")
        wcls_spread = sem("wcls_spread")
        w_done = sem("w_done")
        w_copied = sem("w_copied")
        wsq_ready = sem("wsq_ready")
        norm_step = sem("norm_step")
        invm_ready = sem("invm_ready")
        logits_done = sem("logits_done")
        tcols_ready = sem("tcols_ready")
        nmx_ready = sem("nmx_ready")
        rsm_ready = sem("rsm_ready")
        pi_scaled = sem("pi_scaled")
        sp_ready = sem("sp_ready")
        exp_done = sem("exp_done")
        pi_ready = sem("pi_ready")
        spread_done = sem("spread_done")
        wp_ready = sem("wp_ready")
        wwp_ready = sem("wwp_ready")
        inv_sum_ready = sem("inv_sum_ready")
        att_step = sem("att_step")
        wwp_folded = sem("wwp_folded")
        ds_ready = sem("ds_ready")
        att_ready = sem("att_ready")
        oT_ready = sem("oT_ready")
        ocls_ready = sem("ocls_ready")
        out_done = sem("out_done")
        h1_ready = sem("h1_ready")
        st1_step = sem("st1_step")
        rs1_step = sem("rs1_step")
        yn_ready = sem("yn_ready")
        ync_ready = sem("ync_ready")
        gsum_ready = sem("gsum_ready")
        yn_turned = sem("yn_turned")
        yT_ready = sem("yT_ready")
        y_first = sem("y_first")
        y0_step = sem("y0_step")
        y_step = sem("y_step")
        b1_step = sem("b1_step")
        b1_in_w1q = sem("b1_in_w1q")
        crow_in_h1 = sem("crow_in_h1")
        hid_done = sem("hid_done")
        gl_ready = sem("gl_ready")
        glsq_ready = sem("glsq_ready")
        ffn_done = sem("ffn_done")
        mom_ready = sem("mom_ready")
        ms_step = sem("ms_step")
        fin_step = sem("fin_step")
        stored = [sem("stored_even"), sem("stored_odd")]
        abs_done = sem("abs_done")
        halves_ready = sem("halves_ready")
        q_step = sem("q_step")
        cand_ready = sem("cand_ready")
        mask_ready = sem("mask_ready")
        part_done = sem("part_done")
        part_copied = sem("part_copied")
        count_done = sem("count_done")
        base_ready = sem("base_ready")
        rise_ready = sem("rise_ready")
        hi_value_ready = sem("hi_value_ready")
        low_step = sem("low_step")
        select_step = sem("select_step")
        next_ready = sem("next_ready")
        next_all = sem("next_all")
        tern_step = sem("tern_step")
        scale_ready = sem("scale_ready")
        gb_ready = sem("gb_ready")
        w2g_ready = sem("w2g_ready")
        bet_ready = sem("bet_ready")
        rows_done = sem("rows_done")
        rows_ready = sem("rows_ready")

        N_ATTN = 3
        N_FFN = 3
        CLS = TILES
        JOBS = [(t, 0, P) for t in range(TILES)]
        JOBS.insert(CLS_WITH + 1, (CLS, P, BATCH))
        NJ = len(JOBS)
        starts = [EARLY + TILES + sum(map(len, ATTN_PLAN[:i])) for i in range(len(ATTN_PLAN))]
        rounds_of = {i: {place: starts[i] + k for k, place in enumerate(places)}
                     for i, places in enumerate(ATTN_PLAN)}
        block = ctx.enter_context(nc.Block())

        def job(i):
            t, col, n = JOBS[i]
            return t, CLS_WITH if t == CLS else t, col, n, h1c[:] if t == CLS else h1[:, t, :]

        def last_job(t):
            return t + 2 if t >= CLS_WITH else t + 1

        def width(t):
            return P + BATCH if t == CLS_WITH else P

        def hid_half(i):
            return slice(i * HID // 2, (i + 1) * HID // 2)

        def stores_before(i, j):
            return sum(1 if t == CLS else IPT for t, _, _ in JOBS[i:j:2])

        @block.sync
        def _(sp):
            sp.dma_start(x_sb[:, 0], x_t[0]).then_inc(x_in[0], 16)
            sp.dma_start(flat[0], w1_flat).then_inc(flat_in[0], 16)
            sp.dma_start(x_sb[:, 1], x_t[1]).then_inc(x_in[1], 16)
            sp.dma_start(h0c[:], cls_tok.partition_broadcast(BATCH)).then_inc(row_in, 16)
            sp.dma_start(rows3_sb[:], rows3.partition_broadcast(P)).then_inc(row_in, 16)
            for t in range(2, TILES):
                sp.dma_start(x_sb[:, t], x_t[t]).then_inc(x_in[t], 16)
                if t == 3:
                    sp.dma_start(wqkv_sb[:], w_qkv).then_inc(wqkv_in, 16)
            sp.dma_start(wout_sb[:], w_out).then_inc(attn_in, 16)
            sp.dma_start(w1t_sb[:], w1_t).then_inc(ffn_in, 16)
            sp.dma_start(b1_rest, b1).then_inc(b1_in, 16)
            sp.dma_start(ln1gb_sb[:], ln1_gb).then_inc(ffn_in, 16)
            sp.dma_start(ln2gb_sb[:], ln2_gb).then_inc(ffn_in, 16)
            sp.wait_ge(b1_step, 5)
            for j in range(3):
                sp.dma_start(w1q[HALF + j:HALF + j + 1, 1, :], b1_parts[:, j, :]).then_inc(b1_in_w1q, 16)
            for i, (t, _, n) in enumerate(JOBS):
                sp.wait_ge(fin_step, 2 * (i + 1))
                if t == CLS:
                    sp.dma_start(out[:, 0, :], fin[0:n, i % 2, :]).then_inc(stored[i % 2], 16)
                else:
                    for b in range(IPT):
                        sp.dma_start(out[IPT * t + b, 1:SEQ, :],
                                     fin[PATCHES * b:PATCHES * (b + 1), i % 2, :]).then_inc(stored[i % 2], 16)
            for i in range(2):
                sp.wait_ge(stored[i], 16 * stores_before(i, NJ))

        def turn_bank(f):
            return ps_t if f % 2 == 0 else ps_b[:, 0, :]

        def embed_bank(t):
            return (ps_o, ps_b[:, 1, :], ps_l)[t % 3]

        def ffn_turn_bank(j):
            return ps_c if j % 2 == 0 else ps_l

        def hidden_bank(j):
            return ps_w if j % 2 == 0 else ps_b

        def contract_bank(j):
            return ps_t if j % 2 == 0 else ps_o

        def cands(r):
            return r + 1 if r < HI_ROUNDS else r + 2

        @block.tensor
        def _(pe):
            def count(r, both=False):
                pe.wait_ge(mask_ready, r + 1)
                for m in range(2):
                    chunks = MCH if both or m == 0 else ONES_CH
                    for k in range(chunks):
                        last = nc.tensor.matmul(cnt_part[:, m:m + 1], cmask[:, m, k * P:(k + 1) * P],
                                                twos_bf[:, both:both + 1], start=(k == 0), stop=(k == chunks - 1))
                last.then_inc(part_done, 1)

            def total(r, both=False):
                pe.wait_ge(part_copied, r + 1)
                if not both:
                    nc.tensor.matmul(cnt_all, ones_bf[:], half_n[:], start=True, stop=False)
                    nc.tensor.matmul(cnt_all, ones_bf[:], part[:, 0:2], start=False, stop=False)
                    last = nc.tensor.matmul(cnt_all, ones_bf[:], part[:, 2:4], start=False, stop=True)
                else:
                    last = nc.tensor.matmul(cnt_all, ones_bf[:], part[:, 0:4:3], start=True, stop=True)
                last.then_inc(count_done, 1)

            def embed(t, ks):
                if ks[0] == 0:
                    if t == 0:
                        pe.wait_ge(tokw_in, 16)
                    if t >= 3:
                        pe.wait_ge(h0_ready, t - 2)
                    pe.wait_ge(x_in[t], 16)
                dst = embed_bank(t)[:, 0:D]
                for k in ks:
                    last = nc.tensor.matmul(dst, x_sb[:, t, k, :], tokw_sb[:, k, :],
                                            start=(k == 0), stop=(k == C - 1))
                if ks[-1] == C - 1:
                    last.then_inc(tok_done, 1)

            def turn_hn(f):
                n = BATCH if f == 0 else P
                pe.wait_ge(hn_ready, f + 1)
                if f >= 2:
                    pe.wait_ge(hT_ready, f - 1)
                for k in range(2):
                    last = nc.tensor.transpose(turn_bank(f)[0:HALF, k * P:k * P + n],
                                               hn[0:n, f % 2, k * HALF:(k + 1) * HALF], ident[0:n, 0:n])
                last.then_inc(hn_turned, 1)

            def project(t, cs):
                if cs[0] == 0:
                    pe.wait_ge(hT_ready, t + 2)
                    if t == 0:
                        pe.wait_ge(wqkv_in, 16)
                    else:
                        pe.wait_ge(w_copied, t)
                n = P + 1 if t == 0 else P
                at = t * P + (t > 0)
                for c in cs:
                    for k in range(2):
                        last = nc.tensor.matmul(ps_w[:, c // 3, (c % 3) * n:(c % 3 + 1) * n],
                                                wqkv_sb[:, k, c * P:(c + 1) * P], hT_all[:, k, at:at + n],
                                                start=(k == 0), stop=(k == 1))
                if cs[-1] == C - 1:
                    last.then_inc(w_done, 1)

            def logits(t):
                pe.wait_ge(invm_ready, t + 1)
                if t == 0:
                    pe.wait_ge(h0_ready, TILES - 2)
                else:
                    pe.wait_ge(exp_done, 2 * t)
                for b in range(IPT):
                    for c in range(C):
                        j = 2 * (c % 3) + b
                        g = 32 * (c % 4)
                        last = nc.tensor.matmul(ps_l[g:g + 32, b * SEQ:(b + 1) * SEQ],
                                                invm[:, (c // 3) * 6 + j, :], wsq[:, t % 2, c // 3, j, :],
                                                start=(c < 4), stop=(c + 4 >= C), tile_position=(0, g))
                last.then_inc(logits_done, 1)

            def spread(t, cs):
                if cs[0] == 0:
                    pe.wait_ge(pi_ready, t + 1)
                    if t == 0:
                        pe.wait_ge(h0_ready, TILES)
                        pe.wait_ge(hT_ready, TILES + 1)
                    else:
                        pe.wait_ge(inv_sum_ready, t)
                for c in cs:
                    last = nc.tensor.matmul(ps_b[:, c // 3, (c % 3) * 2 * (SEQ + 1):(c % 3 + 1) * 2 * (SEQ + 1)],
                                            hrows_sb[:, c, :], pi[:, :, :].rearrange("h b n -> h (b n)"),
                                            start=True, stop=True)
                if cs[-1] == C - 1:
                    last.then_inc(spread_done, 1)

            def combine(t, cs):
                if cs[0] == 0:
                    pe.wait_ge(oT_ready, t + 1)
                    if t == 0:
                        pe.wait_ge(attn_in, 16 * N_ATTN)
                    if t >= 1:
                        pe.wait_ge(h1_ready, t)
                for c in cs:
                    last = nc.tensor.matmul(ps_o[:, 0:D], oT[:, t % 2, c, :], wout_sb[:, c, :],
                                            start=(c == 0), stop=(c == C - 1))
                if cs[-1] == C - 1:
                    last.then_inc(out_done, 1)

            def combine_cls():
                pe.wait_ge(ocls_ready, TILES)
                pe.wait_ge(h1_ready, TILES)
                for c in range(C):
                    last = nc.tensor.matmul(ps_o[0:BATCH, 0:D], ocls[:, c, :], wout_sb[:, c, :],
                                            start=(c == 0), stop=(c == C - 1))
                last.then_inc(out_done, 1)

            def beta_row():
                pe.wait_ge(tern_step, 6)
                pe.wait_ge(bet_ready, 1)
                for c in range(C):
                    nc.tensor.matmul(ps_t[:, 0:D], bet_b[:, c, :], w2q[:, c, :], start=(c == 0), stop=(c == C - 1))

            def column_sums():
                pe.wait_ge(w2g_ready, C)
                for c in range(C):
                    last = nc.tensor.matmul(ps_t[:, D:2 * D], ones[:], w2g[:, c, 0:D],
                                            start=(c == 0), stop=(c == C - 1))
                last.then_inc(rows_done, 1)

            def turn_yn(t):
                pe.wait_ge(yn_ready, t + 1)
                if t == 0:
                    pe.wait_ge(gb_ready, 2)
                if t == 1:
                    pe.wait_ge(exp_done, 2 * TILES)
                if t >= 2:
                    pe.wait_ge(yT_ready, 2 * (t - 1))
                if t == CLS_WITH:
                    pe.wait_ge(ync_ready, 1)
                bank = ffn_turn_bank(t)
                for k in range(2):
                    at = 128 + k * width(t)
                    last = nc.tensor.transpose(bank[0:HALF, at:at + P], yn[:, t % 2, k * HALF:(k + 1) * HALF], ident)
                    if t == CLS_WITH:
                        last = nc.tensor.transpose(bank[0:HALF, at + P:at + P + BATCH],
                                                   ync[:, k * HALF:(k + 1) * HALF], ident[0:BATCH, 0:BATCH])
                last.then_inc(yn_turned, 1)

            def hidden(t):
                n = width(t)
                pe.wait_ge(y_first, t + 1)
                if t >= 1:
                    pe.wait_ge(y_step, 3 * t)
                else:
                    pe.wait_ge(y0_step, 3)
                    pe.wait_ge(b1_in_w1q, 48)
                    pe.wait_ge(tern_step, 2)
                    pe.wait_ge(w_copied, TILES)
                if t == 1:
                    pe.wait_ge(inv_sum_ready, TILES)
                if t >= 2:
                    pe.wait_ge(gl_ready, t - 1)
                for c in range(C):
                    if t == 0 and c == C // 2:
                        pe.wait_ge(tern_step, 4)
                    for k in range(2):
                        for j in range(3):
                            rows = HALF + 3 if k == 1 and j == 0 else HALF
                            last = nc.tensor.matmul(hidden_bank(t)[:, c // 3, (c % 3) * n:(c % 3 + 1) * n],
                                                    w1q[0:rows, k, c * P:(c + 1) * P],
                                                    y_parts[0:rows, t % 2, j, k, 0:n],
                                                    start=(k == 0 and j == 0), stop=(k == 1 and j == 2))
                last.then_inc(hid_done, 1)

            def contract(i):
                _, ht, at, n, _ = job(i)
                dst = contract_bank(i)
                pe.wait_ge(gl_ready, ht + 1)
                if i >= 2:
                    pe.wait_ge(fin_step, 2 * (i - 1))
                if i == 0:
                    pe.wait_ge(rows_ready, 2)
                if i == 1:
                    pe.wait_ge(h1_ready, TILES + 1)
                for c in range(C):
                    nc.tensor.matmul(dst[0:n, 0:D + 1], gl[:, ht % 2, c, at:at + n], w2g[:, c, :],
                                     start=(c == 0), stop=(c == C - 1))
                pe.wait_ge(gsum_ready, ht + 1)
                nc.tensor.matmul(dst[0:n, D + 1:D + 2], gsum[:, ht % 2, at:at + n], ones[:, 0:1],
                                 start=True, stop=True).then_inc(ffn_done, 1)

            pe.wait_ge(ones_set, 4)
            embed(0, range(C))
            for r in range(EARLY):
                count(r)
                embed(1, range(3 * r, 3 * r + 3))
                total(r)
            pe.wait_ge(consts_in, 16)
            for t in range(TILES):
                if 1 <= t < TILES - 1:
                    embed(t + 1, range(2, C))
                if t + 2 < TILES:
                    embed(t + 2, range(0, 2))
                if PROJECT_0 <= t < PROJECT_0 + 3:
                    project(0, range(2 * (t - PROJECT_0), 2 * (t - PROJECT_0) + 2))
                elif t == TILES - 1:
                    project(1, range(0, 4))
                count(EARLY + t)
                turn_hn(t)
                total(EARLY + t)
            logits(0)
            project(1, range(4, C))
            turn_hn(TILES)

            for s in range(TILES):
                rr = rounds_of.get(s, {})
                ahead = s + 1 < TILES
                if s == 1:
                    pe.wait_ge(abs_done, 2)
                    pe.wait_ge(mask_ready, rr[0] + 1)
                    nc.tensor.matmul(asum_all, ones[:], asum[:], start=True, stop=True)
                if 0 in rr:
                    count(rr[0])
                if 2 <= s < TILES - 1:
                    project(s + 1, range(1, 2))
                if 0 in rr:
                    total(rr[0])
                if 1 <= s < TILES - 1:
                    project(s + 1, range(1 if s == 1 else 2, 5))
                if 1 in rr:
                    count(rr[1])
                if 1 <= s < TILES - 1:
                    project(s + 1, range(5, C))
                if 1 in rr:
                    total(rr[1])
                if s == LAST_ROUNDS + 1:
                    count(ROUNDS, both=True)
                early = 3 if rr else C
                if s >= 2:
                    combine(s - 2, range(0, early))
                if not ahead:
                    turn_yn(0)
                at = C - 1 if s == 1 else 1
                spread(s, range(0, at))
                if 2 in rr:
                    count(rr[2])
                spread(s, range(at, at + 1))
                if 2 in rr:
                    total(rr[2])
                if s == LAST_ROUNDS + 1:
                    total(ROUNDS, both=True)
                if at + 1 < C:
                    spread(s, range(at + 1, C))
                if s >= 2 and rr:
                    combine(s - 2, range(3, 4))
                if 3 in rr:
                    count(rr[3])
                if s >= 2 and rr:
                    combine(s - 2, range(4, 5))
                if 3 in rr:
                    total(rr[3])
                if s >= 2 and rr:
                    combine(s - 2, range(5, C))
                if ahead:
                    logits(s + 1)
                if s + 2 < TILES:
                    project(s + 2, range(0, 1))

            hidden(0)
            turn_yn(1)
            combine(TILES - 2, range(C))
            hidden(1)
            turn_yn(2)
            beta_row()
            column_sums()
            combine(TILES - 1, range(C))
            combine_cls()
            for t in range(TILES):
                contract(last_job(t - 1) if t else 0)
                if t + 3 < TILES:
                    turn_yn(t + 3)
                if t == CLS_WITH:
                    contract(last_job(t) - 1)
                if t + 2 < TILES:
                    hidden(t + 2)

        @block.scalar
        def _(act):
            act.dma_start(tokw_sb[:], tok_w).then_inc(tokw_in, 16)
            act.dma_start(q_sb[:], sparsity.partition_broadcast(P)).then_inc(q_in, 16)
            act.dma_start(w2f_sb[:], w2_t).then_inc(flat_in[1], 16)
            act.dma_start(ri_sb[:], rows_ident).then_inc(consts_in, 16)
            act.dma_start(temp_rows_sb[:], temp_cols.partition_broadcast(P)).then_inc(attn_in, 16)
            act.dma_start(hcols_sb[:], head_cols).then_inc(attn_in, 16)

            def signs_of(r):
                act.wait_ge(cand_ready, cands(r))
                if r == 0:
                    act.wait_ge(halves_ready, 2)
                keys = hi16 if r < HI_ROUNDS else lo16
                with nc.allow_low_precision(reason="whole numbers up to WCOLS are exact in float16"):
                    nc.scalar.activation(signs[:], keys[:, 1, ONES_COLS:], ACT.Sign, bias=cand[:, 1:2], scale=-1.0,
                                         accum_out=part[:, 1:2])

            def copy_part(r):
                act.wait_ge(part_done, r + 1)
                nc.scalar.copy(part[:, 0:4:3], cnt_part).then_inc(part_copied, 1)

            def copy_hT(f):
                act.wait_ge(hn_turned, f + 1)
                src = turn_bank(f)[0:HALF, 0:2 * P].rearrange("p (k n) -> p k n", k=2)
                if f == 0:
                    nc.scalar.copy(hT_all[:, :, P:P + 1], src[:, :, 0:1]).then_inc(hT_ready, 1)
                else:
                    at = (f - 1) * P + (f > 1)
                    nc.scalar.copy(hT_all[:, :, at:at + P], src).then_inc(hT_ready, 1)

            def w_parts(t):
                if t == 0:
                    for b in range(IPT):
                        src = ps_w[:, :, 0:3 * (P + 1)].rearrange("p k (c n) -> p k c n", n=P + 1)
                        yield (src[:, :, :, b * PATCHES:(b + 1) * PATCHES],
                               lambda buf, b=b: buf[:, 0].rearrange("p k (c b) n -> p k c b n", b=IPT)
                               [:, :, :, b, 0:PATCHES])
                else:
                    yield (ps_w[:, :, 0:3 * P].rearrange("p k (j n) -> p k j n", n=PATCHES),
                           lambda buf: buf[:, t % 2, :, :, 0:PATCHES])

            def square_w(t):
                act.wait_ge(w_done, t + 1)
                if t >= 2:
                    act.wait_ge(logits_done, t - 1)
                for src, at in w_parts(t):
                    last = nc.scalar.activation(at(wsq), src, ACT.Square)
                last.then_inc(wsq_ready, 1)

            def copy_w(t):
                if t >= 2:
                    act.wait_ge(wwp_ready, t - 1)
                for src, at in w_parts(t):
                    last = nc.scalar.copy(at(w_s), src)
                last.then_inc(w_copied, 1)

            def exps(t):
                act.wait_ge(nmx_ready, t + 1)
                for b in range(IPT):
                    nc.scalar.activation(ex[:, b, :], ps_l[:, b * SEQ:(b + 1) * SEQ], ACT.Exp, bias=nmx[:, b:b + 1],
                                         accum_out=sm[:, b:b + 1]).then_inc(exp_done, 1)

            def scale_pi(t):
                act.wait_ge(rsm_ready, t + 1)
                if t >= 1:
                    act.wait_ge(spread_done, t)
                for b in range(IPT):
                    nc.scalar.activation(pi[:, b, 0:SEQ], ex[:, b, :], ACT.Copy, scale=rsm[:, b:b + 1],
                                         accum_out=sp[:, 0, b:b + 1]).then_inc(pi_scaled, 1)

            def spread_beta():
                act.wait_ge(gb_ready, 2)
                nc.scalar.copy(bet_b[:], gb2_s[:, 1, :].unsqueeze(2).to_broadcast([P, C, P])).then_inc(bet_ready, 1)

            def take_yT(t):
                n = width(t)
                act.wait_ge(yn_turned, t + 1)
                if t == 0:
                    act.wait_ge(gb_ready, 2)
                if t >= 2:
                    act.wait_ge(hid_done, t - 1)
                for k in range(2):
                    src = ffn_turn_bank(t)[0:HALF, 128 + k * n:128 + (k + 1) * n]
                    nc.scalar.activation(yT[:, t % 2, k, 0:n], src, ACT.Identity,
                                         scale=gb1_s[:, 0, k:k + 1], bias=gb1_s[:, 1, k:k + 1]).then_inc(yT_ready, 1)
                act.wait_ge(yT_ready, 2 * t + 2)
                nc.scalar.copy(y_parts[0:HALF, t % 2, 0, :, 0:n], yT[:, t % 2, :, 0:n]).then_inc(y_first, 1)

            def gelu(t):
                n = width(t)
                act.wait_ge(hid_done, t + 1)
                if t >= 2:
                    act.wait_ge(ffn_done, last_job(t - 2))
                src = hidden_bank(t)[:, :, 0:3 * n].rearrange("p k (c n) -> p k c n", n=n)
                dst = gl[:, t % 2, :, 0:n].rearrange("p (k c) n -> p k c n", k=2)
                nc.scalar.activation(dst, src, ACT.Gelu_apprx_tanh).then_inc(gl_ready, 1)
                act.wait_ge(gl_ready, t + 1)
                if t >= 2:
                    act.wait_ge(gsum_ready, t - 1)
                nc.scalar.activation(glsq[:, t % 2, :, 0:n], gl[:, t % 2, :, 0:n], ACT.Square).then_inc(glsq_ready, 1)

            def gamma_w2():
                act.wait_ge(gb_ready, 2)
                act.wait_ge(tern_step, 6)
                for c in range(C):
                    nc.scalar.activation(w2g[:, c, 0:D], w2q[:, c, :], ACT.Copy, scale=gb2_s[:, 0, c:c + 1])\
                        .then_inc(w2g_ready, 1)

            def lift_hi(m):
                act.wait_ge(halves_ready, m + 1)
                nc.scalar.activation(hi_value[:, m, :], hi16[:, m, :], ACT.Copy, scale=65536.0)\
                    .then_inc(hi_value_ready, 1)

            def magnitudes(m):
                nc.scalar.activation(absw[:, m, :], flat[m], ACT.Abs, accum_out=asum[:, m:m + 1]).then_inc(abs_done, 1)

            for r in range(EARLY):
                lift_hi(r)
                signs_of(r)
                copy_part(r)
            act.wait_ge(flat_in[0], 16)
            magnitudes(0)
            for t in range(TILES):
                r = EARLY + t
                signs_of(r)
                copy_part(r)
                copy_hT(t)
                if t == 0:
                    act.wait_ge(flat_in[1], 16)
                    magnitudes(1)
                if t == PROJECT_0 + 2:
                    act.wait_ge(w_done, 1)
                    nc.scalar.copy(wcls[:], ps_w[:, :, 0:3 * (P + 1)].rearrange("p k (c n) -> p k c n", n=P + 1)
                                   [:, :, :, P]).then_inc(wcls_copied, 1)
                    square_w(0)
                    copy_w(0)

            for s in range(TILES):
                rr = rounds_of.get(s, {})
                ahead = s + 1 < TILES
                if 0 in rr:
                    signs_of(rr[0])
                if s == 0:
                    copy_hT(TILES)
                    copy_part(rr[0])
                exps(s)
                if 0 in rr and s > 0:
                    copy_part(rr[0])
                scale_pi(s)
                if 1 in rr:
                    signs_of(rr[1])
                    copy_part(rr[1])
                if ahead:
                    square_w(s + 1)
                if s == LAST_ROUNDS + 1:
                    copy_part(ROUNDS)
                if 2 in rr:
                    signs_of(rr[2])
                    copy_part(rr[2])
                if ahead:
                    copy_w(s + 1)
                if 3 in rr:
                    signs_of(rr[3])
                    copy_part(rr[3])
            act.wait_ge(memsets, 3)
            take_yT(0)
            spread_beta()
            take_yT(1)
            gelu(0)
            gamma_w2()
            take_yT(2)
            for t in range(1, TILES):
                gelu(t)
                if t + 2 < TILES:
                    take_yT(t + 2)

        @block.gpsimd
        def _(pool):
            def rstd_front(f):
                i = f % 2
                n = BATCH if f == 0 else P
                pool.wait_ge(st0_step, 2 * f + 2)
                if f >= 2:
                    pool.wait_ge(hn_ready, f - 1)
                nc.gpsimd.tensor_scalar(rs0[0:n, i, 0:1], mv0[0:n, i, 1:2], EPS, None, ALU.add).then_inc(rs0_step, 1)
                pool.wait_ge(rs0_step, 2 * f + 1)
                nc.gpsimd.tensor_tensor(rs0[0:n, i, 1:2], rs0[0:n, i, 0:1], neg_half[0:n, :], ALU.pow)\
                    .then_inc(rs0_step, 1)

            def add_bias(f):
                pool.wait_ge(hn_ready, f + 1)
                if f == 0:
                    nc.gpsimd.tensor_tensor(h0c[:], h0c[:], bout_sb[0:BATCH, :], ALU.add).then_inc(bias_in_h0, 1)
                else:
                    nc.gpsimd.tensor_tensor(h0[:, f - 1, :], h0[:, f - 1, :], bout_sb, ALU.add)\
                        .then_inc(bias_in_h0, 1)

            def spread_cls():
                pool.wait_ge(wcls_copied, 1)
                for i in range(2):
                    for b in range(IPT):
                        nc.gpsimd.tensor_copy(
                            w_s[:, i, :, :, PATCHES].rearrange("p k (c b) -> p k c b", b=IPT)[:, :, :, b], wcls[:])\
                            .then_inc(wcls_spread, 1)
                        nc.gpsimd.tensor_tensor(
                            wsq[:, i, :, :, PATCHES].rearrange("p k (c b) -> p k c b", b=IPT)[:, :, :, b],
                            wcls[:], wcls[:], ALU.mult).then_inc(wcls_spread, 1)

            def dots(t):
                pool.wait_ge(wp_ready, t + 1)
                if t >= 1:
                    pool.wait_ge(ds_ready, t)
                nc.gpsimd.tensor_tensor(wwp[:], w_s[:, t % 2], wp[:, t % 2], ALU.mult).then_inc(wwp_ready, 1)
                pool.wait_ge(wwp_ready, t + 1)
                nc.gpsimd.tensor_tensor(wwp[:, :, :, 0:FOLD], wwp[:, :, :, 0:FOLD], wwp[:, :, :, SEQ - FOLD:SEQ],
                                        ALU.add).then_inc(wwp_folded, 1)

            def plus_one(t):
                pool.wait_ge(ds_ready, t + 1)
                pool.wait_ge(inv_sum_ready, t + 1)
                nc.gpsimd.tensor_tensor(att[:, 0, :], ds[:], inv_sum[:], ALU.mult).then_inc(att_step, 1)
                pool.wait_ge(att_step, 2 * t + 1)
                nc.gpsimd.tensor_scalar(att[:, 1, :], att[:, 0, :], -1.0, -1.0, ALU.mult, ALU.add)\
                    .then_inc(att_step, 1)

            def attend(t):
                pool.wait_ge(att_ready, t + 1)
                if t >= 2:
                    pool.wait_ge(out_done, t - 1)
                src = wp[:, t % 2].rearrange("p k j n -> p (k j) n")
                dst = oT[:, t % 2, :, :].rearrange("p c (b n) -> p (c b) n", b=IPT)
                nc.gpsimd.tensor_tensor(dst, src[:, :, 0:PATCHES],
                                        att[:, 2, :].unsqueeze(2).to_broadcast([P, 12, PATCHES]), ALU.mult)\
                    .then_inc(oT_ready, 1)
                nc.gpsimd.tensor_tensor(ocls[:, :, IPT * t:IPT * (t + 1)],
                                        src[:, :, PATCHES].rearrange("p (c b) -> p c b", b=IPT),
                                        att[:, 2, :].rearrange("p (c b) -> p c b", b=IPT), ALU.mult)\
                    .then_inc(ocls_ready, 1)

            def split_y_0():
                pool.wait_ge(y_first, 1)
                first, second, third = (y_parts[0:HALF, 0, j, :, 0:P] for j in range(3))
                nc.gpsimd.tensor_tensor(second, yT[:, 0, :, 0:P], first, ALU.subtract).then_inc(y0_step, 1)
                nc.gpsimd.tensor_tensor(y0_rest[:], yT[:, 0, :, 0:P], first, ALU.subtract).then_inc(y0_step, 1)
                pool.wait_ge(y0_step, 2)
                nc.gpsimd.tensor_tensor(third, y0_rest[:], second, ALU.subtract).then_inc(y0_step, 1)

            def split_b1():
                pool.wait_ge(b1_in, 16)
                nc.gpsimd.tensor_copy(b1_parts[:, 0, :], b1_rest).then_inc(b1_step, 1)
                pool.wait_ge(b1_step, 1)
                for j in range(2):
                    nc.gpsimd.tensor_tensor(b1_rest, b1_rest, b1_parts[:, j, :], ALU.subtract).then_inc(b1_step, 1)
                    pool.wait_ge(b1_step, 2 * j + 2)
                    nc.gpsimd.tensor_copy(b1_parts[:, j + 1, :], b1_rest).then_inc(b1_step, 1)
                    pool.wait_ge(b1_step, 2 * j + 3)

            def rstd_mid(t):
                n = BATCH if t == CLS else P
                pool.wait_ge(st1_step, 2 * t + 2)
                nc.gpsimd.tensor_scalar(rs1[0:n, t, 0:1], mv1[0:n, t, 1:2], 1.0 + EPS, EPS * EPS, ALU.mult, ALU.add)\
                    .then_inc(rs1_step, 1)
                pool.wait_ge(rs1_step, 2 * t + 1)
                nc.gpsimd.tensor_tensor(rs1[0:n, t, 1:2], rs1[0:n, t, 0:1], neg_half[0:n, :], ALU.pow)\
                    .then_inc(rs1_step, 1)

            def moments(i):
                n = job(i)[3]
                b = i % 2
                pool.wait_ge(mom_ready, i + 1)
                if i >= 2:
                    pool.wait_ge(fin_step, 2 * (i - 1))
                nc.gpsimd.tensor_tensor(ms[0:n, b, 0:1], mom[0:n, b, 0:1], mom[0:n, b, 0:1], ALU.mult)\
                    .then_inc(ms_step, 1)
                pool.wait_ge(ms_step, 5 * i + 1)
                nc.gpsimd.tensor_tensor(ms[0:n, b, 1:2], mom[0:n, b, 1:2], ms[0:n, b, 0:1], ALU.subtract)\
                    .then_inc(ms_step, 1)
                pool.wait_ge(ms_step, 5 * i + 2)
                nc.gpsimd.tensor_scalar(ms[0:n, b, 0:1], ms[0:n, b, 1:2], 0.0, EPS, ALU.max, ALU.add)\
                    .then_inc(ms_step, 1)
                pool.wait_ge(ms_step, 5 * i + 3)
                nc.gpsimd.tensor_tensor(ms[0:n, b, 2:3], ms[0:n, b, 0:1], neg_half[0:n, :], ALU.pow)\
                    .then_inc(ms_step, 1)
                pool.wait_ge(ms_step, 5 * i + 4)
                nc.gpsimd.tensor_tensor(ms[0:n, b, 3:4], mom[0:n, b, 0:1], ms[0:n, b, 2:3], ALU.mult)\
                    .then_inc(ms_step, 1)

            def add_crow(i):
                _, _, _, n, h = job(i)
                pool.wait_ge(rows_ready, 2)
                if i == CLS_WITH + 1:
                    pool.wait_ge(ync_ready, 1)
                else:
                    pool.wait_ge(yn_ready, i + 1 if i <= CLS_WITH else i)
                nc.gpsimd.tensor_tensor(h, h, crow[0:n, :], ALU.add).then_inc(crow_in_h1, 1)

            nc.gpsimd.memset(neg_half[:], -0.5).then_inc(memsets, 1)
            nc.gpsimd.memset(w2g[:, :, D:D + 1], 1.0).then_inc(memsets, 1)
            pool.wait_ge(memsets, 3)
            pool.wait_ge(row_in, 32)
            rstd_front(0)
            add_bias(0)
            for t in range(TILES):
                rstd_front(t + 1)
                add_bias(t + 1)
                if t == PROJECT_0 + 2:
                    spread_cls()
            split_b1()
            for t in range(TILES):
                dots(t)
                if t == TILES - 2:
                    split_y_0()
                if t >= 2:
                    rstd_mid(t - 2)
                plus_one(t)
                attend(t)
                if t == LAST_ROUNDS:
                    pool.wait_ge(next_ready, 1)
                    nc.gpsimd.partition_all_reduce(sel[:, 2, :], sel[:, 1, :], P, bass.bass_isa.ReduceOp.max)\
                        .then_inc(next_all, 1)
            rstd_mid(TILES - 2)
            rstd_mid(TILES - 1)
            rstd_mid(CLS)
            for i in range(NJ):
                add_crow(i)
                moments(i)

        @block.vector
        def _(dve):
            nc.vector.memset(ones[:], 1.0).then_inc(ones_set, 1)
            nc.vector.memset(ones_bf[:], 1.0).then_inc(ones_set, 1)
            nc.vector.memset(twos_bf[:, 0:1], 2.0)
            nc.vector.memset(twos_bf[:, 1:2], 2.0 / LIFT).then_inc(ones_set, 1)
            nc.vector.memset(half_n[:, 0:1], 0.0)
            nc.vector.memset(half_n[:, 1:2], float(WCOLS - ONES_COLS)).then_inc(ones_set, 1)
            nc.vector.memset(part[:, 2:3], 0.0)
            nc.vector.memset(y_parts[HALF:HALF + 3, :, 0, 1, :], 1.0).then_inc(memsets, 1)
            nc.vector.memset(cand_off[:, 0:1], 0.5)
            nc.vector.memset(cand_off[:, 1:2], 0.0)

            def first_cands(rounds):
                nc.vector.memset(cand[:, 0:1], 2.0 ** (rounds - 1))
                nc.vector.memset(cand[:, 1:2], 2.0 ** (rounds - 1) - 0.5).then_inc(cand_ready, 1)

            first_cands(HI_ROUNDS)

            dve.wait_ge(q_in, 16)
            steps = [0]

            def q_op(ins):
                steps[0] += 1
                ins.then_inc(q_step, 1)
                dve.wait_ge(q_step, steps[0])

            def col(i):
                return qs[:, i:i + 1]

            q_op(nc.vector.tensor_scalar(col(0), q_sb[:], float(N_W - 1), None, ALU.mult))
            q_op(nc.vector.tensor_scalar(col(1), col(0), ROUND_MAGIC, None, ALU.add))
            q_op(nc.vector.tensor_scalar(col(1), col(1), ROUND_MAGIC, None, ALU.subtract))
            q_op(nc.vector.tensor_tensor(col(2), col(1), col(0), ALU.is_gt))
            q_op(nc.vector.tensor_tensor(col(2), col(1), col(2), ALU.subtract))
            q_op(nc.vector.tensor_scalar(col(4), col(2), 0.0, float(N_W - 1), ALU.max, ALU.min))
            q_op(nc.vector.tensor_scalar(col(8), col(4), 2.0, None, ALU.mult))
            q_op(nc.vector.tensor_tensor(col(3), col(0), col(2), ALU.subtract))
            q_op(nc.vector.tensor_scalar(col(6), col(3), -1.0, 1.0, ALU.mult, ALU.add))
            q_op(nc.vector.tensor_scalar(col(7), col(3), 0.0, None, ALU.is_gt))
            q_op(nc.vector.tensor_tensor(col(7), col(2), col(7), ALU.add))
            q_op(nc.vector.tensor_scalar(col(5), col(7), 0.0, float(N_W - 1), ALU.max, ALU.min))

            for m in range(2):
                dve.wait_ge(flat_in[m], 16)
                v = flat[m].bitcast(U16).rearrange("p (n e) -> p n e", e=2)
                nc.vector.tensor_scalar(hi16[:, m, :], v[:, :, 1], 0x7FFF, None, ALU.bitwise_and)\
                    .then_inc(halves_ready, 1)

            def step(r):
                return 2.0 ** ((HI_ROUNDS if r < HI_ROUNDS else ROUNDS) - 1 - r)

            def masks(r):
                dve.wait_ge(cand_ready, cands(r))
                keys = hi16 if r < HI_ROUNDS else lo16
                if r == 0:
                    dve.wait_ge(halves_ready, 2)
                nc.vector.tensor_scalar(cmask[:, 0, :], keys[:, 0, :], cand[:, 0:1], None, ALU.is_lt)
                nc.vector.tensor_scalar(cmask[:, 1, 0:ONES_COLS], keys[:, 1, 0:ONES_COLS], cand[:, 1:2], None,
                                        ALU.is_lt).then_inc(mask_ready, 1)
                set_base(r)

            def set_base(r):
                nc.vector.tensor_scalar(base[:, r % 2, :], cand[:], step(r) / 2, None, ALU.subtract)\
                    .then_inc(base_ready, 1)

            def test(r):
                dve.wait_ge(count_done, r + 1)
                nc.vector.tensor_scalar(rise[:], cnt_all, col(8), step(r), ALU.is_le, ALU.mult)\
                    .then_inc(rise_ready, 1)

            def next_cand(r):
                dve.wait_ge(rise_ready, r + 1)
                dve.wait_ge(base_ready, r + 1)
                nc.vector.tensor_tensor(cand[:], base[:, r % 2, :], rise[:], ALU.add).then_inc(cand_ready, 1)

            def next_masks(r):
                if r == HI_ROUNDS - 1:
                    dve.wait_ge(cand_ready, cands(r) + 1)
                    low_keys()
                    masks(r + 1)
                elif r + 1 < ROUNDS:
                    keys = hi16 if r + 1 < HI_ROUNDS else lo16
                    nc.vector.tensor_scalar(cmask[:, 0, :], keys[:, 0, :], rise[:, 0:1], base[:, r % 2, 0:1],
                                            ALU.subtract, ALU.is_lt)
                    nc.vector.tensor_scalar(cmask[:, 1, 0:ONES_COLS], keys[:, 1, 0:ONES_COLS], rise[:, 1:2],
                                            base[:, r % 2, 1:2], ALU.subtract, ALU.is_lt).then_inc(mask_ready, 1)
                    dve.wait_ge(cand_ready, cands(r + 1))
                    set_base(r + 1)

            def low_keys():
                nc.vector.tensor_tensor(hi_f[:], cand[:], cand_off[:], ALU.subtract).then_inc(low_step, 1)
                dve.wait_ge(low_step, 1)
                nc.vector.tensor_scalar(hi_top[:], hi_f[:], 65536.0, None, ALU.mult).then_inc(low_step, 1)
                dve.wait_ge(low_step, 2)
                dve.wait_ge(hi_value_ready, 2)
                for m in range(2):
                    v = flat[m].bitcast(U16).rearrange("p (n e) -> p n e", e=2)
                    nc.vector.scalar_tensor_tensor(wide[:, m, :], hi_value[:, m, :], hi_top[:, m:m + 1], v[:, :, 0],
                                                   ALU.subtract, ALU.add).then_inc(low_step, 1)
                for m in range(2):
                    dve.wait_ge(low_step, 3 + m)
                    nc.vector.tensor_scalar(lo16[:, m, :], wide[:, m, :], 0.0, 65535.0, ALU.max, ALU.min)\
                        .then_inc(low_step, 1)
                dve.wait_ge(low_step, 6)
                first_cands(LO_ROUNDS)

            def stats_front(f):
                n = BATCH if f == 0 else P
                if f >= 1:
                    dve.wait_ge(h0_ready, f)
                nc.vector.bn_stats(st0[0:n, f % 2, :], h0c[:] if f == 0 else h0[:, f - 1, :]).then_inc(st0_step, 1)

            def aggr_front(f):
                n = BATCH if f == 0 else P
                dve.wait_ge(st0_step, 2 * f + 1)
                nc.vector.bn_aggr(mv0[0:n, f % 2, :], st0[0:n, f % 2, :]).then_inc(st0_step, 1)

            def take_tok(t):
                dve.wait_ge(tok_done, t + 1)
                src = embed_bank(t)[:, 0:D]
                nc.vector.tensor_tensor(h0[:, t, :], src, tokb_sb, ALU.add).then_inc(h0_ready, 1)

            def norm_front(f):
                n = BATCH if f == 0 else P
                i = f % 2
                src = h0c[:] if f == 0 else h0[:, f - 1, :]
                dve.wait_ge(rs0_step, 2 * f + 2)
                if f >= 2:
                    dve.wait_ge(hn_turned, f - 1)
                nc.vector.tensor_scalar(hn[0:n, i, :], src, mv0[0:n, i, 0:1], rs0[0:n, i, 1:2],
                                        ALU.subtract, ALU.mult).then_inc(hn_ready, 1)

            def temp_cols_in():
                dve.wait_ge(attn_in, 16 * N_ATTN)
                nc.vector.tensor_tensor(tcols[:], hcols_sb[:], temp_rows_sb[:], ALU.mult).then_inc(tcols_ready, 1)

            def norms(t):
                dve.wait_ge(wsq_ready, t + 1)
                if t == 0:
                    dve.wait_ge(wcls_spread, 4 * IPT)
                nc.vector.tensor_reduce(n2[:], wsq[:, t % 2].rearrange("p k j n -> p (k j) n"), AX.X, ALU.add)\
                    .then_inc(norm_step, 1)

            def guard_norms(t):
                dve.wait_ge(norm_step, 3 * t + 1)
                nc.vector.tensor_scalar(inv[:, 0, :], n2[:], 1e-24, None, ALU.max).then_inc(norm_step, 1)

            def invert_norms(t):
                dve.wait_ge(norm_step, 3 * t + 2)
                nc.vector.reciprocal(inv[:, 1, :], inv[:, 0, :]).then_inc(norm_step, 1)

            def place_norms(t):
                dve.wait_ge(norm_step, 3 * t + 3)
                if t == 0:
                    dve.wait_ge(tcols_ready, 1)
                if t >= 1:
                    dve.wait_ge(logits_done, t)
                nc.vector.tensor_tensor(invm[:, :, :].rearrange("p (c b) h -> p c b h", b=IPT),
                                        tcols[:, :, :].unsqueeze(2).to_broadcast([P, C, IPT, 32]),
                                        inv[:, 1, :].rearrange("p (c b) -> p c b", b=IPT).unsqueeze(3)
                                        .to_broadcast([P, C, IPT, 32]), ALU.mult).then_inc(invm_ready, 1)

            def row_max(t):
                dve.wait_ge(logits_done, t + 1)
                nc.vector.tensor_reduce(nmx[:], ps_l[:, 0:IPT * SEQ].rearrange("p (b n) -> p b n", n=SEQ),
                                        AX.X, ALU.max, negate=True).then_inc(nmx_ready, 1)

            def soft_scale(t):
                dve.wait_ge(exp_done, 2 * (t + 1))
                nc.vector.reciprocal(rsm[:], sm[:]).then_inc(rsm_ready, 1)

            def sum_guard(t):
                dve.wait_ge(pi_scaled, 2 * (t + 1))
                nc.vector.tensor_scalar(sp[:, 1, :], sp[:, 0, :], 1e-8, None, ALU.add).then_inc(sp_ready, 1)

            def invert_sum(t):
                dve.wait_ge(sp_ready, t + 1)
                nc.vector.reciprocal(pi[:, :, SEQ], sp[:, 1, :]).then_inc(pi_ready, 1)

            def spread_view():
                return ps_b[:, :, 0:6 * (SEQ + 1)].rearrange("p k (j n) -> p k j n", n=SEQ + 1)

            def weigh(t):
                dve.wait_ge(spread_done, t + 1)
                dve.wait_ge(w_copied, t + 1)
                if t >= 2:
                    dve.wait_ge(ocls_ready, t - 1)
                nc.vector.tensor_tensor(wp[:, t % 2], w_s[:, t % 2], spread_view()[:, :, :, 0:SEQ], ALU.mult)\
                    .then_inc(wp_ready, 1)
                if t >= 1:
                    dve.wait_ge(att_step, 2 * t)
                nc.vector.tensor_copy(inv_sum[:].rearrange("p (k j) -> p k j", k=2), spread_view()[:, :, :, SEQ])\
                    .then_inc(inv_sum_ready, 1)

            def sum_dots(t):
                dve.wait_ge(wwp_folded, t + 1)
                if t >= 1:
                    dve.wait_ge(att_step, 2 * t)
                nc.vector.tensor_reduce(ds[:], wwp[:, :, :, 0:SEQ - FOLD].rearrange("p k j n -> p (k j) n"),
                                        AX.X, ALU.add).then_inc(ds_ready, 1)

            def invert_att(t):
                dve.wait_ge(att_step, 2 * t + 2)
                if t >= 1:
                    dve.wait_ge(ocls_ready, t)
                nc.vector.reciprocal(att[:, 2, :], att[:, 1, :]).then_inc(att_ready, 1)

            def take_out(t):
                n = P if t < TILES else BATCH
                src = h0[:, t, :] if t < TILES else h0c[:]
                dve.wait_ge(out_done, t + 1)
                dve.wait_ge(bias_in_h0, min(t + 2, TILES + 1))
                nc.vector.tensor_tensor(h1[:, t, :] if t < TILES else h1c[:], ps_o[0:n, 0:D], src, ALU.add)\
                    .then_inc(h1_ready, 1)

            def stats_mid(t):
                n = P if t < TILES else BATCH
                dve.wait_ge(h1_ready, t + 1)
                nc.vector.bn_stats(st1[0:n, t % 2, :], h1[:, t, :] if t < TILES else h1c[:]).then_inc(st1_step, 1)

            def aggr_mid(t):
                n = P if t < TILES else BATCH
                dve.wait_ge(st1_step, 2 * t + 1)
                nc.vector.bn_aggr(mv1[0:n, t, :], st1[0:n, t % 2, :]).then_inc(st1_step, 1)

            done = [0]
            s_lo = bits[:, 3, :].bitcast(F32)

            def sel_op(ins):
                done[0] += 1
                ins.then_inc(select_step, 1)
                dve.wait_ge(select_step, done[0])

            def lower_statistic():
                dve.wait_ge(cand_ready, ROUNDS + 2)
                sel_op(nc.vector.tensor_tensor(bits[:, 0, :], cand[:], cand_off[:], ALU.subtract))
                sel_op(nc.vector.tensor_copy(bits[:, 1, :], hi_f[:]))
                sel_op(nc.vector.tensor_scalar(bits[:, 2, :], bits[:, 1, :], 16, None, ALU.logical_shift_left))
                sel_op(nc.vector.tensor_tensor(bits[:, 3, :], bits[:, 2, :], bits[:, 0, :], ALU.bitwise_or))

            def low_masks():
                dve.wait_ge(abs_done, 2)
                dve.wait_ge(part_done, ROUNDS)
                for m in range(2):
                    last = nc.vector.tensor_scalar(cmask[:, m, :], absw[:, m, :], s_lo[:, m:m + 1], LIFT,
                                                   ALU.is_le, ALU.mult)
                last.then_inc(mask_ready, 1)

            def smallest_above(m):
                dve.wait_ge(mask_ready, ROUNDS + 1)
                nc.vector.tensor_tensor_reduce(out=wide[:, m, :], in0=cmask[:, m, :], in1=absw[:, m, :],
                                               scale=1.0, scalar=BIG, op0=ALU.add, op1=ALU.min,
                                               accum_out=sel[:, 0, m:m + 1]).then_inc(select_step, 1)

            def negate_next():
                dve.wait_ge(select_step, 6)
                nc.vector.tensor_scalar(sel[:, 1, :], sel[:, 0, :], -1.0, None, ALU.mult).then_inc(next_ready, 1)

            def compare_counts():
                dve.wait_ge(count_done, ROUNDS + 1)
                nc.vector.tensor_scalar(sel[:, 3, :], cnt_all, 0.5, col(5), ALU.mult, ALU.is_gt)\
                    .then_inc(select_step, 1)

            def choose_low():
                dve.wait_ge(select_step, 7)
                nc.vector.tensor_tensor(sel[:, 4, :], sel[:, 3, :], s_lo, ALU.mult).then_inc(select_step, 1)
                nc.vector.tensor_scalar(sel[:, 5, :], sel[:, 3, :], 1.0, None, ALU.subtract).then_inc(select_step, 1)
                nc.vector.tensor_scalar(sel[:, 8, :], s_lo, col(6), None, ALU.mult).then_inc(select_step, 1)

            def choose_next():
                dve.wait_ge(next_all, 1)
                dve.wait_ge(select_step, 9)
                nc.vector.tensor_tensor(sel[:, 6, :], sel[:, 5, :], sel[:, 2, :], ALU.mult).then_inc(select_step, 1)

            def take_chosen():
                dve.wait_ge(select_step, 11)
                nc.vector.tensor_tensor(sel[:, 7, :], sel[:, 4, :], sel[:, 6, :], ALU.add).then_inc(select_step, 1)

            def weigh_chosen():
                dve.wait_ge(select_step, 12)
                nc.vector.tensor_scalar(sel[:, 9, :], sel[:, 7, :], col(3), None, ALU.mult).then_inc(select_step, 1)

            def threshold():
                dve.wait_ge(select_step, 13)
                nc.vector.tensor_tensor(sel[:, 10, :], sel[:, 8, :], sel[:, 9, :], ALU.add).then_inc(select_step, 1)

            def negative_threshold():
                dve.wait_ge(select_step, 14)
                nc.vector.tensor_scalar(sel[:, 11, :], sel[:, 10, :], -1.0, None, ALU.mult).then_inc(select_step, 1)

            def above(m, n=P):
                return sel[0:n, 10, m:m + 1]

            def below(m, n=P):
                return sel[0:n, 11, m:m + 1]

            def negatives_1(half):
                if half == 0:
                    dve.wait_ge(ffn_in, 16 * N_FFN)
                    dve.wait_ge(select_step, 15)
                cols = hid_half(half)
                nc.vector.tensor_scalar(w1neg[:, :, cols], w1t_sb[:, :, cols], below(0, HALF), None, ALU.is_lt)\
                    .then_inc(tern_step, 1)

            def ternary_1(half):
                dve.wait_ge(tern_step, 2 * half + 1)
                cols = hid_half(half)
                nc.vector.scalar_tensor_tensor(w1q[0:HALF, :, cols], w1t_sb[:, :, cols], above(0, HALF),
                                               w1neg[:, :, cols], ALU.is_gt, ALU.subtract).then_inc(tern_step, 1)

            def ternary_2():
                nc.vector.tensor_scalar(w2neg, w2f_sb[:], below(1), None, ALU.is_lt).then_inc(tern_step, 1)
                dve.wait_ge(tern_step, 5)
                nc.vector.scalar_tensor_tensor(w2q, w2f_sb[:], above(1), w2neg,
                                               ALU.is_gt, ALU.subtract).then_inc(tern_step, 1)

            def scale_gb():
                dve.wait_ge(scale_ready, 1)
                dve.wait_ge(ffn_in, 16 * N_FFN)
                nc.vector.tensor_scalar(gb1_s[:], ln1gb_sb[:], w_scale[0:HALF, 0:1], None, ALU.mult)\
                    .then_inc(gb_ready, 1)
                nc.vector.tensor_scalar(gb2_s[:], ln2gb_sb[:], w_scale[:, 1:2], None, ALU.mult).then_inc(gb_ready, 1)

            def common_rows():
                dve.wait_ge(rows_done, 1)
                nc.vector.tensor_tensor(crow[:], ps_t[:, 0:D], b2_sb, ALU.add).then_inc(rows_ready, 1)
                nc.vector.tensor_scalar(cg[:], ps_t[:, D:2 * D], -1.0, None, ALU.mult).then_inc(rows_ready, 1)

            def norm_mid(t):
                src, dst, n = (h1c[:], ync[:], BATCH) if t == CLS else (h1[:, t, :], yn[:, t % 2, :], P)
                dve.wait_ge(rs1_step, 2 * t + 2)
                if 2 <= t < TILES:
                    dve.wait_ge(yn_turned, t - 1)
                nc.vector.tensor_scalar(dst, src, mv1[0:n, t, 0:1], rs1[0:n, t, 1:2], ALU.subtract, ALU.mult)\
                    .then_inc(ync_ready if t == CLS else yn_ready, 1)

            def split_y(t):
                n = width(t)
                dve.wait_ge(y_first, t + 1)
                first, second, third = (y_parts[0:HALF, t % 2, j, :, 0:n] for j in range(3))
                nc.vector.tensor_tensor(y_rest[:, :, 0:n], yT[:, t % 2, :, 0:n], first, ALU.subtract)\
                    .then_inc(y_step, 1)
                nc.vector.tensor_tensor(second, yT[:, t % 2, :, 0:n], first, ALU.subtract).then_inc(y_step, 1)
                dve.wait_ge(y_step, 3 * t - 1)
                nc.vector.tensor_tensor(third, y_rest[:, :, 0:n], second, ALU.subtract).then_inc(y_step, 1)

            def sum_squares(t):
                n = width(t)
                dve.wait_ge(glsq_ready, t + 1)
                if t >= 2:
                    dve.wait_ge(ffn_done, last_job(t - 2))
                nc.vector.tensor_reduce(gsum[:, t % 2, 0:n], glsq[:, t % 2, :, 0:n].rearrange("p c n -> p n c"),
                                        AX.X, ALU.add).then_inc(gsum_ready, 1)

            def take_moments(i):
                n = job(i)[3]
                dve.wait_ge(ffn_done, i + 1)
                if i >= 2:
                    dve.wait_ge(ms_step, 5 * (i - 1))
                nc.vector.tensor_scalar(mom[0:n, i % 2, :], contract_bank(i)[0:n, D:D + 2], 1.0 / HID, None, ALU.mult)\
                    .then_inc(mom_ready, 1)

            def add_product(i):
                _, _, _, n, h = job(i)
                b = i % 2
                dve.wait_ge(ms_step, 5 * i + 4)
                dve.wait_ge(crow_in_h1, i + 1)
                if i >= 2:
                    dve.wait_ge(stored[b], 16 * stores_before(b, i - 1))
                nc.vector.scalar_tensor_tensor(fin[0:n, b, :], contract_bank(i)[0:n, 0:D], ms[0:n, b, 2:3], h,
                                               ALU.mult, ALU.add).then_inc(fin_step, 1)

            def take_mean_off(i):
                n = job(i)[3]
                b = i % 2
                dve.wait_ge(ms_step, 5 * (i + 1))
                dve.wait_ge(fin_step, 2 * i + 1)
                nc.vector.scalar_tensor_tensor(fin[0:n, b, :], cg[0:n, :], ms[0:n, b, 3:4], fin[0:n, b, :],
                                               ALU.mult, ALU.add).then_inc(fin_step, 1)

            masks(0)
            dve.wait_ge(row_in, 32)
            stats_front(0)
            aggr_front(0)
            for r in range(EARLY):
                test(r)
                next_cand(r)
                next_masks(r)
                if r == 0:
                    norm_front(0)
            for t in range(TILES):
                take_tok(t)
                test(EARLY + t)
                stats_front(t + 1)
                if t == PROJECT_0 + 4:
                    guard_norms(0)
                next_cand(EARLY + t)
                if t == PROJECT_0 + 4:
                    invert_norms(0)
                aggr_front(t + 1)
                next_masks(EARLY + t)
                if t == PROJECT_0 + 4:
                    place_norms(0)
                norm_front(t + 1)
                if t == PROJECT_0 + 1:
                    temp_cols_in()
                if t == PROJECT_0 + 3:
                    norms(0)

            for s in range(LAST_ROUNDS + 1):
                rr = rounds_of[s]
                before = rounds_of.get(s - 1, {})
                if s >= 1 and 3 not in before:
                    weigh(s - 1)
                row_max(s)
                if 3 in before:
                    weigh(s - 1)
                soft_scale(s)
                if 0 in rr:
                    test(rr[0])
                    next_cand(rr[0])
                if s == 1:
                    nc.vector.tensor_scalar(w_scale[:], asum_all, 1.0 / N_W, None, ALU.mult).then_inc(scale_ready, 1)
                    sum_guard(s)
                    invert_sum(s)
                if 0 in rr:
                    next_masks(rr[0])
                if s != 1:
                    sum_guard(s)
                if s >= 3:
                    take_out(s - 3)
                if s != 1:
                    invert_sum(s)
                if s >= 3:
                    stats_mid(s - 3)
                    aggr_mid(s - 3)
                if 1 in rr:
                    test(rr[1])
                    next_cand(rr[1])
                    next_masks(rr[1])
                norms(s + 1)
                if 2 in rr:
                    test(rr[2])
                guard_norms(s + 1)
                if 2 in rr:
                    next_cand(rr[2])
                invert_norms(s + 1)
                if 2 in rr:
                    next_masks(rr[2])
                place_norms(s + 1)
                if s >= 1:
                    sum_dots(s - 1)
                if 3 in rr:
                    test(rr[3])
                    next_cand(rr[3])
                    next_masks(rr[3])
                if s == LAST_ROUNDS:
                    lower_statistic()
                    row_max(s + 1)
                if s >= 1:
                    invert_att(s - 1)

            s = TILES - 2
            weigh(s - 1)
            soft_scale(s)
            low_masks()
            take_out(s - 3)
            sum_guard(s)
            stats_mid(s - 3)
            invert_sum(s)
            aggr_mid(s - 3)
            smallest_above(0)
            sum_dots(s - 1)
            norms(s + 1)
            invert_att(s - 1)
            guard_norms(s + 1)
            scale_gb()
            invert_norms(s + 1)
            place_norms(s + 1)
            smallest_above(1)
            take_out(s - 2)
            negate_next()
            stats_mid(s - 2)
            compare_counts()
            row_max(s + 1)
            aggr_mid(s - 2)
            choose_low()
            weigh(s)
            norm_mid(0)
            soft_scale(s + 1)
            choose_next()
            take_out(s - 1)
            take_chosen()
            stats_mid(s - 1)
            weigh_chosen()
            sum_guard(s + 1)
            threshold()
            invert_sum(s + 1)
            negative_threshold()
            aggr_mid(s - 1)
            negatives_1(0)
            ternary_1(0)
            negatives_1(1)
            ternary_1(1)
            sum_dots(s)
            norm_mid(1)
            invert_att(s)
            ternary_2()
            weigh(s + 1)
            split_y(1)
            norm_mid(2)
            take_out(s)
            stats_mid(s)
            aggr_mid(s)
            sum_dots(s + 1)
            invert_att(s + 1)
            split_y(2)
            common_rows()
            take_out(s + 1)
            stats_mid(s + 1)
            aggr_mid(s + 1)
            sum_squares(0)
            norm_mid(3)
            take_out(CLS)
            stats_mid(CLS)
            aggr_mid(CLS)
            norm_mid(CLS)
            take_moments(0)
            for t in range(TILES):
                i = last_job(t - 1) if t else 0
                after = i + 2 if t == CLS_WITH else i + 1
                if t + 1 < TILES:
                    sum_squares(t + 1)
                if t != CLS_WITH and t + 3 < TILES:
                    split_y(t + 3)
                add_product(i)
                if t == TILES - 2:
                    take_moments(after)
                take_mean_off(i)
                if t == CLS_WITH:
                    if t + 3 < TILES:
                        split_y(t + 3)
                    take_moments(i + 1)
                    add_product(i + 1)
                    take_mean_off(i + 1)
                if t + 4 < TILES:
                    norm_mid(t + 4)
                if t < TILES - 2:
                    take_moments(after)


def kernel(x, cls_tok, L0_tok_W, L0_tok_b, L0_attn_w_qkv, L0_attn_temp, L0_attn_w_out, L0_attn_b_out, L0_ffn_ln1_g,
           L0_ffn_ln1_b, L0_ffn_W1, L0_ffn_b1, L0_ffn_ln2_g, L0_ffn_ln2_b, L0_ffn_W2, L0_ffn_b2, L0_ffn_sparsity):
    import concourse.bacc as _bacc
    from concourse.bass_utils import run_bass_kernel_spmd as _run

    def chunks(a, rows):
        a = np.asarray(a)
        return a.reshape(a.shape[0] // rows, rows, -1).transpose(1, 0, 2)

    img = np.asarray(x).reshape(BATCH, 8, 16, 8, 16, 3).transpose(2, 4, 5, 0, 1, 3).reshape(C, P, TILES, P)
    head_cols = np.zeros((P, C, 32), np.float32)
    head_rows = np.zeros((P, C, P), np.float32)
    temp_cols = np.zeros((C, 32), np.float32)
    for h in range(HEADS):
        at = slice(h % 2 * PATCHES, (h % 2 + 1) * PATCHES)
        head_cols[at, h // 2, head_row(h) % 32] = 1
        head_rows[head_row(h), h // 2, at] = 1
        temp_cols[h // 2, head_row(h) % 32] = np.asarray(L0_attn_temp).reshape(-1)[h]
    ins = {
        "x_t": img.transpose(2, 1, 0, 3),
        "cls_tok": np.asarray(cls_tok).reshape(D),
        "tok_w": chunks(L0_tok_W, P),
        "rows3": np.stack([np.asarray(a) for a in (L0_tok_b, L0_attn_b_out, L0_ffn_b2)]),
        "w_qkv": chunks(L0_attn_w_qkv, HALF),
        "temp_cols": temp_cols,
        "w_out": chunks(L0_attn_w_out, P),
        "ln1_gb": np.stack([np.asarray(a).reshape(2, HALF).T for a in (L0_ffn_ln1_g, L0_ffn_ln1_b)], axis=1),
        "w1_flat": np.asarray(L0_ffn_W1).reshape(P, WCOLS),
        "w1_t": chunks(np.asarray(L0_ffn_W1).T, HALF),
        "b1": np.asarray(L0_ffn_b1).reshape(1, HID),
        "ln2_gb": np.stack([np.asarray(a).reshape(C, P).T for a in (L0_ffn_ln2_g, L0_ffn_ln2_b)], axis=1),
        "w2_t": chunks(np.asarray(L0_ffn_W2).T, P),
        "sparsity": np.asarray(L0_ffn_sparsity).reshape(1),
        "head_cols": head_cols,
        "rows_ident": np.concatenate([head_rows, np.eye(P, dtype=np.float32)[:, None, :]], axis=1),
    }
    nc = _bacc.Bacc("TRN2", target_bir_lowering=False, num_devices=1)
    arrays, args = {}, {}
    for name, a in ins.items():
        a = np.ascontiguousarray(a)
        arrays[f"in_{name}"] = a
        args[name] = nc.dram_tensor(f"in_{name}", a.shape, mybir.dt.from_np(a.dtype), kind="ExternalInput").ap()
    out = nc.dram_tensor("out_0", (BATCH, SEQ, D), F32, kind="ExternalOutput").ap()
    vit_block(nc, out=out, **args)
    r = _run(nc, [arrays], core_ids=[0])
    return r.results[0]["out_0"]
```
